# Optimizing a Trainium2 kernel written in Bass

```python
import numpy as np
import jax
import jax.numpy as jnp

def _softmax(x, axis=-1):
    return jax.nn.softmax(x, axis=axis)

def _gelu(x):
    return jax.nn.gelu(x, approximate=True)

def _silu(x):
    return jax.nn.silu(x)

def _sigmoid(x):
    return jax.nn.sigmoid(x)

def _layernorm(x, axis=-1, eps=1e-05):
    m = jnp.mean(x, axis=axis, keepdims=True)
    v = jnp.var(x, axis=axis, keepdims=True)
    return (x - m) / jnp.sqrt(v + eps)

def _scatter_add(tgt, idx, src, axis=0):
    return tgt.at[idx].add(src)

def _segment_sum(src, seg, n):
    return jax.ops.segment_sum(src, seg, n)
kernel_name = 'mk_vit_tower_d1_tok_img256_r4_82aa3e'

def setup_inputs(seed: int=0):
    np.random.seed(seed)
    _w = jnp.asarray

    def _rec_inputs():
        import jax
        import jax.numpy as jnp
        _rk = jax.random.key(seed)
        x = 7.22013e-05 + 1.00017 * jax.random.normal(jax.random.fold_in(_rk, 1), (2, 64, 64, 64), jnp.float32)
        return x
    x = _rec_inputs()

    def _L0_tok_setup():
        import jax, jax.numpy as jnp
        import numpy as np
        K = 3
        PAD = (K - 1) // 2
        BN_EPS = 1e-05

        def _unfold(x):
            b, c, h, w = x.shape
            xp = jnp.pad(x, ((0, 0), (0, 0), (PAD, PAD), (PAD, PAD)))
            shifts = [xp[:, :, i:i + h, j:j + w] for i in range(K) for j in range(K)]
            return jnp.stack(shifts, axis=2)
        key = jax.random.key(seed)
        ks = jax.random.split(key, 4)
        b, c, h, w = (8, 64, 64, 64)
        cr = c // 4
        x = jax.random.normal(ks[0], (b, c, h, w), dtype=jnp.float32)
        conv1_w = jax.random.normal(ks[1], (cr, c), dtype=jnp.float32) * (1.0 / np.sqrt(c))
        conv1_b = jnp.zeros((cr,), dtype=jnp.float32)
        bn_gamma = jnp.ones((cr,), dtype=jnp.float32)
        bn_beta = jnp.zeros((cr,), dtype=jnp.float32)
        bn_mean = jnp.zeros((cr,), dtype=jnp.float32)
        bn_var = jnp.ones((cr,), dtype=jnp.float32)
        conv2_w = jax.random.normal(ks[2], (K * K, cr), dtype=jnp.float32) * (1.0 / np.sqrt(cr))
        conv2_b = jnp.zeros((K * K,), dtype=jnp.float32)
        return {'x': x, 'conv1_w': conv1_w, 'conv1_b': conv1_b, 'bn_gamma': bn_gamma, 'bn_beta': bn_beta, 'bn_mean': bn_mean, 'bn_var': bn_var, 'conv2_w': conv2_w, 'conv2_b': conv2_b}
    _L0_tok_all = _L0_tok_setup()
    _L0_tok_in = {k: v for k, v in _L0_tok_all.items() if k in ('conv1_w', 'conv1_b', 'bn_gamma', 'bn_beta', 'bn_mean', 'bn_var', 'conv2_w', 'conv2_b')}
    del _L0_tok_all

    def _L0_attn_setup():
        import jax, jax.numpy as jnp
        import numpy as np
        B, N, D, H = (2, 512, 64, 8)
        DH = D // H
        E = 16384
        EPS = 1e-05

        def _layer_norm(y, gamma, beta):
            mu = jnp.mean(y, axis=-1, keepdims=True)
            var = jnp.var(y, axis=-1, keepdims=True)
            return (y - mu) * jax.lax.rsqrt(var + EPS) * gamma + beta
        key = jax.random.key(seed)
        ks = jax.random.split(key, 12)
        s = 0.02
        inp = {'x': jax.random.normal(ks[0], (B, N, D), jnp.float32), 'edge_index': jax.random.randint(ks[1], (2, E), 0, N, jnp.int64), 'Wq': jax.random.normal(ks[2], (D, D), jnp.float32) * s, 'bq': jnp.zeros((D,), jnp.float32), 'Wk': jax.random.normal(ks[3], (D, D), jnp.float32) * s, 'bk': jnp.zeros((D,), jnp.float32), 'Wv': jax.random.normal(ks[4], (D, D), jnp.float32) * s, 'bv': jnp.zeros((D,), jnp.float32), 'Wo': jax.random.normal(ks[5], (D, D), jnp.float32) * s, 'bo': jnp.zeros((D,), jnp.float32), 'gamma': jnp.ones((D,), jnp.float32), 'beta': jnp.zeros((D,), jnp.float32)}
        return inp
    _L0_attn_all = _L0_attn_setup()
    _L0_attn_in = {k: v for k, v in _L0_attn_all.items() if k in ('edge_index', 'Wq', 'bq', 'Wk', 'bk', 'Wv', 'bv', 'Wo', 'bo', 'gamma', 'beta')}
    del _L0_attn_all

    def _L0_ffn_setup():
        import math
        import jax, jax.numpy as jnp
        import numpy as np
        CAPACITY_FACTOR = 1.25
        TOP_K = 2
        LN_EPS = 1e-05

        def _layer_norm(x, gamma, beta):
            mu = jnp.mean(x, axis=-1, keepdims=True)
            var = jnp.var(x, axis=-1, keepdims=True)
            return (x - mu) * jax.lax.rsqrt(var + LN_EPS) * gamma + beta
        key = jax.random.key(seed)
        ks = jax.random.split(key, 4)
        B, S, D, F, E = (8, 1024, 64, 128, 8)
        x = jax.random.normal(ks[0], (B, S, D), dtype=jnp.float32)
        Wr = jax.random.normal(ks[1], (D, E), dtype=jnp.float32) / np.sqrt(D)
        br = jnp.zeros((E,), jnp.float32)
        W1 = jax.random.normal(ks[2], (E, D, F), dtype=jnp.float32) / np.sqrt(D)
        b1 = jnp.zeros((E, F), jnp.float32)
        W2 = jax.random.normal(ks[3], (E, F, D), dtype=jnp.float32) / np.sqrt(F)
        b2 = jnp.zeros((E, D), jnp.float32)
        gamma = jnp.ones((D,), jnp.float32)
        beta = jnp.zeros((D,), jnp.float32)
        return {'x': x, 'Wr': Wr, 'br': br, 'W1': W1, 'b1': b1, 'W2': W2, 'b2': b2, 'gamma': gamma, 'beta': beta}
    _L0_ffn_all = _L0_ffn_setup()
    _L0_ffn_in = {k: v for k, v in _L0_ffn_all.items() if k in ('Wr', 'br', 'W1', 'b1', 'W2', 'b2', 'gamma', 'beta')}
    del _L0_ffn_all
    return {'x': x, 'L0_tok_conv1_w': _L0_tok_in['conv1_w'], 'L0_tok_conv1_b': _L0_tok_in['conv1_b'], 'L0_tok_bn_gamma': _L0_tok_in['bn_gamma'], 'L0_tok_bn_beta': _L0_tok_in['bn_beta'], 'L0_tok_bn_mean': _L0_tok_in['bn_mean'], 'L0_tok_bn_var': _L0_tok_in['bn_var'], 'L0_tok_conv2_w': _L0_tok_in['conv2_w'], 'L0_tok_conv2_b': _L0_tok_in['conv2_b'], 'L0_attn_edge_index': _L0_attn_in['edge_index'], 'L0_attn_Wq': _L0_attn_in['Wq'], 'L0_attn_bq': _L0_attn_in['bq'], 'L0_attn_Wk': _L0_attn_in['Wk'], 'L0_attn_bk': _L0_attn_in['bk'], 'L0_attn_Wv': _L0_attn_in['Wv'], 'L0_attn_bv': _L0_attn_in['bv'], 'L0_attn_Wo': _L0_attn_in['Wo'], 'L0_attn_bo': _L0_attn_in['bo'], 'L0_attn_gamma': _L0_attn_in['gamma'], 'L0_attn_beta': _L0_attn_in['beta'], 'L0_ffn_Wr': _L0_ffn_in['Wr'], 'L0_ffn_br': _L0_ffn_in['br'], 'L0_ffn_W1': _L0_ffn_in['W1'], 'L0_ffn_b1': _L0_ffn_in['b1'], 'L0_ffn_W2': _L0_ffn_in['W2'], 'L0_ffn_b2': _L0_ffn_in['b2'], 'L0_ffn_gamma': _L0_ffn_in['gamma'], 'L0_ffn_beta': _L0_ffn_in['beta']}

def reference(x, L0_tok_conv1_w, L0_tok_conv1_b, L0_tok_bn_gamma, L0_tok_bn_beta, L0_tok_bn_mean, L0_tok_bn_var, L0_tok_conv2_w, L0_tok_conv2_b, L0_attn_edge_index, L0_attn_Wq, L0_attn_bq, L0_attn_Wk, L0_attn_bk, L0_attn_Wv, L0_attn_bv, L0_attn_Wo, L0_attn_bo, L0_attn_gamma, L0_attn_beta, L0_ffn_Wr, L0_ffn_br, L0_ffn_W1, L0_ffn_b1, L0_ffn_W2, L0_ffn_b2, L0_ffn_gamma, L0_ffn_beta):
    import jax
    import jax.numpy as jnp

    def _L0_tok_ref(x, conv1_w, conv1_b, bn_gamma, bn_beta, bn_mean, bn_var, conv2_w, conv2_b):
        import jax, jax.numpy as jnp
        import numpy as np
        K = 3
        PAD = (K - 1) // 2
        BN_EPS = 1e-05

        def _unfold(x):
            b, c, h, w = x.shape
            xp = jnp.pad(x, ((0, 0), (0, 0), (PAD, PAD), (PAD, PAD)))
            shifts = [xp[:, :, i:i + h, j:j + w] for i in range(K) for j in range(K)]
            return jnp.stack(shifts, axis=2)
        b, c, h, w = x.shape
        y = jnp.einsum('oc,bchw->bohw', conv1_w, x) + conv1_b[None, :, None, None]
        y = (y - bn_mean[None, :, None, None]) * (bn_gamma[None, :, None, None] * jax.lax.rsqrt(bn_var + BN_EPS)[None, :, None, None]) + bn_beta[None, :, None, None]
        y = jax.nn.relu(y)
        wdyn = jnp.einsum('ok,bkhw->bohw', conv2_w, y) + conv2_b[None, :, None, None]
        patches = _unfold(x)
        out = jnp.einsum('bckhw,bkhw->bchw', patches, wdyn)
        return out.reshape(b, h * w, c)

    def _L0_attn_ref(x, edge_index, Wq, bq, Wk, bk, Wv, bv, Wo, bo, gamma, beta):
        import jax, jax.numpy as jnp
        import numpy as np
        B, N, D, H = (2, 512, 64, 8)
        DH = D // H
        E = 16384
        EPS = 1e-05

        def _layer_norm(y, gamma, beta):
            mu = jnp.mean(y, axis=-1, keepdims=True)
            var = jnp.var(y, axis=-1, keepdims=True)
            return (y - mu) * jax.lax.rsqrt(var + EPS) * gamma + beta
        b, n, _ = x.shape
        scale = DH ** (-0.5)
        q = (x @ Wq + bq).reshape(b, n, H, DH)
        k = (x @ Wk + bk).reshape(b, n, H, DH)
        v = (x @ Wv + bv).reshape(b, n, H, DH)
        scores = jnp.einsum('bnhd,bmhd->bhnm', q, k) * scale
        diag = jnp.arange(n)
        mask = jnp.zeros((n, n), bool).at[diag, diag].set(True)
        mask = mask.at[edge_index[0], edge_index[1]].set(True)
        scores = jnp.where(mask[None, None], scores, -jnp.inf)
        w = jax.nn.softmax(scores, axis=-1)
        attended = jnp.einsum('bhnm,bmhd->bnhd', w, v).reshape(b, n, D)
        out = attended @ Wo + bo
        return _layer_norm(out + x, gamma, beta)

    def _L0_ffn_ref(x, Wr, br, W1, b1, W2, b2, gamma, beta):
        import math
        import jax, jax.numpy as jnp
        import numpy as np
        CAPACITY_FACTOR = 1.25
        TOP_K = 2
        LN_EPS = 1e-05

        def _layer_norm(x, gamma, beta):
            mu = jnp.mean(x, axis=-1, keepdims=True)
            var = jnp.var(x, axis=-1, keepdims=True)
            return (x - mu) * jax.lax.rsqrt(var + LN_EPS) * gamma + beta
        B, S, D = x.shape
        E = Wr.shape[1]
        N = B * S
        K = TOP_K
        logits = jnp.mean(x, axis=1) @ Wr + br
        routing_weights = jax.nn.softmax(logits, axis=-1)
        capacity = float(math.ceil(N * CAPACITY_FACTOR / E))
        expected_loads = routing_weights.sum(axis=0) * (N / B)
        scale = jnp.where(expected_loads > capacity, capacity / expected_loads, 1.0)
        routing_weights = jax.nn.softmax(routing_weights * scale, axis=-1)
        rw_tok = jnp.broadcast_to(routing_weights[:, None, :], (B, S, E)).reshape(N, E)
        top_w, top_i = jax.lax.top_k(rw_tok, K)
        top_w = jax.nn.softmax(top_w, axis=-1)
        xf = x.reshape(N, D)
        h = jax.nn.gelu(jnp.einsum('nd,edf->enf', xf, W1) + b1[:, None, :], approximate=False)
        y = jnp.einsum('enf,efd->end', h, W2) + b2[:, None, :]
        w_dense = jnp.zeros((N, E), x.dtype).at[jnp.arange(N)[:, None], top_i].add(top_w)
        out = jnp.einsum('ne,end->nd', w_dense, y).reshape(B, S, D)
        out = _layer_norm(out + x, gamma, beta)
        return out
    h = _L0_tok_ref(x, L0_tok_conv1_w, L0_tok_conv1_b, L0_tok_bn_gamma, L0_tok_bn_beta, L0_tok_bn_mean, L0_tok_bn_var, L0_tok_conv2_w, L0_tok_conv2_b)
    h = h + _L0_attn_ref(_layernorm(h, axis=-1), L0_attn_edge_index, L0_attn_Wq, L0_attn_bq, L0_attn_Wk, L0_attn_bk, L0_attn_Wv, L0_attn_bv, L0_attn_Wo, L0_attn_bo, L0_attn_gamma, L0_attn_beta)
    h = h + _L0_ffn_ref(_layernorm(h, axis=-1), L0_ffn_Wr, L0_ffn_br, L0_ffn_W1, L0_ffn_b1, L0_ffn_W2, L0_ffn_b2, L0_ffn_gamma, L0_ffn_beta)
    return h

_drawn_inputs = setup_inputs


def setup_inputs(seed=0):
    import zlib

    import numpy as np

    out = dict(_drawn_inputs(seed))
    spreads = {'L0_tok_conv1_b': (0.0, 0.1),
     'L0_tok_bn_gamma': (1.0, 0.2),
     'L0_tok_bn_beta': (0.0, 0.1),
     'L0_tok_bn_mean': (0.0, 0.1),
     'L0_tok_bn_var': (1.0, 0.2),
     'L0_tok_conv2_b': (0.0, 0.1),
     'L0_attn_bq': (0.0, 2.0),
     'L0_attn_bk': (0.0, 2.0),
     'L0_attn_bv': (0.0, 0.8),
     'L0_attn_bo': (0.0, 0.37),
     'L0_attn_gamma': (1.0, 0.2),
     'L0_attn_beta': (0.0, 0.294),
     'L0_ffn_br': (0.0, 0.1),
     'L0_ffn_b1': (0.0, 0.79),
     'L0_ffn_b2': (0.0, 0.504),
     'L0_ffn_gamma': (1.0, 0.2),
     'L0_ffn_beta': (0.0, 0.309)}
    factors = {'L0_attn_Wq': 8.0,
     'L0_attn_Wk': 8.0,
     'L0_attn_Wv': 6.943,
     'L0_attn_Wo': 5.812,
     'L0_ffn_Wr': 8.0}
    for name, (base, spread) in spreads.items():
        noise = np.random.default_rng([zlib.crc32(name.encode()), seed]).standard_normal(out[name].shape)
        drawn = base * np.exp(spread * noise) if base else spread * noise
        out[name] = jnp.asarray(drawn.astype(out[name].dtype))
    for name, factor in factors.items():
        out[name] = (out[name] * factor).astype(out[name].dtype)
    return out
```

```python
from contextlib import ExitStack

import concourse.bass as bass
from concourse import mybir

ALU = mybir.AluOpType
ACT = mybir.ActivationFunctionType
AX = mybir.AxisListType.X
F32 = mybir.dt.float32
BF16 = mybir.dt.bfloat16
FP16 = mybir.dt.float16
I32 = mybir.dt.int32
U32 = mybir.dt.uint32

P = 128
EPS = 1e-5
MASKED = -1e30


def vit_tower_kernel(
    nc, x, conv1_w, conv1_b, bn_gamma, bn_beta, bn_mean, bn_var, conv2_w, conv2_b, edge_index,
    Wq, bq, Wk, bk, Wv, bv, Wo, bo, attn_gamma, attn_beta, Wr, br, W1, b1, W2, b2, ffn_gamma, ffn_beta, out,
):
    B, C, IH, IW = x.shape
    CR = conv1_w.shape[0]
    KK = conv2_w.shape[0]
    D = IW
    N = C * IH
    EDGES = edge_index.shape[1]
    NODES = 512
    H = 8
    DH = D // H
    HEADS = B * H
    NE, _, HID = W1.shape
    TOPK = 2
    CAPACITY = float(-(-B * N * 5 // (4 * NE)))
    TILE = 512
    TILES = N // TILE
    CT = TILE // IH
    PAD = IH + 2
    assert (B, D, TILE, NODES, HID) == (2, 64, 512, 512, P)

    CHUNKS = EDGES // P
    GROUP = 16
    GROUPS = CHUNKS // GROUP
    FIELD = 4096
    assert GROUP * P * FIELD < 2 ** 24 and GROUP * P < FIELD

    Q_PART = [0, 0, 1, 1, 0, 2]
    K_PART = [0, 1, 0, 1, 2, 0]
    MAXROW = 64
    HPR = HEADS // 2
    MB = NODES // P

    with ExitStack() as ctx:
        def sb(name, shape, dt=F32):
            return ctx.enter_context(nc.sbuf_tensor(name, shape, dt))

        def sem(name):
            return ctx.enter_context(nc.semaphore(name))

        region_a = sb("region_a", [P, N])
        region_b = sb("region_b", [P, N])
        x_chan = region_a[:, :]
        x_tok = region_b[:, :].rearrange("p (t m) -> p t m", m=P)
        q_stack = region_a[:, :].bitcast(BF16).rearrange("p (h n) -> p h n", h=HEADS)
        k_stack = region_b[:, :].bitcast(BF16).rearrange("p (h n) -> p h n", h=HEADS)
        region_c = sb("region_c", [P, 16384 + 1024])
        Y0 = C * PAD
        PR0 = Y0 + 4096
        OH0 = PR0 + 4 * 3 * TILE
        x_pad = region_c[:, 0:C * PAD]
        y_relu = region_c[0:B * CR, Y0:Y0 + N]
        prod = region_c[:, PR0:PR0 + 12 * TILE].rearrange("p (s i n) -> p s i n", s=4, i=3)
        col_hot = region_c[:, OH0:OH0 + GROUP * 128].bitcast(BF16).rearrange("p (s n) -> p s n", s=GROUP)
        probs = region_c[:, 0:8 * MB * TILE].rearrange("p (s m n) -> p s m n", s=8, m=MB)
        hid = region_c[:, 0:2 * 4 * TILE].rearrange("p (s e n) -> p s e n", s=2, e=4)
        hb = sb("hb", [P, N])
        h1 = sb("h1", [P, N])
        a1 = sb("a1", [P, N])
        a2 = sb("a2", [P, N])
        z3 = a1
        row_hot = h1[:, :].bitcast(BF16).rearrange("p (s n) -> p s n", s=GROUP)
        cnt = a2[:, 0:2 * 2 * NODES].bitcast(I32).rearrange("p (s n) -> p s n", s=2)
        cnt_acc = a2[:, 4 * NODES:6 * NODES].bitcast(I32)
        v_pad = a2[:, 0:MB * HEADS * 32].rearrange("p (m n) -> p m n", m=MB)
        att = a2[:, 6 * NODES:7 * NODES]
        qk = h1[:, 0:2 * TILE].rearrange("p (q n) -> p q n", q=2)
        qk_res = h1[:, 2 * TILE:4 * TILE].rearrange("p (q n) -> p q n", q=2)
        qk_part = h1[:, 4 * TILE:7 * TILE].bitcast(BF16).rearrange("p (s q n) -> p s q n", s=3, q=2)
        pv_sb = h1[:, 0:2 * TILE].rearrange("p (q n) -> p q n", q=2)
        o_tok = region_b[:, :].rearrange("p (t m) -> p t m", m=P)

        regroup_m = a1[:, 0:12 * P].rearrange("p (k n) -> p k n", n=P)
        WT0 = 12 * P
        wd_t = a1[:, WT0:WT0 + IH // 2 * B * KK].rearrange("p (t b k) -> p t b k", b=B, k=KK)
        tnorm = region_c[:, 10 * TILE:12 * TILE].rearrange("p (s n) -> p s n", s=2)
        mask_t = sb("mask_t", [P, MB, NODES], BF16)
        mask_n = sb("mask_n", [P, MB, NODES], BF16)
        edges = sb("edges", [P, 2, CHUNKS], I32)
        edge_row = sb("edge_row", [P, CHUNKS])
        edge_col = sb("edge_col", [P, CHUNKS])
        edge_hi = sb("edge_hi", [P, CHUNKS])
        edge_val = sb("edge_val", [P, CHUNKS])
        iota_i = mask_n[:, 0:2, :].rearrange("p a n -> p (a n)").bitcast(I32)
        iota = sb("iota", [P, NODES], FP16)

        id_f = sb("id_f", [P, P])
        id_b = sb("id_b", [P, P], BF16)
        mean_m = sb("mean_m", [P, P])
        cent_m = sb("cent_m", [P, P])
        shift_m = sb("shift_m", [P, 3, P])
        sel_v = sb("sel_v", [P, 2, P])
        sel_d = sb("sel_d", [P, 2, P])
        w1_bd = sb("w1_bd", [P, B * CR])
        c2_bd = sb("c2_bd", [B * CR, B * KK])
        c2b_bc = sb("c2b_bc", [P, B * KK])
        bn_col = sb("bn_col", [B * CR, 5])
        bn_tmp = sb("bn_tmp", [B * CR, 4])
        wd_s = sb("wd_s", [P, 3, 3, IH])
        qkvo = sb("qkvo", [P, 4, P])
        cols = sb("cols", [P, 8])
        bv_bc = sb("bv_bc", [P, P])
        wr_st = sb("wr_st", [P, NE])
        br_bc = sb("br_bc", [B, NE])
        wo_c = sb("wo_c", [P, P])
        wo_mean = sb("wo_mean", [P, 1])
        wv_t = sb("wv_t", [P, P])
        m3 = sb("m3", [P, P])
        ccols = sb("ccols", [P, 3])
        mark = sb("mark", [1, 4])
        zb = sb("zb", [P, 4])
        sq = sb("sq", [P, 2, TILE])
        lnv = sb("lnv", [P, 2, TILE])
        rstd = sb("rstd", [P, 2, TILE])
        nmax = sb("nmax", [P, HEADS, MB])
        nm = sb("nm", [HEADS * MB, P])
        nm_res = sb("nm_res", [HEADS * MB, P])
        nm_part = sb("nm_part", [HEADS * MB, 3, P], BF16)
        a2_sum = sb("a2_sum", [P, TILES])
        msum = sb("msum", [P, 2])
        mcol = sb("mcol", [P, 1])
        rt = sb("rt", [B, 96])
        rt_idx = sb("rt_idx", [B, 8], U32)
        eye2 = sb("eye2", [B, B])
        ones2 = sb("ones2", [B, P])
        selb = sb("selb", [B, P])
        wb4 = sb("wb4", [P, B * TOPK])
        wcol = sb("wcol", [P, TOPK])
        w1_sel = sb("w1_sel", [P, B * TOPK, HID])
        w2_sel = sb("w2_sel", [P, B * TOPK, D])
        w2_mean = sb("w2_mean", [P, B * TOPK])
        w2_c = sb("w2_c", [P, B * TOPK, D])
        b1_sel = sb("b1_sel", [P, B * TOPK])
        b2_sel = sb("b2_sel", [P, TOPK])
        b2_mix = sb("b2_mix", [P, 1])
        c3b = sb("c3b", [P, 1])

        ps = ctx.enter_context(nc.psum_tensor("ps", [P, 8, TILE], F32))
        part_dram = nc.dram_tensor("part_dram", (3, 2, P, TILE), BF16, kind="Internal").ap()

        names = """zeroed chain_v chain_a chain_g consts edges_in xchan_in xtok_in conv_in weights_in
            onehot chunk_counted counts_copied counts_merged mask_ready mask_diag mask_turned mask_n_ready
            bn_exp bn_ready conv1_done relu_done conv2_done wd_ready regrouped wds_ready turned x_ready
            prepped woc_ready wvt_done wvt_ready m3_done m3_ready
            products prod_used  hb_ready cent_done sq_ready var_done rstd_ready a1_ready
            qkv_done qk_ready qk_split parts_out stacks_in v_ready vpad_ready
            s_done s_maxed nmax_turned nm_ready nm_split nm_in
            st_done exp_done pv_used pv_done pv_copied gathered att_ready
            z_done zsq_ready zvar_done zr_ready h1_ready c1_done c1sq_ready var2_done r2_ready a2_ready
            ms_ready lg_done rt_step rt_pe w_bc_done topw idx_ready w_sel_in w2c_ready b2m_ready c3_done c3_ready
            up_done gelu_done down_done z3_ready sq3_ready var3_done r3_ready o_ready o_turned o_copied stored
            stack_zeroed wb_ready""".split()
        S = {n: sem(n) for n in names}

        def cols_of(dram, pattern):
            return bass.AP(dram.tensor, dram.offset, pattern)

        block = ctx.enter_context(nc.Block())

        @block.sync
        def _(sp):
            sp.dma_start(edges[:, :, :], edge_index.rearrange("r (p c) -> p r c", p=P)).then_inc(S["edges_in"], 16)
            sp.dma_start(x_chan, x.rearrange("b c h w -> (b c) (h w)")).then_inc(S["xchan_in"], 16)
            sp.wait_ge(S["zeroed"], 1)
            for b in range(B):
                sp.dma_start(w1_bd[C * b:C * b + C, CR * b:CR * b + CR],
                             conv1_w.rearrange("o c -> c o")).then_inc(S["conv_in"], 16)
                sp.dma_start(c2_bd[CR * b:CR * b + CR, KK * b:KK * b + KK],
                             conv2_w.rearrange("k o -> o k")).then_inc(S["conv_in"], 16)
            for n, v in enumerate((conv1_b, bn_gamma, bn_beta, bn_mean, bn_var)):
                sp.dma_start(bn_col[:, n:n + 1], cols_of(v, [[0, B], [1, CR], [1, 1]])).then_inc(S["conv_in"], 16)
            sp.dma_start(c2b_bc[:, :], cols_of(conv2_b, [[0, P], [0, B], [1, KK]])).then_inc(S["conv_in"], 16)
            for n, w in enumerate((Wq, Wk, Wv, Wo)):
                for b in range(B):
                    sp.dma_start(qkvo[D * b:D * b + D, n, D * b:D * b + D], w).then_inc(S["weights_in"], 16)
            for n, v in enumerate((bq, bk, bv, bo, attn_gamma, attn_beta, ffn_gamma, ffn_beta)):
                sp.dma_start(cols[:, n:n + 1], cols_of(v, [[0, B], [1, D], [1, 1]])).then_inc(S["weights_in"], 16)
            sp.dma_start(bv_bc[:, :], cols_of(bv, [[0, P], [0, B], [1, D]])).then_inc(S["weights_in"], 16)
            sp.dma_start(wr_st[:, :], cols_of(Wr, [[0, B], [NE, D], [1, NE]])).then_inc(S["weights_in"], 16)
            sp.dma_start(br_bc[:, :], cols_of(br, [[0, B], [1, NE]])).then_inc(S["weights_in"], 16)
            sp.wait_ge(S["qk_split"], 1)
            for n in range(3):
                sp.dma_start(part_dram[n].rearrange("q p n -> p q n"), qk_part[:, n, :, :]).then_inc(S["parts_out"], 16)
            sp.wait_ge(S["parts_out"], 48)
            sp.wait_ge(S["stack_zeroed"], 5)
            for u in range(6):
                for which, stack, part in ((0, q_stack, Q_PART[u]), (1, k_stack, K_PART[u])):
                    sp.dma_start(stack[DH * u:DH * u + DH, :, :],
                                 part_dram[part, which].rearrange("(h d) n -> d h n", d=DH)).then_inc(S["stacks_in"], 16)
            sp.wait_ge(S["nm_split"], 1)
            for n in range(3):
                sp.dma_start(q_stack[MAXROW + n:MAXROW + n + 1, :, :], nm_part[:, n, :]).then_inc(S["nm_in"], 16)
            sp.wait_ge(S["idx_ready"], 1)
            for b in range(B):
                for s in range(TOPK):
                    e = nc.sync.value_load(rt_idx[b:b + 1, s:s + 1], min_val=0, max_val=NE - 1)
                    n = b * TOPK + s
                    sp.dma_start(w1_sel[D * b:D * b + D, n, :],
                                 W1[bass.ds(e, 1), :, :].rearrange("e d f -> (e d) f")).then_inc(S["w_sel_in"], 16)
                    sp.dma_start(w2_sel[:, n, :],
                                 W2[bass.ds(e, 1), :, :].rearrange("e f d -> (e f) d")).then_inc(S["w_sel_in"], 16)
                    sp.dma_start(b1_sel[:, n:n + 1],
                                 b1[bass.ds(e, 1), :].rearrange("e f -> f e")).then_inc(S["w_sel_in"], 16)
                    sp.dma_start(b2_sel[D * b:D * b + D, s:s + 1],
                                 b2[bass.ds(e, 1), :].rearrange("e d -> d e")).then_inc(S["w_sel_in"], 16)
            for t in range(TILES):
                sp.wait_ge(S["o_copied"], t + 1)
                for b in range(B):
                    sp.dma_start(out[b].rearrange("(t p) d -> p t d", p=P)[:, 4 * t:4 * t + 4, :],
                                 o_tok[:, 4 * t:4 * t + 4, D * b:D * b + D]).then_inc(S["stored"], 16)
            sp.wait_ge(S["stored"], 16 * B * TILES)

        @block.gpsimd
        def _(pool):
            steps = [0]

            def then(ins):
                steps[0] += 1
                ins.then_inc(S["chain_g"], 1)
                pool.wait_ge(S["chain_g"], steps[0])

            def diagonal(view, base, pattern):
                then(pool.affine_select(out=view, in_=view, compare_op=ALU.not_equal, fill=1.0, base=base,
                                        pattern=pattern, channel_multiplier=1))

            then(pool.iota(iota_i, [[1, NODES]], base=0, channel_multiplier=0))
            then(pool.tensor_copy(iota[:, :], iota_i))
            pool.memset(mark[:, 0:1], 0.0).then_inc(S["consts"], 1)
            for m in (id_f, mean_m, regroup_m, shift_m, sel_v, sel_d, id_b, eye2, selb):
                then(pool.memset(m[:], 0.0))
            then(pool.memset(ones2[:, :], 1.0))
            xp = x_pad.rearrange("p (c h) -> p c h", h=PAD)
            then(pool.memset(xp[:, :, 0:1], 0.0))
            then(pool.memset(xp[:, :, PAD - 1:PAD], 0.0))
            diagonal(id_f[:, :], 0, [[-1, P]])
            diagonal(id_b[:, :], 0, [[-1, P]])
            diagonal(eye2[:, :], 0, [[-1, B]])
            for b in range(B):
                o = slice(D * b, D * b + D)
                then(pool.memset(mean_m[o, o], 1.0 / D))
                diagonal(selb[:, o], -b, [[0, D]])
                for j in range(3):
                    diagonal(shift_m[o, j, o], 1 - j, [[-1, D]])
                    for h2 in range(2):
                        diagonal(regroup_m[D * h2:D * h2 + D, (b * 2 + h2) * 3 + j, o], j - 1, [[-1, D]])
            for u in range(2):
                for m, off in ((sel_v, 0), (sel_d, DH)):
                    diagonal(m[:, u, D * u:D * u + D].rearrange("p (g d) -> p g d", d=DH), -off, [[-2 * DH, D // DH], [-1, DH]])
            then(pool.tensor_tensor(cent_m[:, :], id_f[:, :], mean_m[:, :], ALU.subtract))
            then(pool.memset(w1_sel[:, :, :], 0.0))
            then(pool.memset(msum[:, :], 0.0))
            pool.memset(mark[:, 1:2], 0.0).then_inc(S["consts"], 1)
            pool.wait_ge(S["mask_ready"], 2)
            for m in range(MB):
                pool.affine_select(out=mask_t[:, m, :], in_=mask_t[:, m, :], compare_op=ALU.not_equal, fill=0.0,
                                   base=P * m, pattern=[[-1, NODES]], channel_multiplier=1).then_inc(S["mask_diag"], 1)
            vp = v_pad[:, :, :].rearrange("p m (g h o d) -> p m g h o d", h=2, o=4, d=DH)
            then(pool.memset(v_pad[:, :, :], 0.0))
            for m in range(MB):
                then(pool.memset(vp[:, m, :, 0, 1, :], 1.0))
                then(pool.memset(vp[:, m, :, 1, 3, :], 1.0))
            pool.memset(mark[:, 2:3], 0.0).then_inc(S["consts"], 1)
            pool.wait_ge(S["relu_done"], TILES)
            for o in (slice(32, 64), slice(64, P)):
                pool.memset(region_a[o, :], 0.0).then_inc(S["stack_zeroed"], 1)
            pool.wait_ge(S["turned"], TILES)
            for o in (slice(32, 64), slice(64, P)):
                pool.memset(region_b[o, :], 0.0).then_inc(S["stack_zeroed"], 1)
            pool.wait_ge(S["stack_zeroed"], 4)
            pool.memset(k_stack[MAXROW:MAXROW + 3, :, :], 1.0).then_inc(S["stack_zeroed"], 1)

        @block.vector
        def _(dve):
            steps = [0]

            def link(ins):
                steps[0] += 1
                ins.then_inc(S["chain_v"], 1)
                dve.wait_ge(S["chain_v"], steps[0])

            nc.vector.memset(w1_bd[:, :], 0.0)
            nc.vector.memset(c2_bd[:, :], 0.0)
            nc.vector.memset(cnt_acc[:, :], 0)
            nc.vector.memset(qkvo[:, :, :], 0.0).then_inc(S["zeroed"], 1)

            dve.wait_ge(S["edges_in"], 16)
            nc.vector.tensor_copy(edge_row[:, :], edges[:, 0, :])
            link(nc.vector.tensor_copy(edge_col[:, :], edges[:, 1, :]))
            link(nc.vector.tensor_scalar(edge_hi[:, :], edge_col[:, :], float(NODES // 2), None, ALU.is_ge))
            nc.vector.tensor_scalar(edge_val[:, :], edge_hi[:, :], float(FIELD - 1), 1.0, ALU.mult, ALU.add)
            link(nc.vector.scalar_tensor_tensor(edge_col[:, :], edge_hi[:, :], -float(NODES // 2), edge_col[:, :],
                                                ALU.mult, ALU.add))
            dve.wait_ge(S["consts"], 1)

            def merge(g_slot, g_after):
                dve.wait_ge(S["counts_copied"], g_after)
                nc.vector.tensor_tensor(cnt_acc[:, :], cnt_acc[:, :], cnt[:, g_slot, :], ALU.bitwise_or)\
                    .then_inc(S["counts_merged"], 1)

            def onehots(q, first):
                for gg in range(2):
                    for k in range(GROUP):
                        c = GROUP * gg + k + q * (2 * GROUP)
                        if not (first and gg == 0):
                            dve.wait_ge(S["chunk_counted"], c - GROUP + 1)
                        nc.vector.tensor_scalar(row_hot[:, k, :], iota[:, :], edge_row[:, bass.ds(c, 1)], None,
                                                ALU.is_equal)
                        nc.vector.tensor_scalar(col_hot[:, k, :], iota[:, 0:NODES // 2], edge_col[:, bass.ds(c, 1)],
                                                edge_val[:, bass.ds(c, 1)], ALU.is_equal, ALU.mult)\
                            .then_inc(S["onehot"], 1)
                    if not (first and gg == 0):
                        if not (first and gg == 1):
                            dve.wait_ge(S["counts_merged"], q * 2 + gg - 1)
                        merge(1 - gg, q * 2 + gg)

            onehots(0, True)
            with dve.Fori(1, GROUPS // 2) as q:
                onehots(q, False)
            dve.wait_ge(S["counts_merged"], GROUPS - 1)
            merge(1, GROUPS)
            dve.wait_ge(S["counts_merged"], GROUPS)
            link(nc.vector.tensor_scalar(cnt[:, 0, :], cnt_acc[:, :], FIELD - 1, None, ALU.bitwise_and))
            nc.vector.tensor_scalar(mask_t[:, 0:2, :], cnt[:, 0, :].rearrange("p (a n) -> p a n", a=2),
                                    0.0, MASKED, ALU.is_equal, ALU.mult).then_inc(S["mask_ready"], 1)
            nc.vector.tensor_scalar(mask_t[:, 2:4, :], cnt_acc[:, :].rearrange("p (a n) -> p a n", a=2),
                                    float(FIELD), MASKED, ALU.is_lt, ALU.mult).then_inc(S["mask_ready"], 1)

            dve.wait_ge(S["conv_in"], 16 * (2 * B + 6))
            dve.wait_ge(S["bn_exp"], 1)
            link(nc.vector.tensor_tensor(bn_tmp[:, 2:3], bn_col[:, 1:2], bn_tmp[:, 1:2], ALU.mult))
            link(nc.vector.tensor_tensor(bn_tmp[:, 0:1], bn_col[:, 0:1], bn_col[:, 3:4], ALU.subtract))
            nc.vector.scalar_tensor_tensor(bn_tmp[:, 3:4], bn_tmp[:, 0:1], bn_tmp[:, 2:3], bn_col[:, 2:3],
                                           ALU.mult, ALU.add).then_inc(S["bn_ready"], 1)
            for n in range(2):
                dve.wait_ge(S["conv2_done"], n + 1)
                w = IH // 4
                nc.vector.tensor_tensor(
                    wd_t[:, w * n:w * n + w, :, :].rearrange("p t b k -> p t (b k)"),
                    ps[:, 6 + n, 0:w * B * KK].rearrange("p (t m) -> p t m", m=B * KK),
                    bass.AP(c2b_bc, 0, [[B * KK, P], [0, w], [1, B * KK]]), ALU.add).then_inc(S["wd_ready"], 1)
            dve.wait_ge(S["weights_in"], 16 * 19)
            link(nc.vector.tensor_reduce(wo_mean[:, :], qkvo[:, 3, :], AX, ALU.add))
            link(nc.vector.tensor_scalar(wo_mean[:, :], wo_mean[:, :], 1.0 / D, None, ALU.mult))
            nc.vector.memset(wo_c[:, :], 0.0).then_inc(S["chain_v"], 1)
            steps[0] += 1
            nc.vector.tensor_copy(ccols[:, 0:1], cols[:, 3:4])
            nc.vector.tensor_copy(ccols[:, 2:3], cols[:, 7:8])
            dve.wait_ge(S["chain_v"], steps[0])
            for b in range(B):
                o = slice(D * b, D * b + D)
                nc.vector.tensor_scalar(wo_c[o, o], qkvo[o, 3, o], wo_mean[o, 0:1], None, ALU.subtract)
            nc.vector.tensor_tensor(ccols[:, 1:2], cols[:, 5:6], cols[:, 7:8], ALU.add).then_inc(S["woc_ready"], 1)
            dve.wait_ge(S["wvt_done"], 1)
            nc.vector.tensor_copy(wv_t[:, :], ps[:, 7, 0:P]).then_inc(S["wvt_ready"], 1)
            dve.wait_ge(S["m3_done"], 1)
            nc.vector.tensor_copy(m3[:, :], ps[:, 6, 0:P])
            nc.vector.tensor_copy(zb[:, 0:1], ps[:, 6, 128:129])
            nc.vector.tensor_copy(zb[:, 1:2], ps[:, 6, 192:193])
            nc.vector.tensor_scalar(zb[:, 2:4], ps[:, 6, 193:195], -1.0, None, ALU.mult).then_inc(S["m3_ready"], 1)

            def product(n):
                t, j = n // 3, n % 3
                if n >= 4:
                    dve.wait_ge(S["prod_used"], n - 3)
                nc.vector.tensor_tensor(
                    prod[:, n % 4, :, :].rearrange("p i (c h) -> p i c h", h=IH),
                    bass.AP(region_c, CT * t * PAD, [[region_c.shape[1], P], [1, 3], [PAD, CT], [1, IH]]),
                    bass.AP(wd_s, j * IH, [[9 * IH, P], [3 * IH, 3], [0, CT], [1, IH]]),
                    ALU.mult).then_inc(S["products"], 1)

            def norm1(t):
                dve.wait_ge(S["rstd_ready"], t + 1)
                dve.wait_ge(S["m3_ready"], 1)
                nc.vector.scalar_tensor_tensor(a1[:, TILE * t:TILE * t + TILE], ps[:, 2 + t % 2, :], zb[:, 2:3],
                                               rstd[:, t % 2, :], ALU.add, ALU.mult).then_inc(S["a1_ready"], 1)

            dve.wait_ge(S["wds_ready"], 6)
            for s in range(TILES + 2):
                if s < TILES:
                    dve.wait_ge(S["x_ready"], s + 1)
                    for j in range(3):
                        product(3 * s + j)
                if s >= 2:
                    norm1(s - 2)

            for n in range(2):
                dve.wait_ge(S["qkv_done"], n + 1)
                nc.vector.tensor_scalar(qk[:, n, :], ps[:, n, :], cols[:, n:n + 1], None, ALU.add)\
                    .then_inc(S["qk_ready"], 1)
            dve.wait_ge(S["qk_ready"], 2)
            link(nc.vector.tensor_copy(qk_part[:, 0, :, :], qk[:, :, :]))
            link(nc.vector.tensor_tensor(qk_res[:, :, :], qk[:, :, :], qk_part[:, 0, :, :], ALU.subtract))
            link(nc.vector.tensor_copy(qk_part[:, 1, :, :], qk_res[:, :, :]))
            link(nc.vector.tensor_tensor(qk[:, :, :], qk_res[:, :, :], qk_part[:, 1, :, :], ALU.subtract))
            nc.vector.tensor_copy(qk_part[:, 2, :, :], qk[:, :, :]).then_inc(S["qk_split"], 1)
            dve.wait_ge(S["qkv_done"], 3)
            dve.wait_ge(S["consts"], 3)
            vp = v_pad[:, :, :].rearrange("p m (g h o d) -> p m g h o d", h=2, o=4, d=DH)
            vs = ps[:, 2, :].rearrange("p (m g h d) -> p m g h d", m=MB, h=2, d=DH)
            for hp in range(2):
                nc.vector.tensor_tensor(vp[:, :, :, hp, 2 * hp, :], vs[:, :, :, hp, :],
                                        bass.AP(bv_bc, hp * DH, [[P, P], [0, MB], [2 * DH, HPR], [1, DH]]),
                                        ALU.add).then_inc(S["vpad_ready"], 1)

            for n in range(HEADS * 2):
                h, pair = n // 2, n % 2
                dve.wait_ge(S["s_done"], n + 1)
                nc.vector.tensor_reduce(nmax[:, h, 2 * pair:2 * pair + 2], ps[:, 4 + 2 * (n % 2):6 + 2 * (n % 2), :], AX,
                                        ALU.max).then_inc(S["s_maxed"], 1)
            dve.wait_ge(S["nmax_turned"], 1)
            link(nc.vector.tensor_scalar(nm[:, :], ps[0:HEADS * MB, 3, 0:P], -1.0, None, ALU.mult))
            link(nc.vector.tensor_copy(nm_part[:, 0, :], nm[:, :]))
            link(nc.vector.tensor_tensor(nm_res[:, :], nm[:, :], nm_part[:, 0, :], ALU.subtract))
            link(nc.vector.tensor_copy(nm_part[:, 1, :], nm_res[:, :]))
            link(nc.vector.tensor_tensor(nm[:, :], nm_res[:, :], nm_part[:, 1, :], ALU.subtract))
            nc.vector.tensor_copy(nm_part[:, 2, :], nm[:, :]).then_inc(S["nm_split"], 1)
            dve.wait_ge(S["pv_done"], 1)
            nc.vector.tensor_copy(pv_sb[:, :, :], ps[:, 4:6, :]).then_inc(S["pv_copied"], 1)
            dve.wait_ge(S["gathered"], 1)
            link(nc.vector.reciprocal(att[:, :], ps[:, 7, :]))
            nc.vector.tensor_tensor(att[:, :], ps[:, 6, :], att[:, :], ALU.mult).then_inc(S["att_ready"], 1)

            def norm_z(t):
                o = slice(TILE * t, TILE * t + TILE)
                dve.wait_ge(S["zr_ready"], t + 1)
                link(nc.vector.scalar_tensor_tensor(tnorm[:, 0, :], ps[:, t % 2, :], zb[:, 1:2] if t == 0 else zb[:, 0:1],
                                                    rstd[:, 0, :], ALU.add, ALU.mult))
                nc.vector.scalar_tensor_tensor(h1[:, o], tnorm[:, 0, :], cols[:, 4:5], hb[:, o], ALU.mult, ALU.add)\
                    .then_inc(S["h1_ready"], 1)

            def norm2(t):
                o = slice(TILE * t, TILE * t + TILE)
                dve.wait_ge(S["r2_ready"], t + 1)
                link(nc.vector.scalar_tensor_tensor(a2[:, o], ps[:, 4 + t % 2, :], zb[:, 3:4], rstd[:, 1, :],
                                                    ALU.add, ALU.mult))
                nc.vector.tensor_reduce(a2_sum[:, t:t + 1], a2[:, o], AX, ALU.add).then_inc(S["a2_ready"], 1)

            for s in range(TILES + 1):
                if s < TILES:
                    norm_z(s)
                if s >= 1:
                    norm2(s - 1)

            dve.wait_ge(S["a2_ready"], TILES)
            link(nc.vector.tensor_reduce(mcol[:, :], a2_sum[:, :], AX, ALU.add))
            nc.vector.tensor_copy(msum[0:D, 0:1], mcol[0:D, :])
            nc.vector.tensor_copy(msum[D:P, 1:2], mcol[D:P, :]).then_inc(S["ms_ready"], 1)
            lg, e1, rw, ld, v8 = (rt[:, 8 * k:8 * k + 8] for k in range(5))
            sc = [rt[:, 48 + k:49 + k] for k in range(8)]

            def softmax(src, tmp, dst, s_max, s_sum, turn):
                link(nc.vector.tensor_reduce(s_max, src, AX, ALU.max))
                link(nc.vector.tensor_scalar(s_max, s_max, -1.0, None, ALU.mult))
                nc.vector.tensor_copy(rt[:, 90:91], s_max).then_inc(S["rt_step"], 1)
                dve.wait_ge(S["bn_exp"], 1 + turn)
                link(nc.vector.tensor_reduce(s_sum, tmp, AX, ALU.add))
                link(nc.vector.reciprocal(s_sum, s_sum))
                link(nc.vector.tensor_scalar(dst, tmp, s_sum, None, ALU.mult))

            dve.wait_ge(S["lg_done"], 1)
            link(nc.vector.scalar_tensor_tensor(lg, ps[0:B, 0, 0:NE], 1.0 / N, br_bc[:, :], ALU.mult, ALU.add))
            softmax(lg, e1, rw, sc[0], sc[1], 1)
            nc.vector.tensor_copy(rt[:, 91:92], sc[0]).then_inc(S["rt_pe"], 1)
            dve.wait_ge(S["lg_done"], 2)
            link(nc.vector.tensor_scalar(ld, ps[0:B, 0, NE:2 * NE], float(N), 1.0, ALU.mult, ALU.max))
            link(nc.vector.reciprocal(ld, ld))
            link(nc.vector.tensor_scalar(ld, ld, CAPACITY, 1.0, ALU.mult, ALU.min))
            link(nc.vector.tensor_tensor(lg, rw, ld, ALU.mult))
            softmax(lg, e1, rw, sc[2], sc[3], 2)
            link(nc.vector.max(v8, rw))
            nc.vector.max_index(rt_idx[:, :], v8, rw).then_inc(S["idx_ready"], 1)
            two = rt[:, 56:58]
            link(nc.vector.tensor_scalar(sc[4], v8[:, 0:1], -1.0, None, ALU.mult))
            nc.vector.tensor_copy(rt[:, 92:93], sc[4]).then_inc(S["rt_step"], 1)
            dve.wait_ge(S["bn_exp"], 4)
            link(nc.vector.tensor_reduce(sc[5], two, AX, ALU.add))
            link(nc.vector.reciprocal(sc[5], sc[5]))
            link(nc.vector.tensor_scalar(rt[:, 60:62], two, sc[5], None, ALU.mult))
            for b in range(B):
                nc.vector.tensor_scalar(rt[:, 64 + 2 * b:66 + 2 * b], rt[:, 60:62], eye2[:, b:b + 1], None, ALU.mult)\
                    .then_inc(S["topw"], 1)
            dve.wait_ge(S["w_bc_done"], 1)
            nc.vector.tensor_copy(wb4[:, :], ps[:, 0, 64:68])
            link(nc.vector.tensor_copy(wcol[:, :], ps[:, 0, 72:74]))
            dve.wait_ge(S["w_sel_in"], 16 * 16)
            link(nc.vector.tensor_reduce(w2_mean[:, :], w2_sel[:, :, :], AX, ALU.add))
            link(nc.vector.tensor_scalar(w2_mean[:, :], w2_mean[:, :], 1.0 / D, None, ALU.mult))
            for n in range(B * TOPK):
                last = nc.vector.tensor_scalar(w2_c[:, n, :], w2_sel[:, n, :], w2_mean[:, n:n + 1], wb4[:, n:n + 1],
                                               ALU.subtract, ALU.mult)
            last.then_inc(S["w2c_ready"], 1)
            link(nc.vector.tensor_tensor(b2_sel[:, :], b2_sel[:, :], wcol[:, :], ALU.mult))
            nc.vector.tensor_reduce(b2_mix[:, :], b2_sel[:, :], AX, ALU.add).then_inc(S["b2m_ready"], 1)
            dve.wait_ge(S["c3_done"], 1)
            link(nc.vector.tensor_copy(c3b[:, :], ps[:, 0, 80:81]))
            nc.vector.tensor_copy(mcol[:, :], c3b[:, :]).then_inc(S["c3_ready"], 1)
            for t in range(TILES):
                o = slice(TILE * t, TILE * t + TILE)
                dve.wait_ge(S["down_done"], t + 1)
                nc.vector.tensor_scalar(z3[:, o], ps[:, 4 + t % 2, :], c3b[:, 0:1], None, ALU.add)\
                    .then_inc(S["z3_ready"], 1)
            for t in range(TILES):
                o = slice(TILE * t, TILE * t + TILE)
                dve.wait_ge(S["r3_ready"], t + 1)
                link(nc.vector.tensor_tensor(tnorm[:, t % 2, :], z3[:, o], rstd[:, t % 2, :], ALU.mult))
                nc.vector.scalar_tensor_tensor(h1[:, o], tnorm[:, t % 2, :], cols[:, 6:7], h1[:, o],
                                               ALU.mult, ALU.add).then_inc(S["o_ready"], 1)

        @block.scalar
        def _(act):
            act.dma_start(x_tok.rearrange("p t (b d) -> p t b d", b=B)[:, :, 0, :],
                          x[0].rearrange("c h w -> (c h) w").rearrange("(t p) w -> p t w", p=P)).then_inc(S["xtok_in"], 16)
            act.dma_start(x_tok.rearrange("p t (b d) -> p t b d", b=B)[:, :, 1, :],
                          x[1].rearrange("c h w -> (c h) w").rearrange("(t p) w -> p t w", p=P)).then_inc(S["xtok_in"], 16)
            steps = [0]

            def link(ins):
                steps[0] += 1
                ins.then_inc(S["chain_a"], 1)
                act.wait_ge(S["chain_a"], steps[0])

            act.wait_ge(S["conv_in"], 16 * (2 * B + 6))
            link(nc.scalar.activation(bn_tmp[:, 0:1], bn_col[:, 4:5], ACT.Ln, bias=EPS))
            nc.scalar.activation(bn_tmp[:, 1:2], bn_tmp[:, 0:1], ACT.Exp, scale=-0.5).then_inc(S["bn_exp"], 1)
            for g in range(GROUPS):
                act.wait_ge(S["chunk_counted"], GROUP * (g + 1))
                if g >= 2:
                    act.wait_ge(S["counts_merged"], g - 1)
                nc.scalar.activation(cnt[:, g % 2, :].rearrange("p (a n) -> p a n", a=2),
                                     ps[:, 2 * (g % 2):2 * (g % 2) + 2, :], ACT.Copy).then_inc(S["counts_copied"], 1)
            act.wait_ge(S["bn_ready"], 1)
            for t in range(TILES):
                act.wait_ge(S["conv1_done"], t + 1)
                nc.scalar.activation(y_relu[:, TILE * t:TILE * t + TILE], ps[0:B * CR, 4 + t % 2, :], ACT.Relu,
                                     bias=bn_tmp[:, 3:4], scale=bn_tmp[:, 2:3]).then_inc(S["relu_done"], 1)
            for j in range(3):
                for h2 in range(2):
                    n = 2 * j + h2
                    act.wait_ge(S["regrouped"], 3 * (n // 3) + 3)
                    nc.scalar.activation(
                        bass.AP(wd_s, j * IH + h2, [[9 * IH, P], [2, IH // 2], [3 * IH, 3]]),
                        ps[:, 4 + n // 3, 96 * (n % 3):96 * (n % 3) + 96].rearrange("p (h i) -> p h i", i=3),
                        ACT.Copy).then_inc(S["wds_ready"], 1)
            xp = x_pad.rearrange("p (c h) -> p c h", h=PAD)
            act.wait_ge(S["consts"], 2)
            for t in range(TILES):
                act.wait_ge(S["turned"], t + 1)
                nc.scalar.activation(xp[:, CT * t:CT * t + CT, 1:IH + 1], ps[:, t % 4, :].rearrange("p (c h) -> p c h", h=IH),
                                     ACT.Copy).then_inc(S["x_ready"], 1)
            for n in range(MB):
                act.wait_ge(S["mask_turned"], n + 1)
                nc.scalar.activation(mask_n[:, n, :], ps[:, 6 + n % 2, 0:256].bitcast(BF16), ACT.Copy)\
                    .then_inc(S["mask_n_ready"], 1)
            act.wait_ge(S["woc_ready"], 1)
            act.wait_ge(S["m3_ready"], 1)

            def rsqrt(src, k, var_sem, n, out_sem, free_sem=None, free_n=0):
                act.wait_ge(S[var_sem], n)
                link(nc.scalar.activation(lnv[:, k, :], src, ACT.Ln, bias=EPS))
                if free_sem:
                    act.wait_ge(S[free_sem], free_n)
                nc.scalar.activation(rstd[:, k, :], lnv[:, k, :], ACT.Exp, scale=-0.5).then_inc(S[out_sem], 1)

            for s in range(TILES + 2):
                if s < TILES:
                    act.wait_ge(S["prod_used"], 3 * (s + 1))
                    nc.scalar.activation(hb[:, TILE * s:TILE * s + TILE], ps[:, s % 2, :], ACT.Identity,
                                         bias=ccols[:, 1:2]).then_inc(S["hb_ready"], 1)
                if 1 <= s <= TILES:
                    t = s - 1
                    act.wait_ge(S["cent_done"], t + 1)
                    if t >= 2:
                        act.wait_ge(S["var_done"], t - 1)
                    nc.scalar.activation(sq[:, t % 2, :], ps[:, 2 + t % 2, :], ACT.Square, bias=zb[:, 2:3])\
                        .then_inc(S["sq_ready"], 1)
                if s >= 2:
                    t = s - 2
                    if t >= 2:
                        act.wait_ge(S["rstd_ready"], t - 1)
                    rsqrt(ps[:, 4 + t % 2, :], t % 2, "var_done", t + 1, "rstd_ready",
                          "a1_ready" if t >= 2 else None, t - 1)
            order = [(u, hp, g) for u in range(2) for hp in range(2) for g in range(4)]
            for n in range(HEADS * 2):
                i, half = n // 2, n % 2
                act.wait_ge(S["st_done"], n + 1)
                if i >= 8:
                    act.wait_ge(S["pv_used"], i // 4 - 1)
                nc.scalar.activation(probs[:, i % 8, 2 * half:2 * half + 2, :], ps[:, 2 * (n % 2):2 * (n % 2) + 2, :],
                                     ACT.Exp, scale=float(DH) ** -0.5).then_inc(S["exp_done"], 1)

            def z_square(t):
                act.wait_ge(S["z_done"], t + 1)
                if t >= 1:
                    act.wait_ge(S["zvar_done"], t)
                nc.scalar.activation(sq[:, 0, :], ps[:, t % 2, :], ACT.Square, bias=zb[:, 1:2] if t == 0 else zb[:, 0:1])\
                    .then_inc(S["zsq_ready"], 1)

            for s in range(TILES + 1):
                if s < TILES:
                    z_square(s)
                    if s >= 1:
                        act.wait_ge(S["zr_ready"], s)
                    rsqrt(ps[:, 2 + s % 2, :], 0, "zvar_done", s + 1, "zr_ready", "h1_ready" if s else None, s)
                if s >= 1:
                    t = s - 1
                    act.wait_ge(S["c1_done"], t + 1)
                    if t >= 1:
                        act.wait_ge(S["var2_done"], t)
                    nc.scalar.activation(sq[:, 1, :], ps[:, 4 + t % 2, :], ACT.Square, bias=zb[:, 3:4])\
                        .then_inc(S["c1sq_ready"], 1)
                    if t >= 1:
                        act.wait_ge(S["r2_ready"], t)
                    rsqrt(ps[:, 6 + t % 2, :], 1, "var2_done", t + 1, "r2_ready", "a2_ready" if t else None, t)
            for turn in range(2):
                act.wait_ge(S["rt_step"], turn + 1)
                nc.scalar.activation(rt[:, 8:16], rt[:, 0:8], ACT.Exp, bias=rt[:, 48 + 2 * turn:49 + 2 * turn])\
                    .then_inc(S["bn_exp"], 1)
            act.wait_ge(S["rt_step"], 3)
            nc.scalar.activation(rt[:, 56:58], rt[:, 32:34], ACT.Exp, bias=rt[:, 52:53]).then_inc(S["bn_exp"], 1)
            act.wait_ge(S["w_sel_in"], 16 * 16)
            for t in range(TILES):
                for n in range(B * TOPK):
                    act.wait_ge(S["up_done"], B * TOPK * t + n + 1)
                    if t >= 2:
                        act.wait_ge(S["down_done"], t - 1)
                    nc.scalar.activation(hid[:, t % 2, n, :], ps[:, n, :], ACT.Gelu, bias=b1_sel[:, n:n + 1])\
                        .then_inc(S["gelu_done"], 1)
            for s in range(TILES + 1):
                if s < TILES:
                    act.wait_ge(S["z3_ready"], s + 1)
                    if s >= 2:
                        act.wait_ge(S["var3_done"], s - 1)
                    nc.scalar.activation(sq[:, s % 2, :], z3[:, TILE * s:TILE * s + TILE], ACT.Square)\
                        .then_inc(S["sq3_ready"], 1)
                if s >= 1:
                    t = s - 1
                    if t >= 2:
                        act.wait_ge(S["r3_ready"], t - 1)
                    rsqrt(ps[:, 6 + t % 2, :], t % 2, "var3_done", t + 1, "r3_ready", "o_ready" if t >= 2 else None, t - 1)
                if s >= 2:
                    o_evac = s - 2
                    act.wait_ge(S["o_turned"], o_evac + 1)
                    nc.scalar.activation(o_tok[:, 4 * o_evac:4 * o_evac + 4, :],
                                         ps[:, o_evac % 2, :].rearrange("p (t m) -> p t m", m=P), ACT.Copy)\
                        .then_inc(S["o_copied"], 1)
            t = TILES - 1
            act.wait_ge(S["o_turned"], t + 1)
            nc.scalar.activation(o_tok[:, 4 * t:4 * t + 4, :], ps[:, t % 2, :].rearrange("p (t m) -> p t m", m=P),
                                 ACT.Copy).then_inc(S["o_copied"], 1)

        @block.tensor
        def _(pe):
            def count(q, first):
                for gg in range(2):
                    if not first:
                        pe.wait_ge(S["counts_copied"], q * 2 + gg - 1)
                    for k in range(GROUP):
                        pe.wait_ge(S["onehot"], q * (2 * GROUP) + (GROUP * gg + k + 1))
                        for j in range(2):
                            last = pe.matmul(ps[:, 2 * gg + j, :], col_hot[:, k, P * j:P * j + P], row_hot[:, k, :],
                                             start=(k == 0), stop=(k == GROUP - 1))
                        last.then_inc(S["chunk_counted"], 1)

            count(0, True)
            with pe.Fori(1, GROUPS // 2) as q:
                count(q, False)

            pe.wait_ge(S["xchan_in"], 16)
            pe.wait_ge(S["conv_in"], 16 * (2 * B + 6))
            for t in range(TILES):
                if t >= 2:
                    pe.wait_ge(S["relu_done"], t - 1)
                pe.matmul(ps[0:B * CR, 4 + t % 2, :], w1_bd[:, :], x_chan[:, TILE * t:TILE * t + TILE],
                          start=True, stop=True).then_inc(S["conv1_done"], 1)
            for t in range(IH // 2):
                pe.wait_ge(S["relu_done"], t // 4 + 1)
                n, k = t // 16, t % 16
                last = pe.matmul(ps[:, 6 + n, B * KK * k:B * KK * k + B * KK], y_relu[:, P * t:P * t + P], c2_bd[:, :],
                                 start=True, stop=True)
                if k == 15:
                    last.then_inc(S["conv2_done"], 1)
            pe.wait_ge(S["wd_ready"], 2)
            pe.wait_ge(S["consts"], 2)
            for j in range(3):
                for h2 in range(2):
                    n = 2 * j + h2
                    for b in range(B):
                        last = pe.matmul(
                            ps[:, 4 + n // 3, 96 * (n % 3):96 * (n % 3) + 96].rearrange("p (h i) -> p h i", i=3),
                            regroup_m[:, (b * 2 + h2) * 3 + j, :],
                            bass.AP(a1, WT0 + b * KK + j, [[N, P], [B * KK, IH // 2], [3, 3]]),
                            start=(b == 0), stop=(b == B - 1))
                    last.then_inc(S["regrouped"], 1)
            pe.wait_ge(S["xtok_in"], 32)
            pe.wait_ge(S["counts_copied"], GROUPS)
            for t in range(4 * TILES):
                if t % 4 == 0 and t >= 16:
                    pe.wait_ge(S["x_ready"], t // 4 - 3)
                last = pe.transpose(ps[:, (t // 4) % 4, P * (t % 4):P * (t % 4) + P], x_tok[:, t, :], id_f[:, :])
                if t % 4 == 3:
                    last.then_inc(S["turned"], 1)
            pe.wait_ge(S["mask_diag"], MB)
            for n in range(MB):
                if n >= 2:
                    pe.wait_ge(S["mask_n_ready"], n - 1)
                for m in range(MB):
                    last = pe.transpose(ps[:, 6 + n % 2, 64 * m:64 * m + 64].bitcast(BF16), mask_t[:, m, P * n:P * n + P],
                                        id_b[:, :])
                last.then_inc(S["mask_turned"], 1)
            pe.wait_ge(S["mask_n_ready"], MB)
            pe.wait_ge(S["woc_ready"], 1)
            pe.transpose(ps[:, 7, 0:P], qkvo[:, 2, :], id_f[:, :]).then_inc(S["wvt_done"], 1)
            pe.wait_ge(S["wvt_ready"], 1)
            pe.matmul(ps[:, 6, 0:P], wv_t[:, :], wo_c[:, :], start=True, stop=False)
            pe.matmul(ps[:, 6, 0:P], id_f[:, :], cent_m[:, :], start=False, stop=True)
            pe.matmul(ps[:, 6, 128:129], wo_c[:, :], cols[:, 2:3], start=True, stop=False)
            pe.matmul(ps[:, 6, 128:129], cent_m[:, :], cols[:, 3:4], start=False, stop=True)
            pe.matmul(ps[:, 6, 192:195], cent_m[:, :], ccols[:, :], start=True, stop=True).then_inc(S["m3_done"], 1)

            pe.wait_ge(S["x_ready"], TILES)
            for s in range(TILES + 2):
                if s < TILES:
                    if s >= 2:
                        pe.wait_ge(S["hb_ready"], s - 1)
                    for j in range(3):
                        n = 3 * s + j
                        pe.wait_ge(S["products"], n + 1)
                        for i in range(3):
                            last = pe.matmul(ps[:, s % 2, :], shift_m[:, j, :], prod[:, n % 4, i, :],
                                             start=(i == 0 and j == 0), stop=(i == 2 and j == 2))
                        last.then_inc(S["prod_used"], 1)
                if 1 <= s <= TILES:
                    t = s - 1
                    pe.wait_ge(S["hb_ready"], t + 1)
                    if t >= 2:
                        pe.wait_ge(S["a1_ready"], t - 1)
                    pe.matmul(ps[:, 2 + t % 2, :], cent_m[:, :], hb[:, TILE * t:TILE * t + TILE],
                              start=True, stop=True).then_inc(S["cent_done"], 1)
                if s >= 2:
                    t = s - 2
                    pe.wait_ge(S["sq_ready"], t + 1)
                    if t >= 2:
                        pe.wait_ge(S["rstd_ready"], t - 1)
                    pe.matmul(ps[:, 4 + t % 2, :], mean_m[:, :], sq[:, t % 2, :], start=True, stop=True)\
                        .then_inc(S["var_done"], 1)
            pe.wait_ge(S["a1_ready"], TILES)
            for n in range(2):
                pe.matmul(ps[:, n, :], qkvo[:, n, :], a1[:, 0:TILE], start=True, stop=True).then_inc(S["qkv_done"], 1)
            for m in range(MB):
                last = pe.matmul(ps[:, 2, P * m:P * m + P], a1[:, P * m:P * m + P], qkvo[:, 2, :], start=True, stop=True)
            last.then_inc(S["qkv_done"], 1)
            pe.wait_ge(S["stacks_in"], 16 * 12)
            for n in range(HEADS * 2):
                h, pair = n // 2, n % 2
                if n >= 2:
                    pe.wait_ge(S["s_maxed"], n - 1)
                for k in range(2):
                    nb = 2 * pair + k
                    bank = 4 + 2 * (n % 2) + k
                    pe.matmul(ps[:, bank, :], q_stack[:, h, P * nb:P * nb + P], k_stack[:, h, :], start=True, stop=False)
                    last = pe.matmul(ps[:, bank, :], id_b[:, :], mask_n[:, nb, :], start=False, stop=True)
                last.then_inc(S["s_done"], 1)
            pe.wait_ge(S["s_maxed"], HEADS * 2)
            pe.wait_ge(S["vpad_ready"], 2)
            pe.transpose(ps[0:HEADS * MB, 3, 0:P], nmax[:, :, :].rearrange("p h m -> p (h m)"), id_f[:, :])\
                .then_inc(S["nmax_turned"], 1)
            pe.wait_ge(S["nm_in"], 48)
            order = [(u, hp, g) for u in range(2) for hp in range(2) for g in range(4)]

            def weigh(quartet):
                pe.wait_ge(S["exp_done"], 8 * (quartet + 1))
                for m in range(MB):
                    for g in range(4):
                        i = 4 * quartet + g
                        u, hp, _ = order[i]
                        head = 8 * u + 2 * g + hp
                        last = pe.matmul(ps[32 * g:32 * g + 32, 4 + u, :], v_pad[:, m, 32 * head:32 * head + 32],
                                         probs[:, i % 8, m, :], start=(hp == 0 and m == 0), stop=(hp == 1 and m == MB - 1),
                                         skip_group_check=True)
                last.then_inc(S["pv_used"], 1)

            for i, (u, hp, g) in enumerate(order):
                head = 8 * u + 2 * g + hp
                for half in range(2):
                    n = 2 * i + half
                    if n >= 2:
                        pe.wait_ge(S["exp_done"], n - 1)
                    for k in range(2):
                        m = 2 * half + k
                        bank = 2 * (n % 2) + k
                        pe.matmul(ps[:, bank, :], k_stack[:, head, P * m:P * m + P], q_stack[:, head, :],
                                  start=True, stop=False)
                        last = pe.matmul(ps[:, bank, :], id_b[:, :], mask_t[:, m, :], start=False, stop=True)
                    last.then_inc(S["st_done"], 1)
                if i % 4 == 1 and i > 4:
                    weigh(i // 4 - 1)
            weigh(3)
            pe.wait_ge(S["pv_used"], 4)
            pe.transpose(ps[0:HEADS * MB, 3, 0:P], nmax[:, :, :].rearrange("p h m -> p (h m)"), id_f[:, :])\
                .then_inc(S["pv_done"], 1)
            pe.wait_ge(S["pv_copied"], 1)
            for bank, m in ((6, sel_v), (7, sel_d)):
                for u in range(2):
                    last = pe.matmul(ps[:, bank, :], m[:, u, :], pv_sb[:, u, :], start=(u == 0), stop=(u == 1))
            last.then_inc(S["gathered"], 1)

            def z_project(t):
                o = slice(TILE * t, TILE * t + TILE)
                if t >= 2:
                    pe.wait_ge(S["h1_ready"], t - 1)
                if t == 0:
                    pe.wait_ge(S["att_ready"], 1)
                    pe.matmul(ps[:, 0, :], cent_m[:, :], a1[:, o], start=True, stop=False)
                    pe.matmul(ps[:, 0, :], wo_c[:, :], att[:, :], start=False, stop=True).then_inc(S["z_done"], 1)
                else:
                    pe.matmul(ps[:, t % 2, :], m3[:, :], a1[:, o], start=True, stop=True).then_inc(S["z_done"], 1)

            def z_var(t):
                pe.wait_ge(S["zsq_ready"], t + 1)
                if t >= 2:
                    pe.wait_ge(S["zr_ready"], t - 1)
                pe.matmul(ps[:, 2 + t % 2, :], mean_m[:, :], sq[:, 0, :], start=True, stop=True).then_inc(S["zvar_done"], 1)

            z_project(0)
            for s in range(TILES + 1):
                if s + 1 < TILES:
                    z_project(s + 1)
                if s < TILES:
                    z_var(s)
                if s >= 1:
                    t = s - 1
                    pe.wait_ge(S["h1_ready"], t + 1)
                    if t >= 2:
                        pe.wait_ge(S["a2_ready"], t - 1)
                    pe.matmul(ps[:, 4 + t % 2, :], cent_m[:, :], h1[:, TILE * t:TILE * t + TILE], start=True, stop=True)\
                        .then_inc(S["c1_done"], 1)
                    pe.wait_ge(S["c1sq_ready"], t + 1)
                    if t >= 2:
                        pe.wait_ge(S["r2_ready"], t - 1)
                    pe.matmul(ps[:, 6 + t % 2, :], mean_m[:, :], sq[:, 1, :], start=True, stop=True)\
                        .then_inc(S["var2_done"], 1)
            pe.wait_ge(S["ms_ready"], 1)
            pe.matmul(ps[0:B, 0, 0:NE], msum[:, :], wr_st[:, :], start=True, stop=True).then_inc(S["lg_done"], 1)
            pe.wait_ge(S["rt_pe"], 1)
            pe.matmul(ps[0:B, 0, NE:2 * NE], ones2[:, 0:B], rt[:, 16:24], start=True, stop=True).then_inc(S["lg_done"], 1)
            pe.wait_ge(S["topw"], 2)
            pe.matmul(ps[:, 0, 64:68], ones2[:, :], rt[:, 64:68], start=True, stop=True)
            pe.matmul(ps[:, 0, 72:74], selb[:, :], rt[:, 60:62], start=True, stop=True).then_inc(S["w_bc_done"], 1)
            pe.wait_ge(S["b2m_ready"], 1)
            pe.matmul(ps[:, 0, 80:81], cent_m[:, :], b2_mix[:, :], start=True, stop=True).then_inc(S["c3_done"], 1)
            pe.wait_ge(S["c3_ready"], 1)

            def up(t):
                for n in range(B * TOPK):
                    if t >= 1:
                        pe.wait_ge(S["gelu_done"], B * TOPK * (t - 1) + n + 1)
                    pe.matmul(ps[:, n, :], w1_sel[:, n, :], a2[:, TILE * t:TILE * t + TILE], start=True, stop=True)\
                        .then_inc(S["up_done"], 1)

            def down(t):
                if t >= 2:
                    pe.wait_ge(S["z3_ready"], t - 1)
                pe.matmul(ps[:, 4 + t % 2, :], cent_m[:, :], a2[:, TILE * t:TILE * t + TILE], start=True, stop=False,
                          skip_group_check=True)
                pe.wait_ge(S["gelu_done"], B * TOPK * (t + 1))
                for s in range(TOPK):
                    for b in range(B):
                        last = pe.matmul(ps[D * b:D * b + D, 4 + t % 2, :], w2_c[:, b * TOPK + s, :],
                                         hid[:, t % 2, b * TOPK + s, :], start=False, stop=(s == TOPK - 1),
                                         skip_group_check=True)
                last.then_inc(S["down_done"], 1)

            pe.wait_ge(S["w2c_ready"], 1)
            for s in range(TILES + 1):
                if s < TILES:
                    up(s)
                if s >= 1:
                    down(s - 1)
            for s in range(TILES + 1):
                if s < TILES:
                    pe.wait_ge(S["sq3_ready"], s + 1)
                    if s >= 2:
                        pe.wait_ge(S["r3_ready"], s - 1)
                    pe.matmul(ps[:, 6 + s % 2, :], mean_m[:, :], sq[:, s % 2, :], start=True, stop=True)\
                        .then_inc(S["var3_done"], 1)
                if s >= 1:
                    t = s - 1
                    pe.wait_ge(S["o_ready"], t + 1)
                    if t >= 2:
                        pe.wait_ge(S["o_copied"], t - 1)
                    for k in range(4):
                        last = pe.transpose(ps[:, t % 2, P * k:P * k + P], h1[:, TILE * t + P * k:TILE * t + P * k + P],
                                            id_f[:, :])
                    last.then_inc(S["o_turned"], 1)


_INS = ['x', 'L0_tok_conv1_w', 'L0_tok_conv1_b', 'L0_tok_bn_gamma', 'L0_tok_bn_beta', 'L0_tok_bn_mean', 'L0_tok_bn_var',
        'L0_tok_conv2_w', 'L0_tok_conv2_b', 'L0_attn_edge_index', 'L0_attn_Wq', 'L0_attn_bq', 'L0_attn_Wk', 'L0_attn_bk',
        'L0_attn_Wv', 'L0_attn_bv', 'L0_attn_Wo', 'L0_attn_bo', 'L0_attn_gamma', 'L0_attn_beta', 'L0_ffn_Wr', 'L0_ffn_br',
        'L0_ffn_W1', 'L0_ffn_b1', 'L0_ffn_W2', 'L0_ffn_b2', 'L0_ffn_gamma', 'L0_ffn_beta']
_OUTS = [((2, 4096, 64), 'float32')]


def kernel(**inputs):
    import numpy as _np
    import concourse.bacc as _bacc
    from concourse import mybir as _mybir
    from concourse.bass_utils import run_bass_kernel_spmd as _run

    nc = _bacc.Bacc("TRN2", target_bir_lowering=False, num_devices=1)
    arrays, args = {}, []
    for name in _INS:
        a = _np.ascontiguousarray(inputs[name])
        arrays[f"in_{name}_dram"] = a
        args.append(nc.dram_tensor(f"in_{name}_dram", a.shape, _mybir.dt.from_np(a.dtype), kind="ExternalInput").ap())
    for i, (shape, dtype) in enumerate(_OUTS):
        dt = _mybir.dt.from_np(_np.dtype(dtype))
        args.append(nc.dram_tensor(f"out_{i}_dram", shape, dt, kind="ExternalOutput").ap())
    with nc.allow_non_contiguous_dma(reason="columns of small vectors"):
        vit_tower_kernel(nc, *args)
    r = _run(nc, [arrays], core_ids=[0])
    got = tuple(r.results[0][f"out_{i}_dram"] for i in range(len(_OUTS)))
    return got[0]
```

```python
from contextlib import ExitStack

import concourse.bass as bass
from concourse import mybir

ALU = mybir.AluOpType
ACT = mybir.ActivationFunctionType
AX = mybir.AxisListType.X
F32 = mybir.dt.float32
BF16 = mybir.dt.bfloat16
FP16 = mybir.dt.float16
I32 = mybir.dt.int32
U32 = mybir.dt.uint32

P = 128
EPS = 1e-5
MASKED = -1e30
NORM_SET = "natural_log_exp_and_others"


def vit_tower_kernel(
    nc, x, conv1_w, conv1_b, bn_gamma, bn_beta, bn_mean, bn_var, conv2_w, conv2_b, edge_index,
    Wq, bq, Wk, bk, Wv, bv, Wo, bo, attn_gamma, attn_beta, Wr, br, W1, b1, W2, b2, ffn_gamma, ffn_beta, out,
):
    B, C, IH, IW = x.shape
    CR = conv1_w.shape[0]
    KK = conv2_w.shape[0]
    D = IW
    N = C * IH
    EDGES = edge_index.shape[1]
    NODES = 512
    H = 8
    DH = D // H
    HEADS = B * H
    NE, _, HID = W1.shape
    TOPK = 2
    CAPACITY = float(-(-B * N * 5 // (4 * NE)))
    TILE = 512
    TILES = N // TILE
    CT = TILE // IH
    PAD = IH + 2
    assert (B, D, TILE, NODES, HID) == (2, 64, 512, 512, P)

    CHUNKS = EDGES // P
    GROUP = 16
    GROUPS = CHUNKS // GROUP
    FIELD = 4096
    assert GROUP * P * FIELD < 2 ** 24 and GROUP * P < FIELD

    Q_PART = [0, 0, 1, 1, 0, 2, 1, 2]
    K_PART = [0, 1, 0, 1, 2, 0, 2, 1]
    MAXROW = DH * len(Q_PART)
    KROWS = MAXROW + 3
    HPR = HEADS // 2
    MB = NODES // P

    with ExitStack() as ctx:
        def sb(name, shape, dt=F32):
            return ctx.enter_context(nc.sbuf_tensor(name, shape, dt))

        def sem(name):
            return ctx.enter_context(nc.semaphore(name))

        region_a = sb("region_a", [P, N])
        region_b = sb("region_b", [P, N])
        x_chan = region_a[:, :]
        x_tok = region_b[:, :].rearrange("p (t m) -> p t m", m=P)
        q_stack = region_a[:, :].bitcast(BF16).rearrange("p (h n) -> p h n", h=HEADS)
        k_stack = region_b[:, :].bitcast(BF16).rearrange("p (h n) -> p h n", h=HEADS)
        region_c = sb("region_c", [P, 17024])
        x_pad = region_c[:, 0:C * PAD]
        PROD0 = C * PAD
        prod = region_c[:, PROD0:PROD0 + 12 * TILE].rearrange("p (s i n) -> p s i n", s=4, i=3)
        y_relu = region_c[0:B * CR, PROD0:PROD0 + N]
        HOT0 = PROD0 + 12 * TILE
        col_hot = region_c[:, HOT0:HOT0 + GROUP * 128].bitcast(BF16).rearrange("p (s n) -> p s n", s=GROUP)
        QK0 = HOT0 + GROUP * 128
        qk_part = region_c[:, QK0:QK0 + 3 * TILE].bitcast(BF16).rearrange("p (s q n) -> p s q n", s=3, q=2)
        V0 = QK0 + 3 * TILE
        v_pad = region_c[:, V0:V0 + 4 * TILE].rearrange("p (m n) -> p m n", m=MB)
        tnorm = region_c[:, V0 + 4 * TILE:V0 + 6 * TILE].rearrange("p (s n) -> p s n", s=2)
        probs = region_c[:, 0:3 * 8 * TILE].rearrange("p (r g m n) -> p r g m n", r=3, g=4, m=2)
        pv_sb = region_c[:, QK0:QK0 + 2 * TILE].rearrange("p (q n) -> p q n", q=2)
        att = region_c[:, QK0 + 2 * TILE:QK0 + 3 * TILE]
        hid = region_c[:, 0:2 * 4 * TILE].rearrange("p (s e n) -> p s e n", s=2, e=4)
        o_tok = region_c[:, 8 * TILE:8 * TILE + N].rearrange("p (t m) -> p t m", m=P)
        assert 3 * 8 * TILE <= QK0 and V0 + 6 * TILE == region_c.shape[1]
        hb = sb("hb", [P, N])
        h1 = sb("h1", [P, N])
        a1 = sb("a1", [P, N])
        a2 = sb("a2", [P, N])
        z3 = a1
        row_hot = h1[:, :].bitcast(BF16).rearrange("p (s n) -> p s n", s=GROUP)
        qk = a2[:, 0:2 * TILE].rearrange("p (q n) -> p q n", q=2)
        qk_res = a2[:, 2 * TILE:4 * TILE].rearrange("p (q n) -> p q n", q=2)
        cnt = a2[:, 4 * TILE:6 * TILE].bitcast(I32)
        cnt_acc = a2[:, 6 * TILE:8 * TILE].bitcast(I32)
        regroup_m = a1[:, 0:12 * P].rearrange("p (k n) -> p k n", n=P)
        WT0 = 12 * P
        wd_t = a1[:, WT0:WT0 + IH // 2 * B * KK].rearrange("p (t b k) -> p t b k", b=B, k=KK)
        mask_t = sb("mask_t", [P, MB, NODES], BF16)
        mask_n = sb("mask_n", [P, MB, NODES], BF16)
        edges = sb("edges", [P, 2, CHUNKS], I32)
        edge_row = sb("edge_row", [P, CHUNKS])
        edge_col = sb("edge_col", [P, CHUNKS])
        edge_hi = sb("edge_hi", [P, CHUNKS])
        edge_val = sb("edge_val", [P, CHUNKS])
        iota_i = mask_n[:, 0:2, :].rearrange("p a n -> p (a n)").bitcast(I32)
        iota = sb("iota", [P, NODES], FP16)

        id_f = sb("id_f", [P, P])
        id_b = sb("id_b", [P, P], BF16)
        mean_m = sb("mean_m", [P, P])
        cent_m = sb("cent_m", [P, P])
        shift_m = sb("shift_m", [P, 3, P])
        sel_v = sb("sel_v", [P, 2, P])
        sel_d = sb("sel_d", [P, 2, P])
        w1_bd = sb("w1_bd", [P, B * CR])
        c2_bd = sb("c2_bd", [B * CR, B * KK])
        c2b_bc = sb("c2b_bc", [P, B * KK])
        bn_col = sb("bn_col", [B * CR, 5])
        bn_tmp = sb("bn_tmp", [B * CR, 4])
        wd_s = sb("wd_s", [P, 3, 3, IH])
        qkvo = sb("qkvo", [P, 4, P])
        cols = sb("cols", [P, 8])
        bv_bc = sb("bv_bc", [P, P])
        wr_st = sb("wr_st", [P, NE])
        br_bc = sb("br_bc", [B, NE])
        wo_c = sb("wo_c", [P, P])
        wo_mean = sb("wo_mean", [P, 1])
        wv_t = sb("wv_t", [P, P])
        m3 = sb("m3", [P, P])
        ccols = sb("ccols", [P, 3])
        mark = sb("mark", [1, 4])
        ones_b = sb("ones_b", [HEADS * MB, 2, P], BF16)
        zb = sb("zb", [P, 4])
        sq = sb("sq", [P, 2, TILE])
        lnv = sb("lnv", [P, 2, TILE])
        rstd = sb("rstd", [P, 2, TILE])
        nmax = sb("nmax", [P, HEADS, MB])
        nm = sb("nm", [HEADS * MB, P])
        nm_res = sb("nm_res", [HEADS * MB, P])
        nm_part = sb("nm_part", [HEADS * MB, 3, P], BF16)
        a2_sum = sb("a2_sum", [P, TILES])
        msum = sb("msum", [P, 2])
        mcol = sb("mcol", [P, 1])
        rt = sb("rt", [B, 96])
        rt_idx = sb("rt_idx", [B, 8], U32)
        eye2 = sb("eye2", [B, B])
        ones2 = sb("ones2", [B, P])
        selb = sb("selb", [B, P])
        wb4 = sb("wb4", [P, B * TOPK])
        wcol = sb("wcol", [P, TOPK])
        w1_sel = sb("w1_sel", [P, B * TOPK, HID])
        w2_sel = sb("w2_sel", [P, B * TOPK, D])
        w2_mean = sb("w2_mean", [P, B * TOPK])
        w2_c = sb("w2_c", [P, B * TOPK, D])
        b1_sel = sb("b1_sel", [P, B * TOPK])
        b2_sel = sb("b2_sel", [P, TOPK])
        b2_mix = sb("b2_mix", [P, 1])
        c3b = sb("c3b", [P, 1])

        ps = ctx.enter_context(nc.psum_tensor("ps", [P, 8, TILE], F32))
        part_dram = nc.dram_tensor("part_dram", (3, 2, P, TILE), BF16, kind="Internal").ap()

        names = """zeroed chain_v chain_a chain_g iota_ready ident_ready consts_ready late_consts
            edges_in xchan_in xtok_in conv_in weights_in
            onehot chunk_counted counts_copied counts_merged mask_ready mask_diag mask_turned mask_n_ready
            bn_exp bn_ready conv1_done relu_done conv2_done wd_ready regrouped wds_ready turned x_ready
            woc_ready wvt_done wvt_ready m3_done m3_ready
            products prod_added prod_used hb_ready cent_done sq_ready var_done rstd_ready a1_ready
            qkv_done qk_ready qk_split parts_out stacks_in vpad_ready
            s_done s_maxed nmax_turned nm_split nm_in
            st_done exp_done pv_used pv_copied gathered att_ready
            z_done zsq_ready zvar_done zr_ready h1_ready c1_done c1sq_ready var2_done r2_ready a2_ready
            ms_ready lg_done rt_step rt_exp rt_pe w_bc_done topw idx_ready w_sel_in w2c_ready b2m_ready c3_done c3_ready
            up_done gelu_done down_done z3_ready sq3_ready var3_done r3_ready o_ready o_turned o_copied stored""".split()
        S = {n: sem(n) for n in names}

        def cols_of(dram, pattern):
            return bass.AP(dram.tensor, dram.offset, pattern)

        def tile_of(t):
            return slice(TILE * t, TILE * t + TILE)

        CONV_DMAS = 2 * B + 6
        WEIGHT_DMAS = 4 * B + 8 + 3
        STACK_DMAS = 2 * (len(Q_PART) + KROWS - MAXROW)
        SLOTS = [(kind, k) for k in range(TILES) for kind in "zvcw"]
        ROUNDS = [(u, hp, half) for u in range(2) for hp in range(2) for half in range(2)]

        def beside(steps, slots, every, lag=0):
            plan = []
            for n in range(steps):
                k = n - lag - every // 2
                if k >= 0 and k % every == 0 and k // every < len(slots):
                    plan.append(("norm", slots[k // every]))
                plan.append(("step", n))
            return plan

        S_SLOTS, S_EVERY = 12, 5
        T_SLOTS, T_EVERY = 12, 5
        PLAN_S = (HEADS * MB, SLOTS[0:S_SLOTS], S_EVERY)
        PLAN_T = (HEADS * MB, SLOTS[S_SLOTS:S_SLOTS + T_SLOTS], T_EVERY)
        assert S_SLOTS + T_SLOTS == 4 * (TILES - 2)
        S_BANKS = 4
        LAST = TILES - 1
        TAIL_SLOTS = [("z", LAST - 1), ("v", LAST - 1), ("c", LAST - 1), ("w", LAST - 1)] + SLOTS[4 * LAST:]

        def norm_bank(k):
            return 2 if k == LAST else 0

        EARLY = 24

        def beside_product(n):
            def bound(m):
                return min(CHUNKS, EARLY + (CHUNKS - EARLY) * m // (3 * TILES - 1))
            return range(bound(n), bound(n + 1))

        def head_of(u, hp, g):
            return 8 * u + 2 * g + hp

        BATCHES = [range(0, 4), range(4, TILES)]

        QKV_STEP = 3

        def acc_bank(s):
            return (s + (3 if s > QKV_STEP else 0)) % 2

        block = ctx.enter_context(nc.Block())

        def fetch_experts(eng, b):
            eng.wait_ge(S["idx_ready"], 1)
            for s in range(TOPK):
                e = eng.value_load(rt_idx[b:b + 1, s:s + 1], min_val=0, max_val=NE - 1)
                n = b * TOPK + s
                for dst, src in ((w1_sel[D * b:D * b + D, n, :], W1[bass.ds(e, 1), :, :].rearrange("e d f -> (e d) f")),
                                 (w2_sel[:, n, :], W2[bass.ds(e, 1), :, :].rearrange("e f d -> (e f) d")),
                                 (b1_sel[:, n:n + 1], b1[bass.ds(e, 1), :].rearrange("e f -> f e")),
                                 (b2_sel[D * b:D * b + D, s:s + 1], b2[bass.ds(e, 1), :].rearrange("e d -> d e"))):
                    eng.dma_start(dst, src).then_inc(S["w_sel_in"], 16)

        @block.sync
        def _(sp):
            sp.dma_start(edges[:, :, :], edge_index.rearrange("r (p c) -> p r c", p=P)).then_inc(S["edges_in"], 16)
            sp.wait_ge(S["zeroed"], 1)
            for b in range(B):
                sp.dma_start(w1_bd[C * b:C * b + C, CR * b:CR * b + CR],
                             conv1_w.rearrange("o c -> c o")).then_inc(S["conv_in"], 16)
                sp.dma_start(c2_bd[CR * b:CR * b + CR, KK * b:KK * b + KK],
                             conv2_w.rearrange("k o -> o k")).then_inc(S["conv_in"], 16)
            for n, v in enumerate((conv1_b, bn_gamma, bn_beta, bn_mean, bn_var)):
                sp.dma_start(bn_col[:, n:n + 1], cols_of(v, [[0, B], [1, CR], [1, 1]])).then_inc(S["conv_in"], 16)
            sp.dma_start(c2b_bc[:, :], cols_of(conv2_b, [[0, P], [0, B], [1, KK]])).then_inc(S["conv_in"], 16)
            for b in range(B):
                sp.dma_start(x_tok.rearrange("p t (b d) -> p t b d", b=B)[:, :, b, :],
                             x[b].rearrange("c h w -> (c h) w").rearrange("(t p) w -> p t w", p=P))\
                    .then_inc(S["xtok_in"], 16)
            for n, w in enumerate((Wq, Wk, Wv, Wo)):
                for b in range(B):
                    sp.dma_start(qkvo[D * b:D * b + D, n, D * b:D * b + D], w).then_inc(S["weights_in"], 16)
            for n, v in enumerate((bq, bk, bv, bo, attn_gamma, attn_beta, ffn_gamma, ffn_beta)):
                sp.dma_start(cols[:, n:n + 1], cols_of(v, [[0, B], [1, D], [1, 1]])).then_inc(S["weights_in"], 16)
            sp.dma_start(bv_bc[:, :], cols_of(bv, [[0, P], [0, B], [1, D]])).then_inc(S["weights_in"], 16)
            sp.dma_start(wr_st[:, :], cols_of(Wr, [[0, B], [NE, D], [1, NE]])).then_inc(S["weights_in"], 16)
            sp.dma_start(br_bc[:, :], cols_of(br, [[0, B], [1, NE]])).then_inc(S["weights_in"], 16)
            sp.wait_ge(S["late_consts"], 1)
            sp.wait_ge(S["conv1_done"], TILES)
            for n in range(MAXROW, KROWS):
                sp.dma_start(q_stack[n:n + 1, :, :], ones_b[:, 0, :]).then_inc(S["stacks_in"], 16)
            sp.wait_ge(S["turned"], TILES)
            for n in range(MAXROW, KROWS):
                sp.dma_start(k_stack[n:n + 1, :, :], ones_b[:, 1, :]).then_inc(S["stacks_in"], 16)
            sp.wait_ge(S["qk_split"], 1)
            for n in range(3):
                sp.dma_start(part_dram[n].rearrange("q p n -> p q n"), qk_part[:, n, :, :]).then_inc(S["parts_out"], 16)
            sp.wait_ge(S["parts_out"], 48)
            for u in range(len(Q_PART)):
                for which, stack, part in ((0, q_stack, Q_PART[u]), (1, k_stack, K_PART[u])):
                    sp.dma_start(stack[DH * u:DH * u + DH, :, :],
                                 part_dram[part, which].rearrange("(h d) n -> d h n", d=DH)).then_inc(S["stacks_in"], 16)
            sp.wait_ge(S["nm_split"], 1)
            for n in range(3):
                sp.dma_start(q_stack[MAXROW + n:MAXROW + n + 1, :, :], nm_part[:, n, :]).then_inc(S["nm_in"], 16)
            fetch_experts(sp, 0)
            for t in range(TILES):
                sp.wait_ge(S["o_copied"], t + 1)
                for b in range(B):
                    sp.dma_start(out[b].rearrange("(t p) d -> p t d", p=P)[:, 4 * t:4 * t + 4, :],
                                 o_tok[:, 4 * t:4 * t + 4, D * b:D * b + D]).then_inc(S["stored"], 16)
            sp.wait_ge(S["stored"], 16 * B * TILES)

        @block.gpsimd
        def _(pool):
            steps = [0]

            def then(ins):
                steps[0] += 1
                ins.then_inc(S["chain_g"], 1)
                pool.wait_ge(S["chain_g"], steps[0])

            def diagonal(view, base, pattern):
                then(pool.affine_select(out=view, in_=view, compare_op=ALU.not_equal, fill=1.0, base=base,
                                        pattern=pattern, channel_multiplier=1))

            then(pool.iota(iota_i, [[1, NODES]], base=0, channel_multiplier=0))
            pool.tensor_copy(iota[:, :], iota_i).then_inc(S["iota_ready"], 1)
            pool.wait_ge(S["zeroed"], 2)
            diagonal(id_f[:, :], 0, [[-1, P]])
            then(pool.memset(mark[:, 0:1], 0.0))
            pool.memset(mark[:, 1:2], 0.0).then_inc(S["ident_ready"], 1)
            for b in range(B):
                o = slice(D * b, D * b + D)
                for j in range(3):
                    for h2 in range(2):
                        diagonal(regroup_m[D * h2:D * h2 + D, (b * 2 + h2) * 3 + j, o], j - 1, [[-1, D]])
            xp = x_pad.rearrange("p (c h) -> p c h", h=PAD)
            then(pool.memset(xp[:, :, 0:1], 0.0))
            then(pool.memset(xp[:, :, PAD - 1:PAD], 0.0))
            for b in range(B):
                o = slice(D * b, D * b + D)
                then(pool.memset(mean_m[o, o], 1.0 / D))
                for j in range(3):
                    diagonal(shift_m[o, j, o], 1 - j, [[-1, D]])
            pool.tensor_tensor(cent_m[:, :], id_f[:, :], mean_m[:, :], ALU.subtract).then_inc(S["consts_ready"], 1)
            then(pool.memset(ones_b[:, 0, :], 0.0))
            pool.memset(ones_b[:, 1, :], 1.0).then_inc(S["late_consts"], 1)
            vp = v_pad[:, :, :].rearrange("p m (g h o d) -> p m g h o d", h=2, o=4, d=DH)
            then(pool.memset(v_pad[:, :, :], 0.0))
            for m in range(MB):
                then(pool.memset(vp[:, m, :, 0, 1, :], 1.0))
                then(pool.memset(vp[:, m, :, 1, 3, :], 1.0))
            for m in (sel_v, sel_d, id_b, eye2, selb):
                then(pool.memset(m[:], 0.0))
            then(pool.memset(ones2[:, :], 1.0))
            diagonal(id_b[:, :], 0, [[-1, P]])
            diagonal(eye2[:, :], 0, [[-1, B]])
            for b in range(B):
                diagonal(selb[:, D * b:D * b + D], -b, [[0, D]])
            for u in range(2):
                for m, off in ((sel_v, 0), (sel_d, DH)):
                    diagonal(m[:, u, D * u:D * u + D].rearrange("p (g d) -> p g d", d=DH), -off,
                             [[-2 * DH, D // DH], [-1, DH]])
            then(pool.memset(w1_sel[:, :, :], 0.0))
            pool.memset(msum[:, :], 0.0).then_inc(S["late_consts"], 1)
            for n in range(3 * TILES):
                pool.wait_ge(S["products"], n + 1)
                pool.tensor_tensor(prod[:, n % 4, 0, :], prod[:, n % 4, 0, :], prod[:, n % 4, 1, :], ALU.add)\
                    .then_inc(S["prod_added"], 1)
            pool.wait_ge(S["mask_ready"], 2)
            for m in range(MB):
                pool.affine_select(out=mask_t[:, m, :], in_=mask_t[:, m, :], compare_op=ALU.not_equal, fill=0.0,
                                   base=P * m, pattern=[[-1, NODES]], channel_multiplier=1)\
                    .then_inc(S["mask_diag"], 1)
            for t in range(TILES):
                pool.wait_ge(S["z3_ready"], t + 1)
                if t >= 2:
                    pool.wait_ge(S["var3_done"], t - 1)
                pool.tensor_tensor(sq[:, t % 2, :], z3[:, tile_of(t)], z3[:, tile_of(t)], ALU.mult)\
                    .then_inc(S["sq3_ready"], 1)

        @block.vector
        def _(dve):
            steps = [0]

            def link(ins):
                steps[0] += 1
                ins.then_inc(S["chain_v"], 1)
                dve.wait_ge(S["chain_v"], steps[0])

            nc.vector.memset(w1_bd[:, :], 0.0)
            nc.vector.memset(c2_bd[:, :], 0.0)
            nc.vector.memset(qkvo[:, :, :], 0.0).then_inc(S["zeroed"], 1)
            for m in (id_f, mean_m, shift_m):
                nc.vector.memset(m[:], 0.0)
            nc.vector.memset(regroup_m, 0.0).then_inc(S["zeroed"], 1)
            nc.vector.memset(cnt_acc, 0)
            nc.vector.memset(wo_c[:, :], 0.0)

            dve.wait_ge(S["edges_in"], 16)
            nc.vector.tensor_copy(edge_row[:, :], edges[:, 0, :])
            link(nc.vector.tensor_copy(edge_col[:, :], edges[:, 1, :]))
            link(nc.vector.tensor_scalar(edge_hi[:, :], edge_col[:, :], float(NODES // 2), None, ALU.is_ge))
            nc.vector.tensor_scalar(edge_val[:, :], edge_hi[:, :], float(FIELD - 1), 1.0, ALU.mult, ALU.add)
            link(nc.vector.scalar_tensor_tensor(edge_col[:, :], edge_hi[:, :], -float(NODES // 2), edge_col[:, :],
                                                ALU.mult, ALU.add))
            dve.wait_ge(S["iota_ready"], 1)

            def merge(g):
                dve.wait_ge(S["counts_copied"], g + 1)
                if g >= 1:
                    dve.wait_ge(S["counts_merged"], g)
                nc.vector.tensor_tensor(cnt_acc, cnt_acc, cnt, ALU.bitwise_or).then_inc(S["counts_merged"], 1)

            def onehots(chunks):
                for c in chunks:
                    k = c % GROUP
                    if c >= GROUP:
                        dve.wait_ge(S["chunk_counted"], c - GROUP + 1)
                    nc.vector.tensor_scalar(row_hot[:, k, :], iota[:, :], edge_row[:, c:c + 1], None, ALU.is_equal)
                    nc.vector.tensor_scalar(col_hot[:, k, :], iota[:, 0:NODES // 2], edge_col[:, c:c + 1],
                                            edge_val[:, c:c + 1], ALU.is_equal, ALU.mult).then_inc(S["onehot"], 1)
                    if k == GROUP // 2 and c >= GROUP:
                        merge(c // GROUP - 1)

            onehots(range(0, EARLY // 3))
            dve.wait_ge(S["conv_in"], 16 * CONV_DMAS)
            dve.wait_ge(S["bn_exp"], 1)
            link(nc.vector.tensor_tensor(bn_tmp[:, 2:3], bn_col[:, 1:2], bn_tmp[:, 1:2], ALU.mult))
            link(nc.vector.tensor_tensor(bn_tmp[:, 0:1], bn_col[:, 0:1], bn_col[:, 3:4], ALU.subtract))
            nc.vector.scalar_tensor_tensor(bn_tmp[:, 3:4], bn_tmp[:, 0:1], bn_tmp[:, 2:3], bn_col[:, 2:3],
                                           ALU.mult, ALU.add).then_inc(S["bn_ready"], 1)
            onehots(range(EARLY // 3, EARLY))
            for n in range(2):
                dve.wait_ge(S["conv2_done"], n + 1)
                w = IH // 4
                nc.vector.tensor_tensor(
                    wd_t[:, w * n:w * n + w, :, :].rearrange("p t b k -> p t (b k)"),
                    ps[:, 4 + n, 0:w * B * KK].rearrange("p (t m) -> p t m", m=B * KK),
                    bass.AP(c2b_bc, 0, [[B * KK, P], [0, w], [1, B * KK]]), ALU.add).then_inc(S["wd_ready"], 1)
            dve.wait_ge(S["weights_in"], 16 * WEIGHT_DMAS)
            link(nc.vector.tensor_reduce(wo_mean[:, :], qkvo[:, 3, :], AX, ALU.add))
            nc.vector.tensor_copy(ccols[:, 0:1], cols[:, 3:4])
            nc.vector.tensor_copy(ccols[:, 2:3], cols[:, 7:8])
            link(nc.vector.tensor_scalar(wo_mean[:, :], wo_mean[:, :], 1.0 / D, None, ALU.mult))
            for b in range(B):
                o = slice(D * b, D * b + D)
                nc.vector.tensor_scalar(wo_c[o, o], qkvo[o, 3, o], wo_mean[o, 0:1], None, ALU.subtract)
            nc.vector.tensor_tensor(ccols[:, 1:2], cols[:, 5:6], cols[:, 7:8], ALU.add).then_inc(S["woc_ready"], 1)

            def weights(part):
                if part == 0:
                    dve.wait_ge(S["wvt_done"], 1)
                    nc.vector.tensor_copy(wv_t[:, :], ps[:, 3, 0:P]).then_inc(S["wvt_ready"], 1)
                else:
                    dve.wait_ge(S["m3_done"], 1)
                    nc.vector.tensor_copy(m3[:, :], ps[:, 2, 0:P])
                    nc.vector.tensor_copy(zb[:, 0:1], ps[:, 2, 128:129])
                    nc.vector.tensor_copy(zb[:, 1:2], ps[:, 2, 192:193])
                    nc.vector.tensor_scalar(zb[:, 2:4], ps[:, 2, 193:195], -1.0, None, ALU.mult)\
                        .then_inc(S["m3_ready"], 1)

            def product(n):
                t, j = n // 3, n % 3
                if n >= 4:
                    dve.wait_ge(S["prod_used"], n - 3)
                nc.vector.tensor_tensor(
                    prod[:, n % 4, :, :].rearrange("p i (c h) -> p i c h", h=IH),
                    bass.AP(region_c, CT * t * PAD, [[region_c.shape[1], P], [1, 3], [PAD, CT], [1, IH]]),
                    bass.AP(wd_s, j * IH, [[9 * IH, P], [3 * IH, 3], [0, CT], [1, IH]]),
                    ALU.mult).then_inc(S["products"], 1)

            def norm1(t):
                dve.wait_ge(S["rstd_ready"], t + 1)
                nc.vector.scalar_tensor_tensor(a1[:, tile_of(t)], ps[:, 2 + t % 2, :], zb[:, 2:3],
                                               rstd[:, t % 2, :], ALU.add, ALU.mult).then_inc(S["a1_ready"], 1)

            def split_qk():
                for n in range(2):
                    dve.wait_ge(S["qkv_done"], n + 1)
                    nc.vector.tensor_scalar(qk[:, n, :], ps[:, n, :], cols[:, n:n + 1], None, ALU.add)\
                        .then_inc(S["qk_ready"], 1)
                dve.wait_ge(S["qk_ready"], 2)
                link(nc.vector.tensor_copy(qk_part[:, 0, :, :], qk))
                link(nc.vector.tensor_tensor(qk_res, qk, qk_part[:, 0, :, :], ALU.subtract))
                link(nc.vector.tensor_copy(qk_part[:, 1, :, :], qk_res))
                link(nc.vector.tensor_tensor(qk, qk_res, qk_part[:, 1, :, :], ALU.subtract))
                nc.vector.tensor_copy(qk_part[:, 2, :, :], qk).then_inc(S["qk_split"], 1)
                dve.wait_ge(S["qkv_done"], 3)
                dve.wait_ge(S["late_consts"], 2)
                vp = v_pad[:, :, :].rearrange("p m (g h o d) -> p m g h o d", h=2, o=4, d=DH)
                vs = ps[:, 0, :].rearrange("p (m g h d) -> p m g h d", m=MB, h=2, d=DH)
                for hp in range(2):
                    nc.vector.tensor_tensor(vp[:, :, :, hp, 2 * hp, :], vs[:, :, :, hp, :],
                                            bass.AP(bv_bc, hp * DH, [[P, P], [0, MB], [2 * DH, HPR], [1, DH]]),
                                            ALU.add).then_inc(S["vpad_ready"], 1)

            def decode_mask():
                merge(GROUPS - 1)
                dve.wait_ge(S["counts_merged"], GROUPS)
                link(nc.vector.tensor_scalar(cnt, cnt_acc, FIELD - 1, None, ALU.bitwise_and))
                nc.vector.tensor_scalar(mask_t[:, 0:2, :], cnt.rearrange("p (a n) -> p a n", a=2),
                                        0.0, MASKED, ALU.is_equal, ALU.mult).then_inc(S["mask_ready"], 1)
                nc.vector.tensor_scalar(mask_t[:, 2:4, :], cnt_acc.rearrange("p (a n) -> p a n", a=2),
                                        float(FIELD), MASKED, ALU.is_lt, ALU.mult).then_inc(S["mask_ready"], 1)

            dve.wait_ge(S["wds_ready"], 6)
            dve.wait_ge(S["x_ready"], TILES)
            for s in range(TILES + 2):
                for j in range(3):
                    if s < TILES:
                        product(3 * s + j)
                        onehots(beside_product(3 * s + j))
                    if s == 0 and j < 2:
                        weights(j)
                if s >= 2:
                    norm1(s - 2)
                if s == QKV_STEP:
                    split_qk()
                if s == TILES - 1:
                    decode_mask()

            def norm_z(k):
                t = (k + 1) % TILES
                dve.wait_ge(S["zr_ready"], k + 1)
                link(nc.vector.scalar_tensor_tensor(tnorm[:, 0, :], ps[:, norm_bank(k), :], zb[:, 1:2] if t == 0 else zb[:, 0:1],
                                                    rstd[:, 0, :], ALU.add, ALU.mult))
                nc.vector.scalar_tensor_tensor(h1[:, tile_of(t)], tnorm[:, 0, :], cols[:, 4:5], hb[:, tile_of(t)],
                                               ALU.mult, ALU.add).then_inc(S["h1_ready"], 1)

            def norm2(k):
                t = (k + 1) % TILES
                dve.wait_ge(S["r2_ready"], k + 1)
                link(nc.vector.scalar_tensor_tensor(a2[:, tile_of(t)], ps[:, norm_bank(k), :], zb[:, 3:4], rstd[:, 1, :],
                                                    ALU.add, ALU.mult))
                nc.vector.tensor_reduce(a2_sum[:, t:t + 1], a2[:, tile_of(t)], AX, ALU.add).then_inc(S["a2_ready"], 1)

            def norms(kind, k):
                if kind == "v":
                    norm_z(k)
                if kind == "w":
                    norm2(k)

            for what, n in beside(*PLAN_S, lag=3):
                if what == "norm":
                    norms(*n)
                    continue
                dve.wait_ge(S["s_done"], n + 1)
                nc.vector.tensor_reduce(nmax[:, n // MB, n % MB:n % MB + 1], ps[:, 2 + n % S_BANKS, :], AX, ALU.max)\
                    .then_inc(S["s_maxed"], 1)
            dve.wait_ge(S["nmax_turned"], 1)
            link(nc.vector.tensor_scalar(nm[:, :], ps[0:HEADS * MB, 6, 0:P], -1.0, None, ALU.mult))
            link(nc.vector.tensor_copy(nm_part[:, 0, :], nm[:, :]))
            link(nc.vector.tensor_tensor(nm_res[:, :], nm[:, :], nm_part[:, 0, :], ALU.subtract))
            link(nc.vector.tensor_copy(nm_part[:, 1, :], nm_res[:, :]))
            link(nc.vector.tensor_tensor(nm[:, :], nm_res[:, :], nm_part[:, 1, :], ALU.subtract))
            nc.vector.tensor_copy(nm_part[:, 2, :], nm[:, :]).then_inc(S["nm_split"], 1)
            for what, n in beside(*PLAN_T):
                if what == "norm":
                    norms(*n)
            dve.wait_ge(S["pv_used"], len(ROUNDS))
            nc.vector.tensor_copy(pv_sb, ps[:, 6:8, :]).then_inc(S["pv_copied"], 1)
            norm_z(LAST - 1)
            dve.wait_ge(S["gathered"], 1)
            link(nc.vector.reciprocal(att, ps[:, 5, :]))
            nc.vector.tensor_tensor(att, ps[:, 4, :], att, ALU.mult).then_inc(S["att_ready"], 1)
            norm2(LAST - 1)
            norm_z(LAST)
            norm2(LAST)

            dve.wait_ge(S["a2_ready"], TILES)
            link(nc.vector.tensor_reduce(mcol[:, :], a2_sum[:, :], AX, ALU.add))
            nc.vector.tensor_copy(msum[0:D, 0:1], mcol[0:D, :])
            nc.vector.tensor_copy(msum[D:P, 1:2], mcol[D:P, :]).then_inc(S["ms_ready"], 1)
            lg, e1, rw, ld, v8 = (rt[:, 8 * k:8 * k + 8] for k in range(5))
            sc = [rt[:, 48 + k:49 + k] for k in range(8)]

            def softmax(src, tmp, dst, s_max, s_sum, turn):
                link(nc.vector.tensor_reduce(s_max, src, AX, ALU.max))
                nc.vector.tensor_scalar(s_max, s_max, -1.0, None, ALU.mult).then_inc(S["rt_step"], 1)
                dve.wait_ge(S["rt_exp"], turn)
                link(nc.vector.tensor_reduce(s_sum, tmp, AX, ALU.add))
                link(nc.vector.reciprocal(s_sum, s_sum))
                return nc.vector.tensor_scalar(dst, tmp, s_sum, None, ALU.mult)

            dve.wait_ge(S["lg_done"], 1)
            link(nc.vector.scalar_tensor_tensor(lg, ps[0:B, 0, 0:NE], 1.0 / N, br_bc[:, :], ALU.mult, ALU.add))
            softmax(lg, e1, rw, sc[0], sc[1], 1).then_inc(S["rt_pe"], 1)
            dve.wait_ge(S["lg_done"], 2)
            link(nc.vector.tensor_scalar(ld, ps[0:B, 0, NE:2 * NE], float(N), 1.0, ALU.mult, ALU.max))
            link(nc.vector.reciprocal(ld, ld))
            link(nc.vector.tensor_scalar(ld, ld, CAPACITY, 1.0, ALU.mult, ALU.min))
            link(nc.vector.tensor_tensor(lg, rw, ld, ALU.mult))
            link(softmax(lg, e1, rw, sc[2], sc[3], 2))
            link(nc.vector.max(v8, rw))
            nc.vector.max_index(rt_idx[:, :], v8, rw).then_inc(S["idx_ready"], 1)
            two = rt[:, 56:58]
            nc.vector.tensor_scalar(sc[4], v8[:, 0:1], -1.0, None, ALU.mult).then_inc(S["rt_step"], 1)
            dve.wait_ge(S["rt_exp"], 3)
            link(nc.vector.tensor_reduce(sc[5], two, AX, ALU.add))
            link(nc.vector.reciprocal(sc[5], sc[5]))
            link(nc.vector.tensor_scalar(rt[:, 60:62], two, sc[5], None, ALU.mult))
            for b in range(B):
                nc.vector.tensor_scalar(rt[:, 64 + 2 * b:66 + 2 * b], rt[:, 60:62], eye2[:, b:b + 1], None, ALU.mult)\
                    .then_inc(S["topw"], 1)
            dve.wait_ge(S["w_bc_done"], 1)
            nc.vector.tensor_copy(wb4[:, :], ps[:, 0, 64:68])
            link(nc.vector.tensor_copy(wcol[:, :], ps[:, 0, 72:74]))
            dve.wait_ge(S["w_sel_in"], 16 * 4 * B * TOPK)
            link(nc.vector.tensor_reduce(w2_mean[:, :], w2_sel[:, :, :], AX, ALU.add))
            link(nc.vector.tensor_scalar(w2_mean[:, :], w2_mean[:, :], 1.0 / D, None, ALU.mult))
            for n in range(B * TOPK):
                last = nc.vector.tensor_scalar(w2_c[:, n, :], w2_sel[:, n, :], w2_mean[:, n:n + 1], wb4[:, n:n + 1],
                                               ALU.subtract, ALU.mult)
            last.then_inc(S["w2c_ready"], 1)
            link(nc.vector.tensor_tensor(b2_sel[:, :], b2_sel[:, :], wcol[:, :], ALU.mult))
            nc.vector.tensor_reduce(b2_mix[:, :], b2_sel[:, :], AX, ALU.add).then_inc(S["b2m_ready"], 1)
            dve.wait_ge(S["c3_done"], 1)
            nc.vector.tensor_copy(c3b[:, :], ps[:, 0, 80:81]).then_inc(S["c3_ready"], 1)
            dve.wait_ge(S["c3_ready"], 1)

            def mix(t):
                dve.wait_ge(S["down_done"], t + 1)
                nc.vector.scalar_tensor_tensor(z3[:, tile_of(t)], ps[:, 4 + t % 2, :], c3b[:, 0:1], a2[:, tile_of(t)],
                                               ALU.add, ALU.add).then_inc(S["z3_ready"], 1)

            def finish(t):
                dve.wait_ge(S["r3_ready"], t + 1)
                link(nc.vector.tensor_tensor(tnorm[:, t % 2, :], z3[:, tile_of(t)], rstd[:, t % 2, :], ALU.mult))
                nc.vector.scalar_tensor_tensor(h1[:, tile_of(t)], tnorm[:, t % 2, :], cols[:, 6:7], h1[:, tile_of(t)],
                                               ALU.mult, ALU.add).then_inc(S["o_ready"], 1)

            def give(t):
                dve.wait_ge(S["o_turned"], t + 1)
                nc.vector.tensor_copy(o_tok[:, 4 * t:4 * t + 4, :], ps[:, 6 + t % 2, :].rearrange("p (t m) -> p t m", m=P))\
                    .then_inc(S["o_copied"], 1)

            for n, batch in enumerate(BATCHES):
                for t in batch:
                    mix(t)
                for t in batch:
                    finish(t)
                    if t > batch[0]:
                        give(t - 1)
                give(batch[-1])

        @block.scalar
        def _(act):
            act.dma_start(x_chan, x.rearrange("b c h w -> (b c) (h w)")).then_inc(S["xchan_in"], 16)
            steps = [0]

            def link(ins):
                steps[0] += 1
                ins.then_inc(S["chain_a"], 1)
                act.wait_ge(S["chain_a"], steps[0])

            nc.scalar.preload_act_table_set(NORM_SET)
            act.wait_ge(S["conv_in"], 16 * CONV_DMAS)
            link(nc.scalar.activation(bn_tmp[:, 0:1], bn_col[:, 4:5], ACT.Ln, bias=EPS))
            nc.scalar.activation(bn_tmp[:, 1:2], bn_tmp[:, 0:1], ACT.Exp, scale=-0.5).then_inc(S["bn_exp"], 1)

            def copy_counts(g):
                act.wait_ge(S["chunk_counted"], GROUP * (g + 1))
                if g >= 1:
                    act.wait_ge(S["counts_merged"], g)
                nc.scalar.activation(cnt.rearrange("p (a n) -> p a n", a=2), ps[:, 6:8, :], ACT.Copy)\
                    .then_inc(S["counts_copied"], 1)

            act.wait_ge(S["bn_ready"], 1)
            for t in range(TILES):
                act.wait_ge(S["conv1_done"], t + 1)
                nc.scalar.activation(y_relu[:, tile_of(t)], ps[0:B * CR, 4 + t % 2, :], ACT.Relu,
                                     bias=bn_tmp[:, 3:4], scale=bn_tmp[:, 2:3]).then_inc(S["relu_done"], 1)
            copy_counts(0)
            xp = x_pad.rearrange("p (c h) -> p c h", h=PAD)
            for t in range(TILES):
                act.wait_ge(S["turned"], t + 1)
                nc.scalar.activation(xp[:, CT * t:CT * t + CT, 1:IH + 1], ps[:, t % 4, :].rearrange("p (c h) -> p c h", h=IH),
                                     ACT.Copy).then_inc(S["x_ready"], 1)
            for j in range(3):
                for h2 in range(2):
                    n = 2 * j + h2
                    act.wait_ge(S["regrouped"], 3 * (n // 3) + 3)
                    nc.scalar.activation(
                        bass.AP(wd_s, j * IH + h2, [[9 * IH, P], [2, IH // 2], [3 * IH, 3]]),
                        ps[:, n // 3, 96 * (n % 3):96 * (n % 3) + 96].rearrange("p (h i) -> p h i", i=3),
                        ACT.Copy).then_inc(S["wds_ready"], 1)

            def rsqrt(src, k, var_sem, n, out_sem):
                act.wait_ge(S[var_sem], n)
                link(nc.scalar.activation(lnv[:, k, :], src, ACT.Ln, bias=EPS))
                nc.scalar.activation(rstd[:, k, :], lnv[:, k, :], ACT.Exp, scale=-0.5).then_inc(S[out_sem], 1)

            act.wait_ge(S["woc_ready"], 1)
            for s in range(TILES + 2):
                for j in range(3):
                    if j == 1 and 1 <= s <= TILES:
                        t = s - 1
                        if t == 0:
                            act.wait_ge(S["m3_ready"], 1)
                        act.wait_ge(S["cent_done"], t + 1)
                        if t >= 2:
                            act.wait_ge(S["var_done"], t - 1)
                        nc.scalar.activation(sq[:, t % 2, :], ps[:, 2 + t % 2, :], ACT.Square, bias=zb[:, 2:3])\
                            .then_inc(S["sq_ready"], 1)
                    if j == 2 and s >= 2:
                        t = s - 2
                        if t >= 2:
                            act.wait_ge(S["a1_ready"], t - 1)
                            act.wait_ge(S["rstd_ready"], t - 1)
                        rsqrt(ps[:, 4 + t % 2, :], t % 2, "var_done", t + 1, "rstd_ready")
                    if j == 2 and s < TILES:
                        act.wait_ge(S["prod_used"], 3 * (s + 1))
                        nc.scalar.activation(hb[:, tile_of(s)], ps[:, acc_bank(s), :], ACT.Identity,
                                             bias=ccols[:, 1:2]).then_inc(S["hb_ready"], 1)
                    if s < TILES:
                        for c in beside_product(3 * s + j):
                            if c % GROUP == GROUP - 1:
                                copy_counts(c // GROUP)
                if s == TILES:
                    for n in range(MB):
                        act.wait_ge(S["mask_turned"], n + 1)
                        nc.scalar.activation(mask_n[:, n, :], ps[:, 6 + n % 2, 0:256].bitcast(BF16), ACT.Copy)\
                            .then_inc(S["mask_n_ready"], 1)

            def z_square(k):
                act.wait_ge(S["z_done"], k + 1)
                if k >= 1:
                    act.wait_ge(S["zvar_done"], k)
                nc.scalar.activation(sq[:, 0, :], ps[:, norm_bank(k), :], ACT.Square, bias=zb[:, 1:2] if k == LAST else zb[:, 0:1])\
                    .then_inc(S["zsq_ready"], 1)

            def c_square(k):
                act.wait_ge(S["c1_done"], k + 1)
                if k >= 1:
                    act.wait_ge(S["var2_done"], k)
                nc.scalar.activation(sq[:, 1, :], ps[:, norm_bank(k), :], ACT.Square, bias=zb[:, 3:4]).then_inc(S["c1sq_ready"], 1)

            def z_rsqrt(k):
                if k >= 1:
                    act.wait_ge(S["h1_ready"], k)
                    act.wait_ge(S["zr_ready"], k)
                rsqrt(ps[:, norm_bank(k) + 1, :], 0, "zvar_done", k + 1, "zr_ready")

            def c_rsqrt(k):
                if k >= 1:
                    act.wait_ge(S["a2_ready"], k)
                    act.wait_ge(S["r2_ready"], k)
                rsqrt(ps[:, norm_bank(k) + 1, :], 1, "var2_done", k + 1, "r2_ready")

            def norms(kind, k):
                {"z": z_square, "v": z_rsqrt, "c": c_square, "w": c_rsqrt}[kind](k)

            for what, n in beside(*PLAN_S):
                if what == "norm":
                    norms(*n)
            for what, n in beside(*PLAN_T):
                if what == "norm":
                    norms(*n)
                    continue
                r, g, m = n // 8, n % 8 // 2, n % 2
                act.wait_ge(S["st_done"], n + 1)
                if r >= 3:
                    act.wait_ge(S["pv_used"], r - 2)
                nc.scalar.activation(probs[:, r % 3, g, m, :], ps[:, 2 + n % S_BANKS, :], ACT.Exp, scale=float(DH) ** -0.5)\
                    .then_inc(S["exp_done"], 1)
            for kind, k in TAIL_SLOTS:
                norms(kind, k)
            for turn in range(2):
                act.wait_ge(S["rt_step"], turn + 1)
                nc.scalar.activation(rt[:, 8:16], rt[:, 0:8], ACT.Exp, bias=rt[:, 48 + 2 * turn:49 + 2 * turn])\
                    .then_inc(S["rt_exp"], 1)
            fetch_experts(act, 1)
            act.wait_ge(S["rt_step"], 3)
            nc.scalar.activation(rt[:, 56:58], rt[:, 32:34], ACT.Exp, bias=rt[:, 52:53]).then_inc(S["rt_exp"], 1)
            nc.scalar.preload_act_table(ACT.Gelu)
            act.wait_ge(S["w_sel_in"], 16 * 4 * B * TOPK)

            def gelu(t):
                for n in range(B * TOPK):
                    act.wait_ge(S["up_done"], B * TOPK * t + n + 1)
                    if t >= 2:
                        act.wait_ge(S["down_done"], t - 1)
                    nc.scalar.activation(hid[:, t % 2, n, :], ps[:, n, :], ACT.Gelu, bias=b1_sel[:, n:n + 1])\
                        .then_inc(S["gelu_done"], 1)

            for batch in BATCHES:
                for t in batch:
                    gelu(t)
                nc.scalar.preload_act_table_set(NORM_SET)
                for t in batch:
                    if t >= 2:
                        act.wait_ge(S["r3_ready"], t - 1)
                        act.wait_ge(S["o_ready"], t - 1)
                    rsqrt(ps[:, 6 + t % 2, :], t % 2, "var3_done", t + 1, "r3_ready")

        @block.tensor
        def _(pe):
            def count(chunks):
                for c in chunks:
                    g, k = c // GROUP, c % GROUP
                    if k == 0 and g >= 1:
                        pe.wait_ge(S["counts_copied"], g)
                    pe.wait_ge(S["onehot"], c + 1)
                    for j in range(2):
                        last = pe.matmul(ps[:, 6 + j, :], col_hot[:, k, P * j:P * j + P], row_hot[:, k, :],
                                         start=(k == 0), stop=(k == GROUP - 1))
                    last.then_inc(S["chunk_counted"], 1)

            count(range(0, EARLY // 3))
            pe.wait_ge(S["xchan_in"], 16)
            pe.wait_ge(S["conv_in"], 16 * CONV_DMAS)
            for t in range(TILES):
                if t >= 2:
                    pe.wait_ge(S["relu_done"], t - 1)
                pe.matmul(ps[0:B * CR, 4 + t % 2, :], w1_bd[:, :], x_chan[:, tile_of(t)],
                          start=True, stop=True).then_inc(S["conv1_done"], 1)
            count(range(EARLY // 3, GROUP))
            pe.wait_ge(S["relu_done"], TILES)
            for t in range(IH // 2):
                n, k = t // 16, t % 16
                last = pe.matmul(ps[:, 4 + n, B * KK * k:B * KK * k + B * KK], y_relu[:, P * t:P * t + P], c2_bd[:, :],
                                 start=True, stop=True)
                if k == 15:
                    last.then_inc(S["conv2_done"], 1)
            count(range(GROUP, EARLY))
            pe.wait_ge(S["xtok_in"], 32)
            pe.wait_ge(S["ident_ready"], 1)
            for t in range(4 * TILES):
                if t % 4 == 0 and t >= 16:
                    pe.wait_ge(S["x_ready"], t // 4 - 3)
                last = pe.transpose(ps[:, (t // 4) % 4, P * (t % 4):P * (t % 4) + P], x_tok[:, t, :], id_f[:, :])
                if t % 4 == 3:
                    last.then_inc(S["turned"], 1)
            pe.wait_ge(S["wd_ready"], 2)
            pe.wait_ge(S["consts_ready"], 1)
            pe.wait_ge(S["x_ready"], TILES)
            for j in range(3):
                for h2 in range(2):
                    n = 2 * j + h2
                    for b in range(B):
                        last = pe.matmul(
                            ps[:, n // 3, 96 * (n % 3):96 * (n % 3) + 96].rearrange("p (h i) -> p h i", i=3),
                            regroup_m[:, (b * 2 + h2) * 3 + j, :],
                            bass.AP(a1, WT0 + b * KK + j, [[N, P], [B * KK, IH // 2], [3, 3]]),
                            start=(b == 0), stop=(b == B - 1))
                    last.then_inc(S["regrouped"], 1)
            pe.wait_ge(S["woc_ready"], 1)
            pe.transpose(ps[:, 3, 0:P], qkvo[:, 2, :], id_f[:, :]).then_inc(S["wvt_done"], 1)
            pe.wait_ge(S["wds_ready"], 6)

            def multiply_weights():
                pe.wait_ge(S["wvt_ready"], 1)
                pe.matmul(ps[:, 2, 0:P], wv_t[:, :], wo_c[:, :], start=True, stop=False)
                pe.matmul(ps[:, 2, 0:P], id_f[:, :], cent_m[:, :], start=False, stop=True)
                pe.matmul(ps[:, 2, 128:129], wo_c[:, :], cols[:, 2:3], start=True, stop=False)
                pe.matmul(ps[:, 2, 128:129], cent_m[:, :], cols[:, 3:4], start=False, stop=True)
                pe.matmul(ps[:, 2, 192:195], cent_m[:, :], ccols[:, :], start=True, stop=True).then_inc(S["m3_done"], 1)

            for s in range(TILES + 2):
                if 2 <= s < TILES:
                    if s == QKV_STEP + 1:
                        pe.wait_ge(S["qk_ready"], 2)
                    elif s == QKV_STEP + 2:
                        pe.wait_ge(S["vpad_ready"], 2)
                    else:
                        pe.wait_ge(S["hb_ready"], s - 1)
                for j in range(3):
                    if s < TILES:
                        n = 3 * s + j
                        pe.wait_ge(S["prod_added"], n + 1)
                        for i in (0, 2):
                            last = pe.matmul(ps[:, acc_bank(s), :], shift_m[:, j, :], prod[:, n % 4, i, :],
                                             start=(i == 0 and j == 0), stop=(i == 2 and j == 2))
                        last.then_inc(S["prod_used"], 1)
                        count(beside_product(n))
                    if s == 0 and j == 0:
                        multiply_weights()
                    if j == 0 and 1 <= s <= TILES:
                        t = s - 1
                        if t == 0:
                            pe.wait_ge(S["m3_ready"], 1)
                        pe.wait_ge(S["hb_ready"], t + 1)
                        if t >= 2:
                            pe.wait_ge(S["a1_ready"], t - 1)
                        pe.matmul(ps[:, 2 + t % 2, :], cent_m[:, :], hb[:, tile_of(t)],
                                  start=True, stop=True).then_inc(S["cent_done"], 1)
                    if j == 1 and s >= 2:
                        t = s - 2
                        pe.wait_ge(S["sq_ready"], t + 1)
                        if t >= 2:
                            pe.wait_ge(S["rstd_ready"], t - 1)
                        pe.matmul(ps[:, 4 + t % 2, :], mean_m[:, :], sq[:, t % 2, :], start=True, stop=True)\
                            .then_inc(S["var_done"], 1)
                if s == QKV_STEP:
                    pe.wait_ge(S["a1_ready"], 1)
                    pe.wait_ge(S["hb_ready"], s + 1)
                    for n in range(2):
                        pe.matmul(ps[:, n, :], qkvo[:, n, :], a1[:, 0:TILE], start=True, stop=True)\
                            .then_inc(S["qkv_done"], 1)
                    pe.wait_ge(S["qk_ready"], 1)
                    for m in range(MB):
                        last = pe.matmul(ps[:, 0, P * m:P * m + P], a1[:, P * m:P * m + P], qkvo[:, 2, :],
                                         start=True, stop=True)
                    last.then_inc(S["qkv_done"], 1)
                if s == TILES:
                    pe.wait_ge(S["mask_diag"], MB)
                    pe.wait_ge(S["late_consts"], 2)
                    for n in range(MB):
                        if n >= 2:
                            pe.wait_ge(S["mask_n_ready"], n - 1)
                        for m in range(MB):
                            last = pe.transpose(ps[:, 6 + n % 2, 64 * m:64 * m + 64].bitcast(BF16),
                                                mask_t[:, m, P * n:P * n + P], id_b[:, :])
                        last.then_inc(S["mask_turned"], 1)

            def z_project(k):
                t, bank = (k + 1) % TILES, norm_bank(k)
                if 1 <= k < LAST:
                    pe.wait_ge(S["a2_ready"], k)
                if t == 0:
                    pe.wait_ge(S["att_ready"], 1)
                    pe.matmul(ps[:, bank, :], cent_m[:, :], a1[:, tile_of(t)], start=True, stop=False)
                    pe.matmul(ps[:, bank, :], wo_c[:, :], att, start=False, stop=True).then_inc(S["z_done"], 1)
                else:
                    pe.matmul(ps[:, bank, :], m3[:, :], a1[:, tile_of(t)], start=True, stop=True)\
                        .then_inc(S["z_done"], 1)

            def z_var(k):
                pe.wait_ge(S["zsq_ready"], k + 1)
                if 1 <= k < LAST:
                    pe.wait_ge(S["r2_ready"], k)
                pe.matmul(ps[:, norm_bank(k) + 1, :], mean_m[:, :], sq[:, 0, :], start=True, stop=True)\
                    .then_inc(S["zvar_done"], 1)

            def c_project(k):
                pe.wait_ge(S["h1_ready"], k + 1)
                pe.matmul(ps[:, norm_bank(k), :], cent_m[:, :], h1[:, tile_of((k + 1) % TILES)], start=True, stop=True)\
                    .then_inc(S["c1_done"], 1)

            def c_var(k):
                pe.wait_ge(S["c1sq_ready"], k + 1)
                pe.wait_ge(S["zr_ready"], k + 1)
                pe.matmul(ps[:, norm_bank(k) + 1, :], mean_m[:, :], sq[:, 1, :], start=True, stop=True)\
                    .then_inc(S["var2_done"], 1)

            def norms(kind, k):
                {"z": z_project, "v": z_var, "c": c_project, "w": c_var}[kind](k)

            pe.wait_ge(S["a1_ready"], TILES)
            pe.wait_ge(S["mask_n_ready"], MB)
            pe.wait_ge(S["stacks_in"], 16 * STACK_DMAS)
            for what, n in beside(*PLAN_S):
                if what == "norm":
                    norms(*n)
                    continue
                h, nb = n // MB, n % MB
                if n >= S_BANKS:
                    pe.wait_ge(S["s_maxed"], n - S_BANKS + 1)
                pe.matmul(ps[:, 2 + n % S_BANKS, :], q_stack[0:KROWS, h, P * nb:P * nb + P], k_stack[0:KROWS, h, :],
                          start=True, stop=False)
                pe.matmul(ps[:, 2 + n % S_BANKS, :], id_b[:, :], mask_n[:, nb, :], start=False, stop=True)\
                    .then_inc(S["s_done"], 1)
            pe.wait_ge(S["s_maxed"], HEADS * MB)
            pe.wait_ge(S["vpad_ready"], 2)
            pe.transpose(ps[0:HEADS * MB, 6, 0:P], nmax[:, :, :].rearrange("p h m -> p (h m)"), id_f[:, :])\
                .then_inc(S["nmax_turned"], 1)

            def weigh(r):
                u, hp, half = ROUNDS[r]
                pe.wait_ge(S["exp_done"], 8 * (r + 1))
                if r == 0:
                    pe.wait_ge(S["nm_split"], 1)
                for m in range(2):
                    for g in range(4):
                        head = head_of(u, hp, g)
                        last = pe.matmul(ps[32 * g:32 * g + 32, 6 + u, :],
                                         v_pad[:, 2 * half + m, 32 * head:32 * head + 32], probs[:, r % 3, g, m, :],
                                         start=(hp == 0 and half == 0 and m == 0), stop=(hp == 1 and half == 1 and m == 1),
                                         skip_group_check=True)
                last.then_inc(S["pv_used"], 1)

            first = True
            for what, n in beside(*PLAN_T):
                if what == "norm":
                    norms(*n)
                    continue
                if first:
                    pe.wait_ge(S["nm_in"], 48)
                    first = False
                r, g, m = n // 8, n % 8 // 2, n % 2
                u, hp, half = ROUNDS[r]
                head = head_of(u, hp, g)
                if n >= S_BANKS:
                    pe.wait_ge(S["exp_done"], n - S_BANKS + 1)
                o = slice(P * (2 * half + m), P * (2 * half + m) + P)
                pe.matmul(ps[:, 2 + n % S_BANKS, :], k_stack[0:KROWS, head, o], q_stack[0:KROWS, head, :], start=True, stop=False)
                pe.matmul(ps[:, 2 + n % S_BANKS, :], id_b[:, :], mask_t[:, 2 * half + m, :], start=False, stop=True)\
                    .then_inc(S["st_done"], 1)
                if n % 8 == 3 and r >= 1:
                    weigh(r - 1)
            weigh(len(ROUNDS) - 1)
            norms(*TAIL_SLOTS[0])
            pe.wait_ge(S["pv_copied"], 1)
            for bank, m in ((4, sel_v), (5, sel_d)):
                for u in range(2):
                    last = pe.matmul(ps[:, bank, :], m[:, u, :], pv_sb[:, u, :], start=(u == 0), stop=(u == 1))
            last.then_inc(S["gathered"], 1)
            for kind, k in TAIL_SLOTS[1:]:
                norms(kind, k)
            pe.wait_ge(S["ms_ready"], 1)
            pe.matmul(ps[0:B, 0, 0:NE], msum[:, :], wr_st[:, :], start=True, stop=True).then_inc(S["lg_done"], 1)
            pe.wait_ge(S["rt_pe"], 1)
            pe.matmul(ps[0:B, 0, NE:2 * NE], ones2[:, 0:B], rt[:, 16:24], start=True, stop=True).then_inc(S["lg_done"], 1)
            pe.wait_ge(S["topw"], 2)
            pe.matmul(ps[:, 0, 64:68], ones2[:, :], rt[:, 64:68], start=True, stop=True)
            pe.matmul(ps[:, 0, 72:74], selb[:, :], rt[:, 60:62], start=True, stop=True).then_inc(S["w_bc_done"], 1)
            pe.wait_ge(S["b2m_ready"], 1)
            pe.matmul(ps[:, 0, 80:81], cent_m[:, :], b2_mix[:, :], start=True, stop=True).then_inc(S["c3_done"], 1)
            pe.wait_ge(S["c3_ready"], 1)

            def up(t):
                for n in range(B * TOPK):
                    if t >= 1:
                        pe.wait_ge(S["gelu_done"], B * TOPK * (t - 1) + n + 1)
                    pe.matmul(ps[:, n, :], w1_sel[:, n, :], a2[:, tile_of(t)], start=True, stop=True)\
                        .then_inc(S["up_done"], 1)

            def down(t):
                if t >= 2:
                    pe.wait_ge(S["z3_ready"], t - 1)
                pe.wait_ge(S["gelu_done"], B * TOPK * (t + 1))
                for s in range(TOPK):
                    for b in range(B):
                        last = pe.matmul(ps[D * b:D * b + D, 4 + t % 2, :], w2_c[:, b * TOPK + s, :],
                                         hid[:, t % 2, b * TOPK + s, :], start=(s == 0), stop=(s == TOPK - 1),
                                         skip_group_check=True)
                last.then_inc(S["down_done"], 1)

            def var3(t):
                pe.wait_ge(S["sq3_ready"], t + 1)
                if t >= 2:
                    pe.wait_ge(S["o_copied"], t - 1)
                pe.matmul(ps[:, 6 + t % 2, :], mean_m[:, :], sq[:, t % 2, :], start=True, stop=True)\
                    .then_inc(S["var3_done"], 1)

            def turn_back(t):
                pe.wait_ge(S["o_ready"], t + 1)
                for k in range(4):
                    last = pe.transpose(ps[:, 6 + t % 2, P * k:P * k + P], h1[:, TILE * t + P * k:TILE * t + P * k + P],
                                        id_f[:, :])
                last.then_inc(S["o_turned"], 1)

            pe.wait_ge(S["w2c_ready"], 1)
            up(0)
            for batch in BATCHES:
                for t in batch:
                    if t + 1 < TILES:
                        up(t + 1)
                    down(t)
                for t in batch:
                    var3(t)
                    if t > batch[0]:
                        turn_back(t - 1)
                turn_back(batch[-1])


_INS = ['x', 'L0_tok_conv1_w', 'L0_tok_conv1_b', 'L0_tok_bn_gamma', 'L0_tok_bn_beta', 'L0_tok_bn_mean', 'L0_tok_bn_var',
        'L0_tok_conv2_w', 'L0_tok_conv2_b', 'L0_attn_edge_index', 'L0_attn_Wq', 'L0_attn_bq', 'L0_attn_Wk', 'L0_attn_bk',
        'L0_attn_Wv', 'L0_attn_bv', 'L0_attn_Wo', 'L0_attn_bo', 'L0_attn_gamma', 'L0_attn_beta', 'L0_ffn_Wr', 'L0_ffn_br',
        'L0_ffn_W1', 'L0_ffn_b1', 'L0_ffn_W2', 'L0_ffn_b2', 'L0_ffn_gamma', 'L0_ffn_beta']
_OUTS = [((2, 4096, 64), 'float32')]


def kernel(**inputs):
    import numpy as _np
    import concourse.bacc as _bacc
    from concourse import mybir as _mybir
    from concourse.bass_utils import run_bass_kernel_spmd as _run

    nc = _bacc.Bacc("TRN2", target_bir_lowering=False, num_devices=1)
    arrays, args = {}, []
    for name in _INS:
        a = _np.ascontiguousarray(inputs[name])
        arrays[f"in_{name}_dram"] = a
        args.append(nc.dram_tensor(f"in_{name}_dram", a.shape, _mybir.dt.from_np(a.dtype), kind="ExternalInput").ap())
    for i, (shape, dtype) in enumerate(_OUTS):
        dt = _mybir.dt.from_np(_np.dtype(dtype))
        args.append(nc.dram_tensor(f"out_{i}_dram", shape, dt, kind="ExternalOutput").ap())
    with nc.allow_non_contiguous_dma(reason="columns of small vectors"):
        vit_tower_kernel(nc, *args)
    r = _run(nc, [arrays], core_ids=[0])
    got = tuple(r.results[0][f"out_{i}_dram"] for i in range(len(_OUTS)))
    return got[0]
```

```python
from contextlib import ExitStack

import concourse.bass as bass
from concourse import mybir

ALU = mybir.AluOpType
ACT = mybir.ActivationFunctionType
AX = mybir.AxisListType.X
F32 = mybir.dt.float32
BF16 = mybir.dt.bfloat16
FP16 = mybir.dt.float16
I32 = mybir.dt.int32
U32 = mybir.dt.uint32

P = 128
EPS = 1e-5
MASKED = -1e30
NORM_SET = "natural_log_exp_and_others"


def vit_tower_kernel(
    nc, x, conv1_w, conv1_b, bn_gamma, bn_beta, bn_mean, bn_var, conv2_w, conv2_b, edge_index,
    Wq, bq, Wk, bk, Wv, bv, Wo, bo, attn_gamma, attn_beta, Wr, br, W1, b1, W2, b2, ffn_gamma, ffn_beta, out,
):
    B, C, IH, IW = x.shape
    CR = conv1_w.shape[0]
    KK = conv2_w.shape[0]
    D = IW
    N = C * IH
    EDGES = edge_index.shape[1]
    NODES = 512
    H = 8
    DH = D // H
    HEADS = B * H
    NE, _, HID = W1.shape
    TOPK = 2
    CAPACITY = float(-(-B * N * 5 // (4 * NE)))
    TILE = 512
    TILES = N // TILE
    CT = TILE // IH
    PAD = IH + 2
    assert (B, D, TILE, NODES, HID) == (2, 64, 512, 512, P)

    CHUNKS = EDGES // P
    GROUP = 26
    GROUPS = -(-CHUNKS // GROUP)
    FIELD = 4096
    assert GROUP * P * (FIELD + 1) < 2 ** 24 and GROUP * P < FIELD
    HOT = 16

    Q_PART = [0, 0, 1, 1, 0, 2, 1, 2]
    K_PART = [0, 1, 0, 1, 2, 0, 2, 1]
    MAXROW = DH * len(Q_PART)
    KROWS = MAXROW + 3
    MB = NODES // P

    with ExitStack() as ctx:
        def sb(name, shape, dt=F32):
            return ctx.enter_context(nc.sbuf_tensor(name, shape, dt))

        def sem(name):
            return ctx.enter_context(nc.semaphore(name))

        region_a = sb("region_a", [P, N])
        region_b = sb("region_b", [P, N])
        x_chan = region_a[:, :]
        x_tok = region_b[:, :].rearrange("p (t m) -> p t m", m=P)
        q_stack = region_a[:, :].bitcast(BF16).rearrange("p (h n) -> p h n", h=HEADS)
        k_stack = region_b[:, :].bitcast(BF16).rearrange("p (h n) -> p h n", h=HEADS)
        region_c = sb("region_c", [P, 17024])
        x_pad = region_c[:, 0:C * PAD]
        PROD0 = C * PAD
        prod = region_c[:, PROD0:PROD0 + 12 * TILE].rearrange("p (s i n) -> p s i n", s=4, i=3)
        y_relu = region_c[0:B * CR, PROD0:PROD0 + N]
        HOT0 = PROD0 + 12 * TILE
        col_hot = region_c[:, HOT0:HOT0 + HOT * 128].bitcast(BF16).rearrange("p (s n) -> p s n", s=HOT)
        QK0 = HOT0 + HOT * 128
        qk_part = region_c[:, QK0:QK0 + 3 * TILE].bitcast(BF16).rearrange("p (s q n) -> p s q n", s=3, q=2)
        V0 = QK0 + 3 * TILE
        v_pad = region_c[:, V0:V0 + 4 * TILE].rearrange("p (m n) -> p m n", m=MB)
        tnorm = region_c[:, V0 + 4 * TILE:V0 + 6 * TILE].rearrange("p (s n) -> p s n", s=2)
        probs = region_c[:, 0:3 * 8 * TILE].rearrange("p (r g m n) -> p r g m n", r=3, g=4, m=2)
        pv_sb = region_c[:, QK0:QK0 + 2 * TILE].rearrange("p (q n) -> p q n", q=2)
        att = region_c[:, QK0 + 2 * TILE:QK0 + 3 * TILE]
        hid = region_c[:, 0:2 * 4 * TILE].rearrange("p (s e n) -> p s e n", s=2, e=4)
        sq3 = region_b[:, 0:4 * TILE].rearrange("p (s n) -> p s n", s=4)
        rstd3 = region_b[:, 4 * TILE:8 * TILE].rearrange("p (s n) -> p s n", s=4)
        lnv3 = region_a[:, 0:4 * TILE].rearrange("p (s n) -> p s n", s=4)
        hot_tmp = region_c[:, V0 + 4 * TILE:V0 + 5 * TILE].rearrange("p (s n) -> p s n", s=2)
        o_tok = region_c[:, 8 * TILE:8 * TILE + N].rearrange("p (t m) -> p t m", m=P)
        assert 3 * 8 * TILE <= QK0 and V0 + 6 * TILE == region_c.shape[1]
        hb = sb("hb", [P, N])
        h1 = sb("h1", [P, N])
        a1 = sb("a1", [P, N])
        a2 = sb("a2", [P, N])
        z3 = a1
        row_hot = h1[:, :].bitcast(BF16).rearrange("p (s n) -> p s n", s=HOT)
        qk = a2[:, 0:2 * TILE].rearrange("p (q n) -> p q n", q=2)
        qk_res = a2[:, 2 * TILE:4 * TILE].rearrange("p (q n) -> p q n", q=2)
        cnt = a2[:, 4 * TILE:6 * TILE].bitcast(I32)
        own_edges = a2[:, 4 * TILE:6 * TILE]
        cnt_acc = a2[:, 6 * TILE:8 * TILE].bitcast(I32)
        regroup_m = a1[:, 0:12 * P].rearrange("p (k n) -> p k n", n=P)
        WT0 = 12 * P
        wd_t = a1[:, WT0:WT0 + IH // 2 * B * KK].rearrange("p (t b k) -> p t b k", b=B, k=KK)
        warm = a1[:, 7 * TILE:8 * TILE]
        mask_t = sb("mask_t", [P, MB, NODES], BF16)
        mask_n = sb("mask_n", [P, MB, NODES], BF16)
        edge_region = sb("edge_region", [P, 8 * CHUNKS])
        edges = edge_region[:, 0:2 * CHUNKS].bitcast(I32).rearrange("p (r c) -> p r c", r=2)
        edge_row, edge_col, edge_hi, edge_val, edge_ncol, edge_nval = (
            edge_region[:, k * CHUNKS:k * CHUNKS + CHUNKS] for k in range(2, 8))
        iota_i = mask_n[:, 0:2, :].rearrange("p a n -> p (a n)").bitcast(I32)
        iota = sb("iota", [P, NODES], FP16)

        id_f = sb("id_f", [P, P])
        id_b = sb("id_b", [P, P], BF16)
        mean_m = sb("mean_m", [P, P])
        cent_m = sb("cent_m", [P, P])
        shift_m = sb("shift_m", [P, 3, P])
        sel_v = sb("sel_v", [P, D])
        sel_d = sb("sel_d", [P, D])
        w1_bd = sb("w1_bd", [P, B * CR])
        c2_bd = sb("c2_bd", [B * CR, B * KK])
        c2b_bc = sb("c2b_bc", [P, B * KK])
        bn_col = sb("bn_col", [B * CR, 5])
        bn_tmp = sb("bn_tmp", [B * CR, 4])
        wd_s = sb("wd_s", [P, 3, 3, IH])
        qkvo = sb("qkvo", [P, 4, P])
        cols = sb("cols", [P, 8])
        bv_bc = sb("bv_bc", [P, P])
        wr_st = sb("wr_st", [P, NE])
        br_bc = sb("br_bc", [B, NE])
        wo_c = sb("wo_c", [P, P])
        wo_mean = sb("wo_mean", [P, 1])
        wv_t = sb("wv_t", [P, P])
        m3 = sb("m3", [P, P])
        ccols = sb("ccols", [P, 3])
        mark = sb("mark", [1, 4])
        ones_b = sb("ones_b", [HEADS * MB, 2, P], BF16)
        zb = sb("zb", [P, 4])
        sq = sb("sq", [P, 2, TILE])
        lnv = sb("lnv", [P, 2, TILE])
        rstd = sb("rstd", [P, 2, TILE])
        nmax = sb("nmax", [P, HEADS, MB])
        nm = sb("nm", [4 * MB, P])
        nm_res = sb("nm_res", [4 * MB, P])
        nm_part = sb("nm_part", [4 * MB, 3, P], BF16)
        a2_sum = sb("a2_sum", [P, TILES])
        msum = sb("msum", [P, 2])
        mcol = sb("mcol", [P, 1])
        rt = sb("rt", [B, 96])
        rt_idx = sb("rt_idx", [B, 8], U32)
        eye2 = sb("eye2", [B, B])
        ones2 = sb("ones2", [B, P])
        selb = sb("selb", [B, P])
        wb4 = sb("wb4", [P, B * TOPK])
        wcol = sb("wcol", [P, TOPK])
        w1_sel = sb("w1_sel", [P, B * TOPK, HID])
        w2_sel = sb("w2_sel", [P, B * TOPK, D])
        w2_mean = sb("w2_mean", [P, B * TOPK])
        w2_c = sb("w2_c", [P, B * TOPK, D])
        b1_sel = sb("b1_sel", [P, B * TOPK])
        b2_sel = sb("b2_sel", [P, TOPK])
        b2_mix = sb("b2_mix", [P, 1])
        c3b = sb("c3b", [P, 1])

        ps = ctx.enter_context(nc.psum_tensor("ps", [P, 8, TILE], F32))
        part_dram = nc.dram_tensor("part_dram", (3, 2, P, TILE), BF16, kind="Internal").ap()

        names = """warm_ready zeroed chain_v chain_a chain_g iota_ready ident_ready consts_ready late_consts
            edges_in edges_ready xtok_in conv1_in conv2_in bn_in weights_in
            onehot hot_squared cols_hot chunk_counted counts_copied counts_merged own_edges own_counted mask_ready mask_turned mask_n_ready
            bn_exp bn_ready conv1_done relu_done conv2_done wd_ready regrouped wds_ready turned x_ready
            woc_ready wvt_done wvt_ready m3_done m3_ready
            products prod_third prod_half prod_added prod_used part_ready hb_ready cent_done sq_ready var_done rstd_ready a1_ready
            qkv_done qk_ready qk_parts qk_rest parts_out stacks_in vpad_ready
            s_done s_maxed nmax_turned nm_split
            st_done exp_done pv_used pv_copied gathered att_ready
            z_done zsq_ready zvar_done zr_ready h1_ready c1_done c1sq_ready var2_done r2_ready a2_ready
            ms_ready lg_done rt_step rt_exp rt_pe w_bc_done topw idx_ready b1_in b2_in w2_in w2c_ready b2m_ready c3_done c3_ready
            up_done gelu_done down_done z3_ready sq3_ready var3_done r3_ready o_ready o_turned o_copied o_copied_late stored""".split()
        S = {n: sem(n) for n in names}
        XQ = 4
        xchan_in = [sem(f"xchan_in_{q}") for q in range(XQ)]
        nm_in = [sem(f"nm_in_{q}") for q in range(4)]
        w1_in = [sem(f"w1_in_{n}") for n in range(B * TOPK)]

        def cols_of(dram, pattern):
            return bass.AP(dram.tensor, dram.offset, pattern)

        def tile_of(t):
            return slice(TILE * t, TILE * t + TILE)

        CONV2_DMAS = B + 1
        WEIGHT_DMAS = 4 * B + 8 + 3
        STACK_DMAS = 2 * (len(Q_PART) + KROWS - MAXROW)
        SLOTS = [(kind, k) for k in range(TILES) for kind in "zvcw"]
        ROUNDS = [(u, hp, half) for u in range(2) for hp in range(2) for half in range(2)]

        def beside(steps, slots, lag=0):
            plan = []
            for n, step in enumerate(steps):
                plan.append(step)
                plan += [("norm", slot) for k, slot in enumerate(slots)
                         if n == 2 + k * (len(steps) - 4) // len(slots) + lag]
            return plan

        PAIRS = HEADS * MB // 2
        QUARTER = PAIRS // 4
        WIDE = QUARTER + 4
        NARROW_T = 2 * (PAIRS - WIDE)
        STEPS = []
        for p in range(PAIRS):
            STEPS += [("maxima", p)]
            if p >= QUARTER and p % QUARTER == 0:
                STEPS += [("turn", p // QUARTER - 1)]
            if p >= WIDE:
                STEPS += [("weights", 2 * (p - WIDE) + k) for k in range(2)]
        STEPS += [("turn", 3)] + [("weights", n) for n in range(NARROW_T, 2 * PAIRS)]
        PLAN = (STEPS, SLOTS[0:4 * (TILES - 3)])

        def maxima_bank(p):
            return 4 if p % 2 == 0 and p < WIDE else 2

        def weights_bank(n):
            return 4 + n % 2 if n < NARROW_T else 2 + n % 4

        LAG = 2
        PV_STEP, GATHER_STEP = HEADS * MB // 2 + 6, HEADS * MB // 2 + 12
        LAST = TILES - 1
        WARM_UP, WARM = 3, (3, 1, 4)
        BEFORE_PV = [("z", LAST - 2), ("v", LAST - 2)]
        BEHIND = [("c", LAST - 2), ("z", LAST - 1), ("w", LAST - 2), ("v", LAST - 1), ("z", LAST), ("v", LAST), ("c", LAST - 1),
                  ("c", LAST), ("w", LAST - 1), ("w", LAST)]

        def second_slot(k):
            return 0 if k == LAST else 1

        def norm_bank(k):
            return {LAST - 1: 2, LAST: 4}.get(k, 0)

        FIRST, EARLY = 4, 16
        COUNT_STEPS = 3 * TILES - 2
        QKV_STEP = 2

        def acc_bank(s):
            return (s - (QKV_STEP if s > QKV_STEP else 0)) % 2

        ORDER = (0, 2, 1)
        LONE = 3 * TILES - 2

        def centred_bank(t):
            return 2 if t < TILES - 1 else acc_bank(TILES - 2)

        SPLIT_STEP = 3 * QKV_STEP + 3

        def third_by_pool(n):
            return n % 3 == 2 and 3 <= n < 3 * TILES - 1

        def wait_for_product_buffer(eng, n):
            if n >= 4 and (n - 4) % 3 == 2:
                eng.wait_ge(S["hb_ready"], (n - 4) // 3 + 1)
            elif n >= 4:
                eng.wait_ge(S["prod_used"], products_used(n - 4))

        def multiply_rows(eng, n, first, rows):
            t, j = n // 3, ORDER[n % 3]
            return eng.tensor_tensor(
                prod[:, n % 4, first:first + rows, :].rearrange("p i (c h) -> p i c h", h=IH),
                bass.AP(region_c, CT * t * PAD + first, [[region_c.shape[1], P], [1, rows], [PAD, CT], [1, IH]]),
                bass.AP(wd_s, j * IH + 3 * IH * first, [[9 * IH, P], [3 * IH, rows], [0, CT], [1, IH]]),
                ALU.mult)

        def products_used(n):
            return 2 * (n // 3) + n % 3 + 1

        def beside_product(n):
            def bound(m):
                return min(CHUNKS, EARLY + (CHUNKS - EARLY) * m // COUNT_STEPS)
            return range(bound(n), bound(n + 1))

        def ends_group(c):
            return c % GROUP == GROUP - 1 or c == CHUNKS - 1

        SCALAR_COLS = (2, 4)

        def by_scalar(c):
            return c >= EARLY and c % 5 in SCALAR_COLS

        def scalar_chunks(c):
            return sum(by_scalar(k) for k in range(c + 1))

        def head_of(u, hp, g):
            return 8 * u + 4 * hp + g

        BATCHES = [range(0, 4), range(4, TILES)]

        def var3_bank(t):
            return 6 + t % 2 if t < 4 else (7, 0, 1, 2)[t - 4]

        def turn_bank(t):
            return 6 if t < 4 else 6 + t % 2

        block = ctx.enter_context(nc.Block())

        def expert_of(eng, n):
            return eng.value_load(rt_idx[n // TOPK:n // TOPK + 1, n % TOPK:n % TOPK + 1], min_val=0, max_val=NE - 1)

        @block.sync
        def _(sp):
            sp.dma_start(edges[:, :, :], edge_index.rearrange("r (p c) -> p r c", p=P)).then_inc(S["edges_in"], 16)
            for n, v in enumerate((conv1_b, bn_gamma, bn_beta, bn_mean, bn_var)):
                sp.dma_start(bn_col[:, n:n + 1], cols_of(v, [[0, B], [1, CR], [1, 1]])).then_inc(S["bn_in"], 16)
            sp.wait_ge(S["zeroed"], 1)
            for b in range(B):
                sp.dma_start(w1_bd[C * b:C * b + C, CR * b:CR * b + CR],
                             conv1_w.rearrange("o c -> c o")).then_inc(S["conv1_in"], 16)
            for b in range(B):
                sp.dma_start(c2_bd[CR * b:CR * b + CR, KK * b:KK * b + KK],
                             conv2_w.rearrange("k o -> o k")).then_inc(S["conv2_in"], 16)
            sp.dma_start(c2b_bc[:, :], cols_of(conv2_b, [[0, P], [0, B], [1, KK]])).then_inc(S["conv2_in"], 16)
            for b in range(B):
                sp.dma_start(x_tok.rearrange("p t (b d) -> p t b d", b=B)[:, :, b, :],
                             x[b].rearrange("c h w -> (c h) w").rearrange("(t p) w -> p t w", p=P))\
                    .then_inc(S["xtok_in"], 16)
            for n, w in enumerate((Wq, Wk, Wv, Wo)):
                for b in range(B):
                    sp.dma_start(qkvo[D * b:D * b + D, n, D * b:D * b + D], w).then_inc(S["weights_in"], 16)
            for n, v in enumerate((bq, bk, bv, bo, attn_gamma, attn_beta, ffn_gamma, ffn_beta)):
                sp.dma_start(cols[:, n:n + 1], cols_of(v, [[0, B], [1, D], [1, 1]])).then_inc(S["weights_in"], 16)
            sp.dma_start(bv_bc[:, :], cols_of(bv, [[0, P], [0, B], [1, D]])).then_inc(S["weights_in"], 16)
            sp.dma_start(wr_st[:, :], cols_of(Wr, [[0, B], [NE, D], [1, NE]])).then_inc(S["weights_in"], 16)
            sp.dma_start(br_bc[:, :], cols_of(br, [[0, B], [1, NE]])).then_inc(S["weights_in"], 16)
            sp.wait_ge(S["late_consts"], 1)
            sp.wait_ge(S["conv1_done"], TILES)
            for n in range(MAXROW, KROWS):
                sp.dma_start(q_stack[n:n + 1, :, :], ones_b[:, 0, :]).then_inc(S["stacks_in"], 16)
            sp.wait_ge(S["turned"], TILES)
            for n in range(MAXROW, KROWS):
                sp.dma_start(k_stack[n:n + 1, :, :], ones_b[:, 1, :]).then_inc(S["stacks_in"], 16)
            sp.wait_ge(S["qk_parts"], 3)
            for n in range(3):
                sp.dma_start(part_dram[n].rearrange("q p n -> p q n"), qk_part[:, n, :, :]).then_inc(S["parts_out"], 16)
            sp.wait_ge(S["parts_out"], 48)
            for u in range(len(Q_PART)):
                for which, stack, part in ((0, q_stack, Q_PART[u]), (1, k_stack, K_PART[u])):
                    sp.dma_start(stack[DH * u:DH * u + DH, :, :],
                                 part_dram[part, which].rearrange("(h d) n -> d h n", d=DH)).then_inc(S["stacks_in"], 16)
            for q in range(4):
                sp.wait_ge(S["nm_split"], q + 1)
                for n in range(3):
                    sp.dma_start(q_stack[MAXROW + n:MAXROW + n + 1, 4 * q:4 * q + 4, :], nm_part[:, n, :]).then_inc(nm_in[q], 16)
            sp.wait_ge(S["idx_ready"], 1)
            experts = []
            for n in range(B * TOPK):
                o = slice(D * (n // TOPK), D * (n // TOPK) + D)
                experts.append(expert_of(sp, n))
                sp.dma_start(w1_sel[o, n, :], W1[bass.ds(experts[n], 1), :, :].rearrange("e d f -> (e d) f"))\
                    .then_inc(w1_in[n], 16)
            for n, e in enumerate(experts):
                o = slice(D * (n // TOPK), D * (n // TOPK) + D)
                sp.dma_start(b2_sel[o, n % TOPK:n % TOPK + 1], b2[bass.ds(e, 1), :].rearrange("e d -> d e"))\
                    .then_inc(S["b2_in"], 16)
            for t in range(TILES):
                if t in BATCHES[-1]:
                    sp.wait_ge(S["o_copied_late"], t - BATCHES[-1][0] + 1)
                else:
                    sp.wait_ge(S["o_copied"], t + 1)
                for b in range(B):
                    sp.dma_start(out[b].rearrange("(t p) d -> p t d", p=P)[:, 4 * t:4 * t + 4, :],
                                 o_tok[:, 4 * t:4 * t + 4, D * b:D * b + D]).then_inc(S["stored"], 16)
            sp.wait_ge(S["stored"], 16 * B * TILES)

        @block.gpsimd
        def _(pool):
            steps = [0]

            def then(ins):
                steps[0] += 1
                ins.then_inc(S["chain_g"], 1)
                pool.wait_ge(S["chain_g"], steps[0])

            def diagonal(view, base, pattern):
                then(pool.affine_select(out=view, in_=view, compare_op=ALU.not_equal, fill=1.0, base=base,
                                        pattern=pattern, channel_multiplier=1))

            then(pool.iota(iota_i, [[1, NODES]], base=0, channel_multiplier=0))
            pool.tensor_copy(iota[:, :], iota_i).then_inc(S["iota_ready"], 1)
            pool.wait_ge(S["zeroed"], 2)
            diagonal(id_f[:, :], 0, [[-1, P]])
            then(pool.memset(mark[:, 0:1], 0.0))
            pool.memset(mark[:, 1:2], 0.0).then_inc(S["ident_ready"], 1)
            then(pool.memset(own_edges, 0.0))
            for m in range(MB):
                view = own_edges[:, NODES * (m % 2):NODES * (m % 2) + NODES]
                own = pool.affine_select(out=view, in_=view, compare_op=ALU.not_equal, fill=(1.0, float(FIELD))[m // 2],
                                         base=P * m, pattern=[[-1, NODES]], channel_multiplier=1)
                if m < MB - 1:
                    then(own)
            own.then_inc(S["own_edges"], 1)
            for b in range(B):
                o = slice(D * b, D * b + D)
                for j in range(3):
                    for h2 in range(2):
                        diagonal(regroup_m[D * h2:D * h2 + D, (b * 2 + h2) * 3 + j, o], j - 1, [[-1, D]])
            xp = x_pad.rearrange("p (c h) -> p c h", h=PAD)
            then(pool.memset(xp[:, :, 0:1], 0.0))
            then(pool.memset(xp[:, :, PAD - 1:PAD], 0.0))
            for b in range(B):
                o = slice(D * b, D * b + D)
                then(pool.memset(mean_m[o, o], 1.0 / D))
                for j in range(3):
                    diagonal(shift_m[o, j, o], 1 - j, [[-1, D]])
            pool.tensor_tensor(cent_m[:, :], id_f[:, :], mean_m[:, :], ALU.subtract).then_inc(S["consts_ready"], 1)
            then(pool.memset(ones_b[:, 0, :], 0.0))
            pool.memset(ones_b[:, 1, :], 1.0).then_inc(S["late_consts"], 1)
            vp = v_pad[:, :, :].rearrange("p m (u h g o d) -> p m u h g o d", u=B, h=2, o=4, d=DH)
            then(pool.memset(v_pad[:, :, :], 0.0))
            for m in range(MB):
                then(pool.memset(vp[:, m, :, 0, :, 1, :], 1.0))
                then(pool.memset(vp[:, m, :, 1, :, 3, :], 1.0))
            for m in (sel_v, sel_d, id_b, eye2, selb):
                then(pool.memset(m[:], 0.0))
            then(pool.memset(ones2[:, :], 1.0))
            diagonal(id_b[:, :], 0, [[-1, P]])
            diagonal(eye2[:, :], 0, [[-1, B]])
            for b in range(B):
                diagonal(selb[:, D * b:D * b + D], -b, [[0, D]])
            for m, off in ((sel_v, 0), (sel_d, DH)):
                diagonal(m[:, :].rearrange("p (h g d) -> p h g d", h=2, d=DH), -off,
                         [[-2 * DH, 2], [-4 * DH, 4], [-1, DH]])
            then(pool.memset(w1_sel[:, :, :], 0.0))
            pool.memset(msum[:, :], 0.0).then_inc(S["late_consts"], 1)
            def add_middle(t):
                n = 3 * t + 2
                pool.wait_ge(S["prod_added"], n + 1 - (n > LONE))
                pool.wait_ge(S["part_ready"], t + 1)
                pool.tensor_tensor(hb[:, tile_of(t)], hb[:, tile_of(t)], prod[:, n % 4, 0, :], ALU.add)\
                    .then_inc(S["hb_ready"], 1)

            for n in range(3 * TILES):
                if n == LONE:
                    continue
                if third_by_pool(n):
                    wait_for_product_buffer(pool, n)
                    pool.wait_ge(S["wds_ready"], 6)
                    pool.wait_ge(S["x_ready"], TILES)
                    multiply_rows(pool, n, 2, 1).then_inc(S["prod_third"], 1)
                    pool.wait_ge(S["prod_third"], sum(third_by_pool(k) for k in range(n + 1)))
                pool.wait_ge(S["products"], n + 1)
                pool.tensor_tensor(prod[:, n % 4, 0, :], prod[:, n % 4, 0, :], prod[:, n % 4, 1, :], ALU.add)\
                    .then_inc(S["prod_half"], 1)
                pool.wait_ge(S["prod_half"], n + 1 - (n > LONE))
                pool.tensor_tensor(prod[:, n % 4, 0, :], prod[:, n % 4, 0, :], prod[:, n % 4, 2, :], ALU.add)\
                    .then_inc(S["prod_added"], 1)
                if n % 3 == 0 and n >= 3:
                    add_middle(n // 3 - 1)
                if n == SPLIT_STEP + 1:
                    pool.wait_ge(S["qk_parts"], 1)
                    pool.tensor_tensor(qk_res, qk, qk_part[:, 0, :, :], ALU.subtract).then_inc(S["qk_rest"], 1)
                if n == SPLIT_STEP + 3:
                    pool.wait_ge(S["qk_parts"], 2)
                    pool.tensor_tensor(qk, qk_res, qk_part[:, 1, :, :], ALU.subtract).then_inc(S["qk_rest"], 1)
            add_middle(TILES - 1)
            pool.wait_ge(S["idx_ready"], 1)
            experts = [expert_of(pool, n) for n in range(B * TOPK)]
            for n, e in enumerate(experts):
                pool.dma_start(w2_sel[:, n, :], W2[bass.ds(e, 1), :, :].rearrange("e f d -> (e f) d"))\
                    .then_inc(S["w2_in"], 16)
            for t in range(TILES):
                pool.wait_ge(S["z3_ready"], t + 1)
                if t >= 4:
                    pool.wait_ge(S["var3_done"], t - 3)
                pool.tensor_tensor(sq3[:, t % 4, :], z3[:, tile_of(t)], z3[:, tile_of(t)], ALU.mult)\
                    .then_inc(S["sq3_ready"], 1)

        @block.vector
        def _(dve):
            steps = [0]

            def link(ins):
                steps[0] += 1
                ins.then_inc(S["chain_v"], 1)
                dve.wait_ge(S["chain_v"], steps[0])

            nc.vector.memset(warm, 0.0).then_inc(S["warm_ready"], 1)
            nc.vector.memset(w1_bd[:, :], 0.0)
            nc.vector.memset(c2_bd[:, :], 0.0)
            nc.vector.memset(qkvo[:, :, :], 0.0).then_inc(S["zeroed"], 1)
            for m in (id_f, mean_m, shift_m):
                nc.vector.memset(m[:], 0.0)
            nc.vector.memset(regroup_m, 0.0).then_inc(S["zeroed"], 1)
            nc.vector.memset(wo_c[:, :], 0.0)

            dve.wait_ge(S["edges_in"], 16)
            nc.vector.tensor_copy(edge_row[:, :], edges[:, 0, :])
            link(nc.vector.tensor_copy(edge_col[:, :], edges[:, 1, :]))
            link(nc.vector.tensor_scalar(edge_hi[:, :], edge_col[:, :], float(NODES // 2), None, ALU.is_ge))
            nc.vector.tensor_scalar(edge_val[:, :], edge_hi[:, :], float(FIELD - 1), 1.0, ALU.mult, ALU.add)
            link(nc.vector.scalar_tensor_tensor(edge_col[:, :], edge_hi[:, :], -float(NODES // 2), edge_col[:, :],
                                                ALU.mult, ALU.add))
            nc.vector.tensor_scalar(edge_nval[:, :], edge_hi[:, :], -float(FIELD - 1), -1.0, ALU.mult, ALU.add)
            nc.vector.tensor_scalar(edge_ncol[:, :], edge_col[:, :], -1.0, None, ALU.mult).then_inc(S["edges_ready"], 1)
            dve.wait_ge(S["iota_ready"], 1)

            def merge(g):
                dve.wait_ge(S["counts_copied"], g + 1)
                if g >= 1:
                    dve.wait_ge(S["counts_merged"], g)
                else:
                    dve.wait_ge(S["own_counted"], 1)
                nc.vector.tensor_tensor(cnt_acc, cnt_acc, cnt, ALU.bitwise_or).then_inc(S["counts_merged"], 1)

            def onehots(chunks):
                for c in chunks:
                    k = c % HOT
                    if c >= HOT:
                        dve.wait_ge(S["chunk_counted"], c - HOT + 1)
                    if not by_scalar(c):
                        nc.vector.tensor_scalar(col_hot[:, k, :], iota[:, 0:NODES // 2], edge_col[:, c:c + 1],
                                                edge_val[:, c:c + 1], ALU.is_equal, ALU.mult)
                    nc.vector.tensor_scalar(row_hot[:, k, :], iota[:, :], edge_row[:, c:c + 1], None, ALU.is_equal)\
                        .then_inc(S["onehot"], 1)
                    if c % GROUP == GROUP // 2 and c >= GROUP:
                        merge(c // GROUP - 1)

            onehots(range(0, FIRST))
            dve.wait_ge(S["bn_in"], 16 * 5)
            dve.wait_ge(S["bn_exp"], 1)
            link(nc.vector.tensor_tensor(bn_tmp[:, 2:3], bn_col[:, 1:2], bn_tmp[:, 1:2], ALU.mult))
            link(nc.vector.tensor_tensor(bn_tmp[:, 0:1], bn_col[:, 0:1], bn_col[:, 3:4], ALU.subtract))
            nc.vector.scalar_tensor_tensor(bn_tmp[:, 3:4], bn_tmp[:, 0:1], bn_tmp[:, 2:3], bn_col[:, 2:3],
                                           ALU.mult, ALU.add).then_inc(S["bn_ready"], 1)
            onehots(range(FIRST, EARLY))
            dve.wait_ge(S["own_edges"], 1)
            nc.vector.tensor_copy(cnt_acc, own_edges).then_inc(S["own_counted"], 1)
            dve.wait_ge(S["conv2_in"], 16 * CONV2_DMAS)
            for n in range(2):
                dve.wait_ge(S["conv2_done"], n + 1)
                w = IH // 4
                nc.vector.tensor_tensor(
                    wd_t[:, w * n:w * n + w, :, :].rearrange("p t b k -> p t (b k)"),
                    ps[:, 4 + n, 0:w * B * KK].rearrange("p (t m) -> p t m", m=B * KK),
                    bass.AP(c2b_bc, 0, [[B * KK, P], [0, w], [1, B * KK]]), ALU.add).then_inc(S["wd_ready"], 1)
            dve.wait_ge(S["weights_in"], 16 * WEIGHT_DMAS)
            link(nc.vector.tensor_reduce(wo_mean[:, :], qkvo[:, 3, :], AX, ALU.add))
            nc.vector.tensor_copy(ccols[:, 0:1], cols[:, 3:4])
            nc.vector.tensor_copy(ccols[:, 2:3], cols[:, 7:8])
            link(nc.vector.tensor_scalar(wo_mean[:, :], wo_mean[:, :], 1.0 / D, None, ALU.mult))
            for b in range(B):
                o = slice(D * b, D * b + D)
                nc.vector.tensor_scalar(wo_c[o, o], qkvo[o, 3, o], wo_mean[o, 0:1], None, ALU.subtract)
            nc.vector.tensor_tensor(ccols[:, 1:2], cols[:, 5:6], cols[:, 7:8], ALU.add).then_inc(S["woc_ready"], 1)

            def weights(part):
                if part == 0:
                    dve.wait_ge(S["wvt_done"], 1)
                    nc.vector.tensor_copy(wv_t[:, :], ps[:, 3, 0:P]).then_inc(S["wvt_ready"], 1)
                else:
                    dve.wait_ge(S["m3_done"], 1)
                    nc.vector.tensor_copy(m3[:, :], ps[:, 2, 0:P])
                    nc.vector.tensor_copy(zb[:, 0:1], ps[:, 2, 128:129])
                    nc.vector.tensor_copy(zb[:, 1:2], ps[:, 2, 192:193])
                    nc.vector.tensor_scalar(zb[:, 2:4], ps[:, 2, 193:195], -1.0, None, ALU.mult)\
                        .then_inc(S["m3_ready"], 1)

            def product(n):
                wait_for_product_buffer(dve, n)
                multiply_rows(nc.vector, n, 0, 2 if third_by_pool(n) else 3).then_inc(S["products"], 1)

            def norm1(t):
                dve.wait_ge(S["rstd_ready"], t + 1)
                nc.vector.scalar_tensor_tensor(a1[:, tile_of(t)], ps[:, centred_bank(t), :], zb[:, 2:3],
                                               rstd[:, t % 2, :], ALU.add, ALU.mult).then_inc(S["a1_ready"], 1)

            def pad_values():
                dve.wait_ge(S["qkv_done"], 3)
                dve.wait_ge(S["late_consts"], 2)
                vp = v_pad[:, :, :].rearrange("p m (u h g o d) -> p m u h g o d", u=B, h=2, o=4, d=DH)
                vs = ps[:, 0, :].rearrange("p (m u h g d) -> p m u h g d", m=MB, u=B, h=2, d=DH)
                for u in range(B):
                    for hp in range(2):
                        nc.vector.tensor_tensor(
                            vp[:, :, u, hp, :, 2 * hp, :], vs[:, :, u, hp, :, :],
                            bass.AP(bv_bc, D * u + 4 * DH * hp, [[P, P], [0, MB], [DH, 4], [1, DH]]),
                            ALU.add).then_inc(S["vpad_ready"], 1)

            def decode_mask():
                merge(GROUPS - 1)
                dve.wait_ge(S["counts_merged"], GROUPS)
                link(nc.vector.tensor_scalar(cnt, cnt_acc, FIELD - 1, None, ALU.bitwise_and))
                nc.vector.tensor_scalar(mask_t[:, 0:2, :], cnt.rearrange("p (a n) -> p a n", a=2),
                                        0.0, MASKED, ALU.is_equal, ALU.mult).then_inc(S["mask_ready"], 1)
                nc.vector.tensor_scalar(mask_t[:, 2:4, :], cnt_acc.rearrange("p (a n) -> p a n", a=2),
                                        float(FIELD), MASKED, ALU.is_lt, ALU.mult).then_inc(S["mask_ready"], 1)

            dve.wait_ge(S["wds_ready"], 6)
            dve.wait_ge(S["x_ready"], TILES)
            for s in range(TILES + 1):
                for j in range(3):
                    n = 3 * s + j
                    if s < TILES:
                        product(n)
                    if s < TILES:
                        onehots(beside_product(n))
                    if j == 0 and s >= 2:
                        norm1(s - 2)
                    if s == 0 and j < 2:
                        weights(j)
                    if n == SPLIT_STEP + 2:
                        pad_values()
                if s == TILES - 1:
                    decode_mask()
            norm1(TILES - 1)

            def norm_z(k):
                t = (k + 1) % TILES
                dve.wait_ge(S["zr_ready"], k + 1)
                link(nc.vector.scalar_tensor_tensor(tnorm[:, 0, :], ps[:, norm_bank(k), :], zb[:, 1:2] if t == 0 else zb[:, 0:1],
                                                    rstd[:, 0, :], ALU.add, ALU.mult))
                nc.vector.scalar_tensor_tensor(h1[:, tile_of(t)], tnorm[:, 0, :], cols[:, 4:5], hb[:, tile_of(t)],
                                               ALU.mult, ALU.add).then_inc(S["h1_ready"], 1)

            def norm2(k):
                t = (k + 1) % TILES
                dve.wait_ge(S["r2_ready"], k + 1)
                nc.vector.scalar_tensor_tensor(a2[:, tile_of(t)], ps[:, norm_bank(k), :], zb[:, 3:4], rstd[:, second_slot(k), :],
                                               ALU.add, ALU.mult, accum_out=a2_sum[:, t:t + 1]).then_inc(S["a2_ready"], 1)

            def norms(kind, k):
                if kind == "v":
                    norm_z(k)
                if kind == "w":
                    norm2(k)

            def split_maxima(q):
                dve.wait_ge(S["nmax_turned"], q + 1)
                if q >= 1:
                    dve.wait_ge(nm_in[q - 1], 48)
                link(nc.vector.tensor_scalar(nm[:, :], ps[0:4 * MB, 7, 0:P], -1.0, None, ALU.mult))
                link(nc.vector.tensor_copy(nm_part[:, 0, :], nm[:, :]))
                link(nc.vector.tensor_tensor(nm_res[:, :], nm[:, :], nm_part[:, 0, :], ALU.subtract))
                link(nc.vector.tensor_copy(nm_part[:, 1, :], nm_res[:, :]))
                link(nc.vector.tensor_tensor(nm[:, :], nm_res[:, :], nm_part[:, 1, :], ALU.subtract))
                nc.vector.tensor_copy(nm_part[:, 2, :], nm[:, :]).then_inc(S["nm_split"], 1)

            def attended(u):
                o, d = slice(D * u, D * u + D), slice(D * (1 - u), D * (1 - u) + D)
                dve.wait_ge(S["gathered"], u + 1)
                link(nc.vector.reciprocal(att[o, :], ps[d, 6 + u, :]))
                nc.vector.tensor_tensor(att[o, :], ps[o, 6 + u, :], att[o, :], ALU.mult).then_inc(S["att_ready"], 1)

            def take_pv(u):
                dve.wait_ge(S["pv_used"], len(ROUNDS) // B * (u + 1))
                nc.vector.tensor_copy(pv_sb[:, u, :], ps[:, 6 + u, :]).then_inc(S["pv_copied"], 1)

            for what, n in beside(*PLAN, lag=LAG):
                if what == "norm":
                    norms(*n)
                elif what == "turn":
                    split_maxima(n)
                elif what == "maxima":
                    k, nb = 2 * n // MB, 2 * n % MB
                    dve.wait_ge(S["s_done"], n + 1)
                    nc.vector.tensor_reduce(nmax[:, k, nb:nb + 2], ps[:, maxima_bank(n):maxima_bank(n) + 2, :], AX,
                                            ALU.max).then_inc(S["s_maxed"], 1)
                elif n == PV_STEP:
                    take_pv(0)
                elif n == GATHER_STEP:
                    attended(0)
            norm_z(LAST - 2)
            take_pv(1)
            attended(1)
            for kind, k in BEHIND:
                norms(kind, k)

            dve.wait_ge(S["a2_ready"], TILES)
            link(nc.vector.tensor_reduce(mcol[:, :], a2_sum[:, :], AX, ALU.add))
            nc.vector.tensor_copy(msum[0:D, 0:1], mcol[0:D, :])
            nc.vector.tensor_copy(msum[D:P, 1:2], mcol[D:P, :]).then_inc(S["ms_ready"], 1)
            lg, e1, rw, ld, v8 = (rt[:, 8 * k:8 * k + 8] for k in range(5))
            sc = [rt[:, 48 + k:49 + k] for k in range(8)]

            def softmax(src, tmp, dst, s_max, s_sum, turn):
                link(nc.vector.tensor_reduce(s_max, src, AX, ALU.max))
                nc.vector.tensor_scalar(s_max, s_max, -1.0, None, ALU.mult).then_inc(S["rt_step"], 1)
                dve.wait_ge(S["rt_exp"], turn)
                link(nc.vector.tensor_reduce(s_sum, tmp, AX, ALU.add))
                link(nc.vector.reciprocal(s_sum, s_sum))
                return nc.vector.tensor_scalar(dst, tmp, s_sum, None, ALU.mult)

            dve.wait_ge(S["lg_done"], 1)
            link(nc.vector.scalar_tensor_tensor(lg, ps[0:B, 7, 0:NE], 1.0 / N, br_bc[:, :], ALU.mult, ALU.add))
            softmax(lg, e1, rw, sc[0], sc[1], 1).then_inc(S["rt_pe"], 1)
            dve.wait_ge(S["lg_done"], 2)
            link(nc.vector.tensor_scalar(ld, ps[0:B, 7, NE:2 * NE], float(N), 1.0, ALU.mult, ALU.max))
            link(nc.vector.reciprocal(ld, ld))
            link(nc.vector.tensor_scalar(ld, ld, CAPACITY, 1.0, ALU.mult, ALU.min))
            link(nc.vector.tensor_tensor(lg, rw, ld, ALU.mult))
            link(softmax(lg, e1, rw, sc[2], sc[3], 2))
            link(nc.vector.max(v8, rw))
            nc.vector.max_index(rt_idx[:, :], v8, rw).then_inc(S["idx_ready"], 1)
            two = rt[:, 56:58]
            nc.vector.tensor_scalar(sc[4], v8[:, 0:1], -1.0, None, ALU.mult).then_inc(S["rt_step"], 1)
            dve.wait_ge(S["rt_exp"], 3)
            link(nc.vector.tensor_reduce(sc[5], two, AX, ALU.add))
            link(nc.vector.reciprocal(sc[5], sc[5]))
            link(nc.vector.tensor_scalar(rt[:, 60:62], two, sc[5], None, ALU.mult))
            for b in range(B):
                nc.vector.tensor_scalar(rt[:, 64 + 2 * b:66 + 2 * b], rt[:, 60:62], eye2[:, b:b + 1], None, ALU.mult)\
                    .then_inc(S["topw"], 1)
            dve.wait_ge(S["w_bc_done"], 1)
            nc.vector.tensor_copy(wb4[:, :], ps[:, 7, 64:68])
            link(nc.vector.tensor_copy(wcol[:, :], ps[:, 7, 72:74]))
            dve.wait_ge(S["w2_in"], 16 * B * TOPK)
            link(nc.vector.tensor_reduce(w2_mean[:, :], w2_sel[:, :, :], AX, ALU.add))
            link(nc.vector.tensor_scalar(w2_mean[:, :], w2_mean[:, :], 1.0 / D, None, ALU.mult))
            for n in range(B * TOPK):
                last = nc.vector.tensor_scalar(w2_c[:, n, :], w2_sel[:, n, :], w2_mean[:, n:n + 1], wb4[:, n:n + 1],
                                               ALU.subtract, ALU.mult)
            last.then_inc(S["w2c_ready"], 1)
            dve.wait_ge(S["b2_in"], 16 * B * TOPK)
            link(nc.vector.tensor_tensor(b2_sel[:, :], b2_sel[:, :], wcol[:, :], ALU.mult))
            nc.vector.tensor_reduce(b2_mix[:, :], b2_sel[:, :], AX, ALU.add).then_inc(S["b2m_ready"], 1)
            dve.wait_ge(S["c3_done"], 1)
            nc.vector.tensor_copy(c3b[:, :], ps[:, 7, 80:81]).then_inc(S["c3_ready"], 1)
            dve.wait_ge(S["c3_ready"], 1)

            def mix(t):
                dve.wait_ge(S["down_done"], t + 1)
                nc.vector.scalar_tensor_tensor(z3[:, tile_of(t)], ps[:, 4 + t % 2, :], c3b[:, 0:1], a2[:, tile_of(t)],
                                               ALU.add, ALU.add).then_inc(S["z3_ready"], 1)

            def finish(t):
                dve.wait_ge(S["r3_ready"], t + 1)
                link(nc.vector.tensor_tensor(tnorm[:, t % 2, :], z3[:, tile_of(t)], rstd3[:, t % 4, :], ALU.mult))
                nc.vector.scalar_tensor_tensor(h1[:, tile_of(t)], tnorm[:, t % 2, :], cols[:, 6:7], h1[:, tile_of(t)],
                                               ALU.mult, ALU.add).then_inc(S["o_ready"], 1)

            def give(t):
                dve.wait_ge(S["o_turned"], t + 1)
                nc.vector.tensor_copy(o_tok[:, 4 * t:4 * t + 4, :], ps[:, turn_bank(t), :].rearrange("p (t m) -> p t m", m=P))\
                    .then_inc(S["o_copied"], 1)

            early, late = BATCHES
            for t in early:
                mix(t)
            for t in early:
                finish(t)
            for n, t in enumerate(late):
                mix(t)
                if n < len(early):
                    give(early[n])
            for t in late:
                finish(t)

        @block.scalar
        def _(act):
            def load_x(q):
                o = slice(N // XQ * q, N // XQ * q + N // XQ)
                act.dma_start(x_chan[:, o], x.rearrange("b c h w -> (b c) (h w)")[:, o]).then_inc(xchan_in[q], 16)

            for q in range(XQ):
                load_x(q)
            steps = [0]

            def link(ins):
                steps[0] += 1
                ins.then_inc(S["chain_a"], 1)
                act.wait_ge(S["chain_a"], steps[0])

            def hot_columns(chunks):
                for c in chunks:
                    if by_scalar(c):
                        k, n = c % HOT, scalar_chunks(c)
                        act.wait_ge(S["chunk_counted"], c - HOT + 1)
                        if n > 2:
                            act.wait_ge(S["cols_hot"], n - 2)
                        nc.scalar.activation(hot_tmp[:, n % 2, :], iota[:, 0:NODES // 2], ACT.Square,
                                             bias=edge_ncol[:, c:c + 1]).then_inc(S["hot_squared"], 1)
                        act.wait_ge(S["hot_squared"], n)
                        nc.scalar.activation(col_hot[:, k, :], hot_tmp[:, n % 2, :], ACT.Relu, bias=edge_val[:, c:c + 1],
                                             scale=edge_nval[:, c:c + 1]).then_inc(S["cols_hot"], 1)

            nc.scalar.preload_act_table_set(NORM_SET)
            act.wait_ge(S["bn_in"], 16 * 5)
            link(nc.scalar.activation(bn_tmp[:, 0:1], bn_col[:, 4:5], ACT.Ln, bias=EPS))
            nc.scalar.activation(bn_tmp[:, 1:2], bn_tmp[:, 0:1], ACT.Exp, scale=-0.5).then_inc(S["bn_exp"], 1)

            def copy_counts(g):
                act.wait_ge(S["chunk_counted"], min(CHUNKS, GROUP * (g + 1)))
                if g >= 1:
                    act.wait_ge(S["counts_merged"], g)
                else:
                    act.wait_ge(S["own_counted"], 1)
                nc.scalar.activation(cnt.rearrange("p (a n) -> p a n", a=2), ps[:, 6 - 2 * (g % 2):8 - 2 * (g % 2), :], ACT.Copy)\
                    .then_inc(S["counts_copied"], 1)

            act.wait_ge(S["bn_ready"], 1)
            for t in range(TILES):
                act.wait_ge(S["conv1_done"], t + 1)
                nc.scalar.activation(y_relu[:, tile_of(t)], ps[0:B * CR, 4 + t % 2, :], ACT.Relu,
                                     bias=bn_tmp[:, 3:4], scale=bn_tmp[:, 2:3]).then_inc(S["relu_done"], 1)
            xp = x_pad.rearrange("p (c h) -> p c h", h=PAD)
            for t in range(TILES):
                act.wait_ge(S["turned"], t + 1)
                nc.scalar.activation(xp[:, CT * t:CT * t + CT, 1:IH + 1], ps[:, t % 4, :].rearrange("p (c h) -> p c h", h=IH),
                                     ACT.Copy).then_inc(S["x_ready"], 1)
            for j in range(3):
                for h2 in range(2):
                    n = 2 * j + h2
                    act.wait_ge(S["regrouped"], 3 * (n // 3) + 3)
                    nc.scalar.activation(
                        bass.AP(wd_s, j * IH + h2, [[9 * IH, P], [2, IH // 2], [3 * IH, 3]]),
                        ps[:, n // 3, 96 * (n % 3):96 * (n % 3) + 96].rearrange("p (h i) -> p h i", i=3),
                        ACT.Copy).then_inc(S["wds_ready"], 1)

            def rsqrt(src, ln, dst, var_sem, n, out_sem):
                act.wait_ge(S[var_sem], n)
                link(nc.scalar.activation(ln, src, ACT.Ln, bias=EPS))
                nc.scalar.activation(dst, ln, ACT.Exp, scale=-0.5).then_inc(S[out_sem], 1)

            act.wait_ge(S["woc_ready"], 1)
            act.wait_ge(S["edges_ready"], 1)
            act.wait_ge(S["iota_ready"], 1)
            hot_columns(beside_product(0))
            for s in range(TILES + 1):
                for j in range(3):
                    n = 3 * s + j
                    if n >= 1:
                        for c in beside_product(n - 1):
                            if ends_group(c):
                                copy_counts(c // GROUP)
                    if n == SPLIT_STEP:
                        for k in range(2):
                            act.wait_ge(S["qkv_done"], k + 1)
                            nc.scalar.activation(qk[:, k, :], ps[:, k, :], ACT.Identity, bias=cols[:, k:k + 1])\
                                .then_inc(S["qk_ready"], 1)
                        act.wait_ge(S["qk_ready"], 2)
                        nc.scalar.activation(qk_part[:, 0, :, :], qk, ACT.Copy).then_inc(S["qk_parts"], 1)
                    if n == SPLIT_STEP + 2:
                        act.wait_ge(S["qk_rest"], 1)
                        nc.scalar.activation(qk_part[:, 1, :, :], qk_res, ACT.Copy).then_inc(S["qk_parts"], 1)
                    if n == SPLIT_STEP + 4:
                        act.wait_ge(S["qk_rest"], 2)
                        nc.scalar.activation(qk_part[:, 2, :, :], qk, ACT.Copy).then_inc(S["qk_parts"], 1)
                    if s >= 1 and j == 1:
                        t = s - 1
                        if t == 0:
                            act.wait_ge(S["m3_ready"], 1)
                        act.wait_ge(S["cent_done"], t + 1)
                        if t >= 2:
                            act.wait_ge(S["var_done"], t - 1)
                        nc.scalar.activation(sq[:, t % 2, :], ps[:, centred_bank(t), :], ACT.Square, bias=zb[:, 2:3])\
                            .then_inc(S["sq_ready"], 1)
                    if s == TILES and j == 1:
                        for n in range(MB):
                            act.wait_ge(S["mask_turned"], n + 1)
                            nc.scalar.activation(mask_n[:, n, :], ps[:, 6 + n % 2, 0:256].bitcast(BF16), ACT.Copy)\
                                .then_inc(S["mask_n_ready"], 1)
                    if j == 2 and s < TILES:
                        act.wait_ge(S["prod_used"], 2 * (s + 1))
                        nc.scalar.activation(hb[:, tile_of(s)], ps[:, acc_bank(s), :], ACT.Identity,
                                             bias=ccols[:, 1:2]).then_inc(S["part_ready"], 1)
                    if s >= 1 and j == 2:
                        t = s - 1
                        if t >= 2:
                            act.wait_ge(S["a1_ready"], t - 1)
                            act.wait_ge(S["rstd_ready"], t - 1)
                        rsqrt(ps[:, 3, :], lnv[:, t % 2, :], rstd[:, t % 2, :], "var_done", t + 1, "rstd_ready")
                    if s < TILES:
                        hot_columns(beside_product(n + 1))

            def z_square(k):
                act.wait_ge(S["z_done"], k + 1)
                if k >= 1:
                    act.wait_ge(S["zvar_done"], k)
                nc.scalar.activation(sq[:, 0, :], ps[:, norm_bank(k), :], ACT.Square, bias=zb[:, 1:2] if k == LAST else zb[:, 0:1])\
                    .then_inc(S["zsq_ready"], 1)

            def c_square(k):
                act.wait_ge(S["c1_done"], k + 1)
                if k == LAST:
                    act.wait_ge(S["zvar_done"], TILES)
                elif k >= 1:
                    act.wait_ge(S["var2_done"], k)
                nc.scalar.activation(sq[:, second_slot(k), :], ps[:, norm_bank(k), :], ACT.Square, bias=zb[:, 3:4]).then_inc(S["c1sq_ready"], 1)

            def z_rsqrt(k):
                if k >= 1:
                    act.wait_ge(S["h1_ready"], k)
                    act.wait_ge(S["zr_ready"], k)
                rsqrt(ps[:, norm_bank(k) + 1, :], lnv[:, 0, :], rstd[:, 0, :], "zvar_done", k + 1, "zr_ready")

            def c_rsqrt(k):
                if k == LAST:
                    act.wait_ge(S["h1_ready"], TILES)
                elif k >= 1:
                    act.wait_ge(S["a2_ready"], k)
                    act.wait_ge(S["r2_ready"], k)
                rsqrt(ps[:, norm_bank(k) + 1, :], lnv[:, second_slot(k), :], rstd[:, second_slot(k), :], "var2_done", k + 1, "r2_ready")

            def norms(kind, k):
                {"z": z_square, "v": z_rsqrt, "c": c_square, "w": c_rsqrt}[kind](k)

            for what, n in beside(*PLAN):
                if what == "norm":
                    norms(*n)
                elif what == "weights":
                    r, g, m = n // 8, n % 8 // 2, n % 2
                    act.wait_ge(S["st_done"], n + 1)
                    if r >= 3:
                        act.wait_ge(S["pv_used"], r - 2)
                    nc.scalar.activation(probs[:, r % 3, g, m, :], ps[:, weights_bank(n), :], ACT.Exp,
                                         scale=float(DH) ** -0.5).then_inc(S["exp_done"], 1)
            for kind, k in BEFORE_PV + BEHIND:
                norms(kind, k)
            for turn in range(2):
                act.wait_ge(S["rt_step"], turn + 1)
                nc.scalar.activation(rt[:, 8:16], rt[:, 0:8], ACT.Exp, bias=rt[:, 48 + 2 * turn:49 + 2 * turn])\
                    .then_inc(S["rt_exp"], 1)
            act.wait_ge(S["rt_step"], 3)
            nc.scalar.activation(rt[:, 56:58], rt[:, 32:34], ACT.Exp, bias=rt[:, 52:53]).then_inc(S["rt_exp"], 1)
            act.wait_ge(S["idx_ready"], 1)
            for n in range(B * TOPK):
                e = expert_of(act, n)
                act.dma_start(b1_sel[:, n:n + 1], b1[bass.ds(e, 1), :].rearrange("e f -> f e")).then_inc(S["b1_in"], 16)
            nc.scalar.preload_act_table(ACT.Gelu)
            act.wait_ge(S["b1_in"], 16 * B * TOPK)

            def gelu(t):
                for n in range(B * TOPK):
                    act.wait_ge(S["up_done"], B * TOPK * t + n + 1)
                    if t >= 2:
                        act.wait_ge(S["down_done"], t - 1)
                    nc.scalar.activation(hid[:, t % 2, n, :], ps[:, n, :], ACT.Gelu, bias=b1_sel[:, n:n + 1])\
                        .then_inc(S["gelu_done"], 1)

            for batch in BATCHES:
                for t in batch:
                    gelu(t)
                nc.scalar.preload_act_table_set(NORM_SET)
                for t in batch:
                    if t >= 4:
                        act.wait_ge(S["r3_ready"], t - 3)
                        act.wait_ge(S["o_ready"], t - 3)
                    rsqrt(ps[:, var3_bank(t), :], lnv3[:, t % 4, :], rstd3[:, t % 4, :], "var3_done", t + 1, "r3_ready")
                if batch is BATCHES[0]:
                    nc.scalar.preload_act_table(ACT.Gelu)
            for t in BATCHES[-1]:
                act.wait_ge(S["o_turned"], t + 1)
                nc.scalar.activation(o_tok[:, 4 * t:4 * t + 4, :], ps[:, turn_bank(t), :].rearrange("p (t m) -> p t m", m=P),
                                     ACT.Copy).then_inc(S["o_copied_late"], 1)

        @block.tensor
        def _(pe):
            def count(chunks):
                for c in chunks:
                    g, k = c // GROUP, c % HOT
                    if c % GROUP == 0 and g >= 2:
                        pe.wait_ge(S["counts_copied"], g - 1)
                    pe.wait_ge(S["onehot"], c + 1)
                    if by_scalar(c):
                        pe.wait_ge(S["cols_hot"], scalar_chunks(c))
                    for j in range(2):
                        last = pe.matmul(ps[:, 6 - 2 * (g % 2) + j, :], col_hot[:, k, P * j:P * j + P], row_hot[:, k, :],
                                         start=(c % GROUP == 0), stop=ends_group(c))
                    last.then_inc(S["chunk_counted"], 1)

            def keep_warm(bank, times):
                for _ in range(times):
                    pe.matmul(ps[:, bank, :], mean_m[:, :], sq[:, 0, :], start=True, stop=True)

            pe.wait_ge(S["warm_ready"], 1)
            for _ in range(WARM_UP):
                pe.matmul(ps[:, 0, :], warm[:, 0:P], warm, start=True, stop=True)
            count(range(0, FIRST))
            pe.wait_ge(S["conv1_in"], 16 * B)
            for t in range(TILES):
                if t % (TILES // XQ) == 0:
                    pe.wait_ge(xchan_in[t // (TILES // XQ)], 16)
                if t >= 2:
                    pe.wait_ge(S["relu_done"], t - 1)
                pe.matmul(ps[0:B * CR, 4 + t % 2, :], w1_bd[:, :], x_chan[:, tile_of(t)],
                          start=True, stop=True).then_inc(S["conv1_done"], 1)
            pe.wait_ge(S["relu_done"], TILES)
            pe.wait_ge(S["conv2_in"], 16 * CONV2_DMAS)
            for t in range(IH // 2):
                n, k = t // 16, t % 16
                last = pe.matmul(ps[:, 4 + n, B * KK * k:B * KK * k + B * KK], y_relu[:, P * t:P * t + P], c2_bd[:, :],
                                 start=True, stop=True)
                if k == 15:
                    last.then_inc(S["conv2_done"], 1)
            pe.wait_ge(S["xtok_in"], 32)
            pe.wait_ge(S["ident_ready"], 1)
            for t in range(4 * TILES):
                if t % 4 == 0 and t >= 16:
                    pe.wait_ge(S["x_ready"], t // 4 - 3)
                last = pe.transpose(ps[:, (t // 4) % 4, P * (t % 4):P * (t % 4) + P], x_tok[:, t, :], id_f[:, :])
                if t % 4 == 3:
                    last.then_inc(S["turned"], 1)
            pe.wait_ge(S["wd_ready"], 2)
            pe.wait_ge(S["consts_ready"], 1)
            pe.wait_ge(S["x_ready"], TILES)
            for j in range(3):
                for h2 in range(2):
                    n = 2 * j + h2
                    for b in range(B):
                        last = pe.matmul(
                            ps[:, n // 3, 96 * (n % 3):96 * (n % 3) + 96].rearrange("p (h i) -> p h i", i=3),
                            regroup_m[:, (b * 2 + h2) * 3 + j, :],
                            bass.AP(a1, WT0 + b * KK + j, [[N, P], [B * KK, IH // 2], [3, 3]]),
                            start=(b == 0), stop=(b == B - 1))
                    last.then_inc(S["regrouped"], 1)
            pe.wait_ge(S["woc_ready"], 1)
            pe.transpose(ps[:, 3, 0:P], qkvo[:, 2, :], id_f[:, :]).then_inc(S["wvt_done"], 1)
            count(range(FIRST, EARLY))
            pe.wait_ge(S["wds_ready"], 6)

            def multiply_weights():
                pe.wait_ge(S["wvt_ready"], 1)
                pe.matmul(ps[:, 2, 0:P], wv_t[:, :], wo_c[:, :], start=True, stop=False)
                pe.matmul(ps[:, 2, 0:P], id_f[:, :], cent_m[:, :], start=False, stop=True)
                pe.matmul(ps[:, 2, 128:129], wo_c[:, :], cols[:, 2:3], start=True, stop=False)
                pe.matmul(ps[:, 2, 128:129], cent_m[:, :], cols[:, 3:4], start=False, stop=True)
                pe.matmul(ps[:, 2, 192:195], cent_m[:, :], ccols[:, :], start=True, stop=True).then_inc(S["m3_done"], 1)

            for s in range(TILES + 1):
                if 2 <= s < TILES:
                    if s == QKV_STEP + 1:
                        pe.wait_ge(S["qk_ready"], 2)
                    elif s == QKV_STEP + 2:
                        pe.wait_ge(S["vpad_ready"], 4)
                    else:
                        pe.wait_ge(S["part_ready"], s - 1)
                for j in range(3):
                    if s < TILES:
                        n = 3 * s + j
                        if n == LONE:
                            pe.wait_ge(S["products"], n + 1)
                        elif j < 2:
                            pe.wait_ge(S["prod_added"], n + 1)
                        if j < 2:
                            rows = 3 if n == LONE else 1
                            for i in range(rows):
                                last = pe.matmul(ps[:, acc_bank(s), :], shift_m[:, ORDER[j], :], prod[:, n % 4, i, :],
                                                 start=(j == 0 and i == 0), stop=(j == 1 and i == rows - 1))
                            last.then_inc(S["prod_used"], 1)
                        count(beside_product(n))
                    if s == 0 and j == 0:
                        multiply_weights()
                    if s >= 1 and j == 0:
                        t = s - 1
                        if t == 0:
                            pe.wait_ge(S["m3_ready"], 1)
                        elif t < TILES - 1:
                            pe.wait_ge(S["a1_ready"], t)
                        pe.wait_ge(S["hb_ready"], t + 1)
                        pe.matmul(ps[:, centred_bank(t), :], cent_m[:, :], hb[:, tile_of(t)], start=True, stop=True)\
                            .then_inc(S["cent_done"], 1)
                    if s == TILES and j == 1:
                        pe.wait_ge(S["mask_ready"], 2)
                        pe.wait_ge(S["late_consts"], 2)
                        for n in range(MB):
                            if n >= 2:
                                pe.wait_ge(S["mask_n_ready"], n - 1)
                            for m in range(MB):
                                last = pe.transpose(ps[:, 6 + n % 2, 64 * m:64 * m + 64].bitcast(BF16),
                                                    mask_t[:, m, P * n:P * n + P], id_b[:, :])
                            last.then_inc(S["mask_turned"], 1)
                    if s >= 1 and j == 1:
                        t = s - 1
                        pe.wait_ge(S["sq_ready"], t + 1)
                        if t >= 1:
                            pe.wait_ge(S["rstd_ready"], t)
                        pe.matmul(ps[:, 3, :], mean_m[:, :], sq[:, t % 2, :], start=True, stop=True)\
                            .then_inc(S["var_done"], 1)
                    if s == QKV_STEP and j == 2:
                        pe.wait_ge(S["a1_ready"], 1)
                        pe.wait_ge(S["part_ready"], s + 1)
                        for n in range(2):
                            pe.matmul(ps[:, n, :], qkvo[:, n, :], a1[:, 0:TILE], start=True, stop=True)\
                                .then_inc(S["qkv_done"], 1)
                    if s == QKV_STEP + 1 and j == 0:
                        for m in range(MB):
                            last = pe.matmul(ps[:, 0, P * m:P * m + P], a1[:, P * m:P * m + P], qkvo[:, 2, :],
                                             start=True, stop=True)
                        last.then_inc(S["qkv_done"], 1)

            def z_project(k):
                t, bank = (k + 1) % TILES, norm_bank(k)
                if 1 <= k < LAST - 1:
                    pe.wait_ge(S["a2_ready"], k)
                if t == 0:
                    pe.matmul(ps[:, bank, :], cent_m[:, :], a1[:, tile_of(t)], start=True, stop=False)
                    pe.wait_ge(S["att_ready"], B)
                    pe.matmul(ps[:, bank, :], wo_c[:, :], att, start=False, stop=True).then_inc(S["z_done"], 1)
                else:
                    pe.matmul(ps[:, bank, :], m3[:, :], a1[:, tile_of(t)], start=True, stop=True)\
                        .then_inc(S["z_done"], 1)

            def z_var(k):
                pe.wait_ge(S["zsq_ready"], k + 1)
                if 1 <= k < LAST - 1:
                    pe.wait_ge(S["r2_ready"], k)
                pe.matmul(ps[:, norm_bank(k) + 1, :], mean_m[:, :], sq[:, 0, :], start=True, stop=True)\
                    .then_inc(S["zvar_done"], 1)

            def c_project(k):
                pe.wait_ge(S["h1_ready"], k + 1)
                pe.matmul(ps[:, norm_bank(k), :], cent_m[:, :], h1[:, tile_of((k + 1) % TILES)], start=True, stop=True)\
                    .then_inc(S["c1_done"], 1)

            def c_var(k):
                pe.wait_ge(S["c1sq_ready"], k + 1)
                pe.wait_ge(S["zr_ready"], k + 1)
                pe.matmul(ps[:, norm_bank(k) + 1, :], mean_m[:, :], sq[:, second_slot(k), :], start=True, stop=True)\
                    .then_inc(S["var2_done"], 1)

            def norms(kind, k):
                {"z": z_project, "v": z_var, "c": c_project, "w": c_var}[kind](k)

            def scores(p):
                if p == 1:
                    pe.wait_ge(S["a1_ready"], TILES)
                elif 2 <= p < WIDE:
                    pe.wait_ge(S["s_maxed"], p - 1)
                elif p >= WIDE:
                    pe.wait_ge(S["s_maxed"], p)
                for n in range(2 * p, 2 * p + 2):
                    h, nb, bank = n // MB, n % MB, maxima_bank(p) + n % 2
                    pe.matmul(ps[:, bank, :], q_stack[0:KROWS, h, P * nb:P * nb + P], k_stack[0:KROWS, h, :],
                              start=True, stop=False)
                    last = pe.matmul(ps[:, bank, :], id_b[:, :], mask_n[:, nb, :], start=False, stop=True)
                last.then_inc(S["s_done"], 1)

            def turn_maxima(q):
                pe.wait_ge(S["s_maxed"], QUARTER * (q + 1))
                if q == 0:
                    pe.wait_ge(S["mask_n_ready"], MB)
                else:
                    pe.wait_ge(S["nm_split"], q)
                pe.transpose(ps[0:4 * MB, 7, 0:P], nmax[:, 4 * q:4 * q + 4, :].rearrange("p h m -> p (h m)"), id_f[:, :])\
                    .then_inc(S["nmax_turned"], 1)

            def gather(u):
                pe.wait_ge(S["pv_copied"], u + 1)
                o, d = slice(D * u, D * u + D), slice(D * (1 - u), D * (1 - u) + D)
                pe.matmul(ps[d, 6 + u, :], sel_d[:, :], pv_sb[:, u, :], start=True, stop=True, skip_group_check=True)
                pe.matmul(ps[o, 6 + u, :], sel_v[:, :], pv_sb[:, u, :], start=True, stop=True, skip_group_check=True)\
                    .then_inc(S["gathered"], 1)

            def weigh(r):
                u, hp, half = ROUNDS[r]
                pe.wait_ge(S["exp_done"], 8 * (r + 1))
                if r == 4:
                    pe.wait_ge(S["nm_split"], 4)
                for m in range(2):
                    for g in range(4):
                        head = head_of(u, hp, g)
                        last = pe.matmul(ps[32 * g:32 * g + 32, 6 + u, :],
                                         v_pad[:, 2 * half + m, 32 * head:32 * head + 32], probs[:, r % 3, g, m, :],
                                         start=(hp == 0 and half == 0 and m == 0), stop=(hp == 1 and half == 1 and m == 1),
                                         skip_group_check=True)
                last.then_inc(S["pv_used"], 1)

            def turned_scores(n):
                r, g, m = n // 8, n % 8 // 2, n % 2
                u, hp, half = ROUNDS[r]
                head = head_of(u, hp, g)
                if n % (2 * QUARTER) == 0:
                    pe.wait_ge(nm_in[n // (2 * QUARTER)], 48)
                if n == 0:
                    pe.wait_ge(S["s_maxed"], WIDE - 1)
                if n == NARROW_T:
                    pe.wait_ge(S["s_maxed"], PAIRS)
                if 2 <= n < NARROW_T:
                    pe.wait_ge(S["exp_done"], n - 1)
                if n >= NARROW_T:
                    pe.wait_ge(S["exp_done"], n - 3)
                o = slice(P * (2 * half + m), P * (2 * half + m) + P)
                pe.matmul(ps[:, weights_bank(n), :], k_stack[0:KROWS, head, o], q_stack[0:KROWS, head, :],
                          start=True, stop=False)
                pe.matmul(ps[:, weights_bank(n), :], id_b[:, :], mask_t[:, 2 * half + m, :], start=False, stop=True)\
                    .then_inc(S["st_done"], 1)
                if n % 8 == 3 and r >= 1:
                    weigh(r - 1)
                if n == PV_STEP + 3:
                    gather(0)

            pe.wait_ge(S["mask_n_ready"], MB)
            pe.wait_ge(S["stacks_in"], 16 * STACK_DMAS)
            pe.wait_ge(S["vpad_ready"], 4)
            for what, n in beside(*PLAN):
                {"norm": lambda slot: norms(*slot), "maxima": scores, "turn": turn_maxima,
                 "weights": turned_scores}[what](n)
            for kind, k in BEFORE_PV:
                norms(kind, k)
            weigh(len(ROUNDS) - 1)
            gather(1)
            for kind, k in BEHIND:
                norms(kind, k)
            keep_warm(6, WARM[0])
            pe.wait_ge(S["ms_ready"], 1)
            pe.matmul(ps[0:B, 7, 0:NE], msum[:, :], wr_st[:, :], start=True, stop=True).then_inc(S["lg_done"], 1)
            keep_warm(6, WARM[1])
            pe.wait_ge(S["rt_pe"], 1)
            pe.matmul(ps[0:B, 7, NE:2 * NE], ones2[:, 0:B], rt[:, 16:24], start=True, stop=True).then_inc(S["lg_done"], 1)
            keep_warm(6, WARM[2])
            pe.wait_ge(S["topw"], 2)
            pe.matmul(ps[:, 7, 64:68], ones2[:, :], rt[:, 64:68], start=True, stop=True)
            pe.matmul(ps[:, 7, 72:74], selb[:, :], rt[:, 60:62], start=True, stop=True).then_inc(S["w_bc_done"], 1)
            def up(t):
                for n in range(B * TOPK):
                    if t >= 1:
                        pe.wait_ge(S["gelu_done"], B * TOPK * (t - 1) + n + 1)
                    else:
                        pe.wait_ge(w1_in[n], 16)
                    pe.matmul(ps[:, n, :], w1_sel[:, n, :], a2[:, tile_of(t)], start=True, stop=True)\
                        .then_inc(S["up_done"], 1)

            def down(t):
                if t >= 2:
                    pe.wait_ge(S["z3_ready"], t - 1)
                pe.wait_ge(S["gelu_done"], B * TOPK * (t + 1))
                for s in range(TOPK):
                    for b in range(B):
                        last = pe.matmul(ps[D * b:D * b + D, 4 + t % 2, :], w2_c[:, b * TOPK + s, :],
                                         hid[:, t % 2, b * TOPK + s, :], start=(s == 0), stop=(s == TOPK - 1),
                                         skip_group_check=True)
                last.then_inc(S["down_done"], 1)

            def var3(t):
                pe.wait_ge(S["sq3_ready"], t + 1)
                if t in BATCHES[0] and t >= 2:
                    pe.wait_ge(S["r3_ready"], t - 1)
                if t == 1:
                    pe.wait_ge(S["c3_ready"], 1)
                if t == 4:
                    pe.wait_ge(S["r3_ready"], 4)
                if t > 4:
                    pe.wait_ge(S["gelu_done"], B * TOPK * (TILES - 1) + var3_bank(t) + 1)
                pe.matmul(ps[:, var3_bank(t), :], mean_m[:, :], sq3[:, t % 4, :], start=True, stop=True)\
                    .then_inc(S["var3_done"], 1)

            def turn_back(t):
                pe.wait_ge(S["o_ready"], t + 1)
                if t == 0:
                    pe.wait_ge(S["r3_ready"], 4)
                elif t <= 4:
                    pe.wait_ge(S["o_copied"], t)
                elif t == 5:
                    pe.wait_ge(S["r3_ready"], 5)
                else:
                    pe.wait_ge(S["o_copied_late"], t - 5)
                for k in range(4):
                    last = pe.transpose(ps[:, turn_bank(t), P * k:P * k + P], h1[:, TILE * t + P * k:TILE * t + P * k + P],
                                        id_f[:, :])
                last.then_inc(S["o_turned"], 1)

            up(0)
            early, late = BATCHES
            for t in early:
                up(t + 1)
                if t == 0:
                    pe.wait_ge(S["b2m_ready"], 1)
                    pe.matmul(ps[:, 7, 80:81], cent_m[:, :], b2_mix[:, :], start=True, stop=True)\
                        .then_inc(S["c3_done"], 1)
                    pe.wait_ge(S["w2c_ready"], 1)
                down(t)
                if 1 <= t <= 2:
                    var3(t - 1)
            for t in early[2:]:
                var3(t)
            for n, t in enumerate(late):
                if t + 1 < TILES:
                    up(t + 1)
                else:
                    var3(late[1])
                down(t)
                turn_back(early[n])
                if n == 1:
                    var3(late[0])
            for t in late[2:]:
                var3(t)
            for t in late:
                turn_back(t)


_INS = ['x', 'L0_tok_conv1_w', 'L0_tok_conv1_b', 'L0_tok_bn_gamma', 'L0_tok_bn_beta', 'L0_tok_bn_mean', 'L0_tok_bn_var',
        'L0_tok_conv2_w', 'L0_tok_conv2_b', 'L0_attn_edge_index', 'L0_attn_Wq', 'L0_attn_bq', 'L0_attn_Wk', 'L0_attn_bk',
        'L0_attn_Wv', 'L0_attn_bv', 'L0_attn_Wo', 'L0_attn_bo', 'L0_attn_gamma', 'L0_attn_beta', 'L0_ffn_Wr', 'L0_ffn_br',
        'L0_ffn_W1', 'L0_ffn_b1', 'L0_ffn_W2', 'L0_ffn_b2', 'L0_ffn_gamma', 'L0_ffn_beta']
_OUTS = [((2, 4096, 64), 'float32')]


def kernel(**inputs):
    import numpy as _np
    import concourse.bacc as _bacc
    from concourse import mybir as _mybir
    from concourse.bass_utils import run_bass_kernel_spmd as _run

    nc = _bacc.Bacc("TRN2", target_bir_lowering=False, num_devices=1)
    arrays, args = {}, []
    for name in _INS:
        a = _np.ascontiguousarray(inputs[name])
        arrays[f"in_{name}_dram"] = a
        args.append(nc.dram_tensor(f"in_{name}_dram", a.shape, _mybir.dt.from_np(a.dtype), kind="ExternalInput").ap())
    for i, (shape, dtype) in enumerate(_OUTS):
        dt = _mybir.dt.from_np(_np.dtype(dtype))
        args.append(nc.dram_tensor(f"out_{i}_dram", shape, dt, kind="ExternalOutput").ap())
    with nc.allow_non_contiguous_dma(reason="columns of small vectors"):
        vit_tower_kernel(nc, *args)
    r = _run(nc, [arrays], core_ids=[0])
    got = tuple(r.results[0][f"out_{i}_dram"] for i in range(len(_OUTS)))
    return got[0]
```
